# Optimizing a Trainium2 kernel written in Bass

```python
import numpy as np
import jax
import jax.numpy as jnp

def _softmax(x, axis=-1):
    return jax.nn.softmax(x, axis=axis)

def _gelu(x):
    return jax.nn.gelu(x, approximate=True)

def _silu(x):
    return jax.nn.silu(x)

def _sigmoid(x):
    return jax.nn.sigmoid(x)

def _layernorm(x, axis=-1, eps=1e-05):
    m = jnp.mean(x, axis=axis, keepdims=True)
    v = jnp.var(x, axis=axis, keepdims=True)
    return (x - m) / jnp.sqrt(v + eps)

def _scatter_add(tgt, idx, src, axis=0):
    return tgt.at[idx].add(src)

def _segment_sum(src, seg, n):
    return jax.ops.segment_sum(src, seg, n)
kernel_name = 'mk_vit_tower_cls_d1_tok_img1024_r4_ad4f4f'

def setup_inputs(seed: int=0):
    np.random.seed(seed)
    _w = jnp.asarray

    def _rec_inputs():
        import jax
        import jax.numpy as jnp
        _rk = jax.random.key(seed)
        x = 7.22013e-05 + 1.00017 * jax.random.normal(jax.random.fold_in(_rk, 1), (32, 64, 256, 4), jnp.float32)
        cls_tok = 0.02 * jax.random.normal(jax.random.fold_in(_rk, 5), (1, 1, 256), jnp.float32)
        return (x, cls_tok)
    x, cls_tok = _rec_inputs()

    def _L0_tok_setup():
        import jax, jax.numpy as jnp
        import numpy as np
        B, F, L, H, D = (8, 64, 256, 4, 64)
        MODEL = H * F
        WIN = 128

        def _local_mask():
            m = np.ones((L, L), dtype=bool)
            m = np.tril(m, WIN - 1)
            m = np.triu(m, -(WIN - 1))
            return jnp.asarray(m)

        def _flatten(y):
            n = y.shape[0]
            return y.transpose(0, 2, 3, 1).reshape(n, L, -1)
        key = jax.random.key(seed)
        ks = jax.random.split(key, 12)
        s = lambda n: 1.0 / np.sqrt(n)
        xav = np.sqrt(6.0 / (L + L))
        return {'x': jax.random.normal(ks[0], (B, F, L, H), jnp.float32), 'Wq_w': jax.random.normal(ks[1], (D, F), jnp.float32) * s(F), 'Wq_b': jnp.zeros((D,), jnp.float32), 'Wk_w': jax.random.normal(ks[2], (D, F), jnp.float32) * s(F), 'Wk_b': jnp.zeros((D,), jnp.float32), 'Wv_w': jax.random.normal(ks[3], (D, F), jnp.float32) * s(F), 'Wv_b': jnp.zeros((D,), jnp.float32), 'w_bias': jax.random.uniform(ks[4], (L, L), jnp.float32, -xav, xav), 'out_w': jax.random.normal(ks[5], (H * D, MODEL), jnp.float32) * s(H * D), 'out_b': jnp.zeros((MODEL,), jnp.float32), 'ln_g': jnp.ones((MODEL,), jnp.float32), 'ln_b': jnp.zeros((MODEL,), jnp.float32), 'local_mask': _local_mask()}
    _L0_tok_all = _L0_tok_setup()
    _L0_tok_in = {k: v for k, v in _L0_tok_all.items() if k in ('Wq_w', 'Wq_b', 'Wk_w', 'Wk_b', 'Wv_w', 'Wv_b', 'w_bias', 'out_w', 'out_b', 'ln_g', 'ln_b', 'local_mask')}
    del _L0_tok_all

    def _L0_attn_setup():
        import jax, jax.numpy as jnp
        import numpy as np
        NUM_HEADS = 16
        DIM = 256
        HARMONICS = 32
        B, L = (2, 512)

        def holo_linear(x, basis, phase, amp):
            resonance = jnp.einsum('bli,hi->blh', x, basis)
            w = amp * jnp.cos(phase)
            return jnp.einsum('blh,oh->blo', resonance, w)
        key = jax.random.key(seed)
        ks = jax.random.split(key, 13)
        two_pi = 2.0 * np.pi

        def make_proj(k0, k1):
            basis = jax.random.normal(k0, (HARMONICS, DIM), dtype=jnp.float32)
            basis = basis / jnp.linalg.norm(basis, axis=1, keepdims=True)
            phase = jax.random.normal(k1, (DIM, HARMONICS), dtype=jnp.float32) * two_pi
            amp = jnp.ones((DIM, HARMONICS), dtype=jnp.float32) / HARMONICS
            return (basis, phase, amp)
        x = jax.random.normal(ks[0], (B, L, DIM), dtype=jnp.float32)
        bq, pq, aq = make_proj(ks[1], ks[2])
        bk, pk, ak = make_proj(ks[3], ks[4])
        bv, pv, av = make_proj(ks[5], ks[6])
        bo, po, ao = make_proj(ks[7], ks[8])
        return {'x': x, 'basis_q': bq, 'phase_q': pq, 'amp_q': aq, 'basis_k': bk, 'phase_k': pk, 'amp_k': ak, 'basis_v': bv, 'phase_v': pv, 'amp_v': av, 'basis_o': bo, 'phase_o': po, 'amp_o': ao}
    _L0_attn_all = _L0_attn_setup()
    _L0_attn_in = {k: v for k, v in _L0_attn_all.items() if k in ('basis_q', 'phase_q', 'amp_q', 'basis_k', 'phase_k', 'amp_k', 'basis_v', 'phase_v', 'amp_v', 'basis_o', 'phase_o', 'amp_o')}
    del _L0_attn_all

    def _L0_ffn_setup():
        import jax, jax.numpy as jnp
        import numpy as np
        N_EXPERTS = 8
        TOP_K = 2
        D_MODEL = 256
        HIDDEN = 1024
        ROUTED_H = 256
        BATCH, SEQ = (2, 1024)
        key = jax.random.key(seed)
        ks = jax.random.split(key, 8)
        std = 0.02
        return {'x': jax.random.normal(ks[0], (BATCH, SEQ, D_MODEL), dtype=jnp.float32), 'w12': std * jax.random.normal(ks[1], (N_EXPERTS, 2 * ROUTED_H, D_MODEL), dtype=jnp.float32), 'w3': std * jax.random.normal(ks[2], (N_EXPERTS, D_MODEL, ROUTED_H), dtype=jnp.float32), 'shared_w1': std * jax.random.normal(ks[3], (HIDDEN, D_MODEL), dtype=jnp.float32), 'shared_w2': std * jax.random.normal(ks[4], (HIDDEN, D_MODEL), dtype=jnp.float32), 'shared_w3': std * jax.random.normal(ks[5], (D_MODEL, HIDDEN), dtype=jnp.float32), 'router_w': std * jax.random.normal(ks[6], (N_EXPERTS, D_MODEL), dtype=jnp.float32), 'expert_bias': jnp.zeros((N_EXPERTS,), dtype=jnp.float32)}
    _L0_ffn_all = _L0_ffn_setup()
    _L0_ffn_in = {k: v for k, v in _L0_ffn_all.items() if k in ('w12', 'w3', 'shared_w1', 'shared_w2', 'shared_w3', 'router_w', 'expert_bias')}
    del _L0_ffn_all
    return {'x': x, 'cls_tok': cls_tok, 'L0_tok_Wq_w': _L0_tok_in['Wq_w'], 'L0_tok_Wq_b': _L0_tok_in['Wq_b'], 'L0_tok_Wk_w': _L0_tok_in['Wk_w'], 'L0_tok_Wk_b': _L0_tok_in['Wk_b'], 'L0_tok_Wv_w': _L0_tok_in['Wv_w'], 'L0_tok_Wv_b': _L0_tok_in['Wv_b'], 'L0_tok_w_bias': _L0_tok_in['w_bias'], 'L0_tok_out_w': _L0_tok_in['out_w'], 'L0_tok_out_b': _L0_tok_in['out_b'], 'L0_tok_ln_g': _L0_tok_in['ln_g'], 'L0_tok_ln_b': _L0_tok_in['ln_b'], 'L0_tok_local_mask': _L0_tok_in['local_mask'], 'L0_attn_basis_q': _L0_attn_in['basis_q'], 'L0_attn_phase_q': _L0_attn_in['phase_q'], 'L0_attn_amp_q': _L0_attn_in['amp_q'], 'L0_attn_basis_k': _L0_attn_in['basis_k'], 'L0_attn_phase_k': _L0_attn_in['phase_k'], 'L0_attn_amp_k': _L0_attn_in['amp_k'], 'L0_attn_basis_v': _L0_attn_in['basis_v'], 'L0_attn_phase_v': _L0_attn_in['phase_v'], 'L0_attn_amp_v': _L0_attn_in['amp_v'], 'L0_attn_basis_o': _L0_attn_in['basis_o'], 'L0_attn_phase_o': _L0_attn_in['phase_o'], 'L0_attn_amp_o': _L0_attn_in['amp_o'], 'L0_ffn_w12': _L0_ffn_in['w12'], 'L0_ffn_w3': _L0_ffn_in['w3'], 'L0_ffn_shared_w1': _L0_ffn_in['shared_w1'], 'L0_ffn_shared_w2': _L0_ffn_in['shared_w2'], 'L0_ffn_shared_w3': _L0_ffn_in['shared_w3'], 'L0_ffn_router_w': _L0_ffn_in['router_w'], 'L0_ffn_expert_bias': _L0_ffn_in['expert_bias']}

def reference(x, cls_tok, L0_tok_Wq_w, L0_tok_Wq_b, L0_tok_Wk_w, L0_tok_Wk_b, L0_tok_Wv_w, L0_tok_Wv_b, L0_tok_w_bias, L0_tok_out_w, L0_tok_out_b, L0_tok_ln_g, L0_tok_ln_b, L0_tok_local_mask, L0_attn_basis_q, L0_attn_phase_q, L0_attn_amp_q, L0_attn_basis_k, L0_attn_phase_k, L0_attn_amp_k, L0_attn_basis_v, L0_attn_phase_v, L0_attn_amp_v, L0_attn_basis_o, L0_attn_phase_o, L0_attn_amp_o, L0_ffn_w12, L0_ffn_w3, L0_ffn_shared_w1, L0_ffn_shared_w2, L0_ffn_shared_w3, L0_ffn_router_w, L0_ffn_expert_bias):
    import jax
    import jax.numpy as jnp

    def _L0_tok_ref(x, Wq_w, Wq_b, Wk_w, Wk_b, Wv_w, Wv_b, w_bias, out_w, out_b, ln_g, ln_b, local_mask):
        import jax, jax.numpy as jnp
        import numpy as np
        B, F, L, H, D = (8, 64, 256, 4, 64)
        MODEL = H * F
        WIN = 128

        def _local_mask():
            m = np.ones((L, L), dtype=bool)
            m = np.tril(m, WIN - 1)
            m = np.triu(m, -(WIN - 1))
            return jnp.asarray(m)

        def _flatten(y):
            n = y.shape[0]
            return y.transpose(0, 2, 3, 1).reshape(n, L, -1)

        def proj(w, b):
            y = jnp.einsum('nclh,dc->ndlh', x, w) + b[None, :, None, None]
            return _flatten(y)
        q = proj(Wq_w, Wq_b)
        k = proj(Wk_w, Wk_b)
        v = proj(Wv_w, Wv_b)
        wb = w_bias * local_mask.astype(w_bias.dtype)
        ew = jnp.exp(wb)
        ek = jnp.exp(k)
        num = jnp.einsum('ts,nsd->ntd', ew, ek * v)
        den = jnp.einsum('ts,nsd->ntd', ew, ek)
        y = jax.nn.sigmoid(q) * num / den
        h = y @ out_w + out_b + _flatten(x)
        mu = jnp.mean(h, axis=-1, keepdims=True)
        var = jnp.mean(jnp.square(h - mu), axis=-1, keepdims=True)
        return (h - mu) * jax.lax.rsqrt(var + 1e-05) * ln_g + ln_b

    def _L0_attn_ref(x, basis_q, phase_q, amp_q, basis_k, phase_k, amp_k, basis_v, phase_v, amp_v, basis_o, phase_o, amp_o):
        import jax, jax.numpy as jnp
        import numpy as np
        NUM_HEADS = 16
        DIM = 256
        HARMONICS = 32
        B, L = (2, 512)

        def holo_linear(x, basis, phase, amp):
            resonance = jnp.einsum('bli,hi->blh', x, basis)
            w = amp * jnp.cos(phase)
            return jnp.einsum('blh,oh->blo', resonance, w)
        Bsz, Ls, C = x.shape
        head_dim = C // NUM_HEADS
        scale = head_dim ** (-0.5)

        def split_heads(t):
            return t.reshape(Bsz, Ls, NUM_HEADS, head_dim).transpose(0, 2, 1, 3)
        q = split_heads(holo_linear(x, basis_q, phase_q, amp_q))
        k = split_heads(holo_linear(x, basis_k, phase_k, amp_k))
        v = split_heads(holo_linear(x, basis_v, phase_v, amp_v))
        attn = jnp.einsum('bhqd,bhkd->bhqk', q, k) * scale
        attn = jax.nn.softmax(attn, axis=-1)
        out = jnp.einsum('bhqk,bhkd->bhqd', attn, v)
        out = out.transpose(0, 2, 1, 3).reshape(Bsz, Ls, C)
        return holo_linear(out, basis_o, phase_o, amp_o)

    def _L0_ffn_ref(x, w12, w3, shared_w1, shared_w2, shared_w3, router_w, expert_bias):
        import jax, jax.numpy as jnp
        import numpy as np
        N_EXPERTS = 8
        TOP_K = 2
        D_MODEL = 256
        HIDDEN = 1024
        ROUTED_H = 256
        BATCH, SEQ = (2, 1024)
        b, s, d = x.shape
        xf = x.reshape(-1, d)
        shared = jax.nn.silu(xf @ shared_w1.T) * (xf @ shared_w2.T) @ shared_w3.T
        scores = jax.nn.sigmoid(xf @ router_w.T)
        _, top_idx = jax.lax.top_k(scores + expert_bias, TOP_K)
        mask = jax.nn.one_hot(top_idx, N_EXPERTS, dtype=xf.dtype).sum(axis=-2)
        gates = scores * mask
        h12 = jnp.einsum('td,ehd->teh', xf, w12)
        h1, h2 = jnp.split(h12, 2, axis=-1)
        h = jax.nn.silu(h1) * h2 * gates[:, :, None]
        routed = jnp.einsum('teh,edh->td', h, w3)
        return (shared + routed).reshape(b, s, d)
    h = _L0_tok_ref(x, L0_tok_Wq_w, L0_tok_Wq_b, L0_tok_Wk_w, L0_tok_Wk_b, L0_tok_Wv_w, L0_tok_Wv_b, L0_tok_w_bias, L0_tok_out_w, L0_tok_out_b, L0_tok_ln_g, L0_tok_ln_b, L0_tok_local_mask)
    h = jnp.concatenate([jnp.broadcast_to(cls_tok, (h.shape[0], 1, h.shape[2])), h], axis=1)
    h = h + _L0_attn_ref(_layernorm(h, axis=-1), L0_attn_basis_q, L0_attn_phase_q, L0_attn_amp_q, L0_attn_basis_k, L0_attn_phase_k, L0_attn_amp_k, L0_attn_basis_v, L0_attn_phase_v, L0_attn_amp_v, L0_attn_basis_o, L0_attn_phase_o, L0_attn_amp_o)
    h = h + _L0_ffn_ref(_layernorm(h, axis=-1), L0_ffn_w12, L0_ffn_w3, L0_ffn_shared_w1, L0_ffn_shared_w2, L0_ffn_shared_w3, L0_ffn_router_w, L0_ffn_expert_bias)
    return h

_drawn_inputs = setup_inputs


def setup_inputs(seed=0):
    import zlib

    import numpy as np

    out = dict(_drawn_inputs(seed))
    spreads = {'L0_tok_Wq_b': (0.0, 0.8),
     'L0_tok_Wk_b': (0.0, 2.0),
     'L0_tok_Wv_b': (0.0, 0.1),
     'L0_tok_out_b': (0.0, 0.1),
     'L0_tok_ln_g': (1.0, 0.2),
     'L0_tok_ln_b': (0.0, 0.1),
     'L0_attn_amp_q': (0.03125, 0.6),
     'L0_attn_amp_k': (0.03125, 0.6),
     'L0_attn_amp_v': (0.03125, 0.6),
     'L0_attn_amp_o': (0.03125, 0.6),
     'L0_ffn_expert_bias': (0.0, 0.643)}
    factors = {'cls_tok': 8.0,
     'L0_tok_w_bias': 8.0,
     'L0_attn_basis_q': 8.0,
     'L0_attn_phase_q': 8.0,
     'L0_attn_basis_k': 8.0,
     'L0_attn_phase_k': 8.0,
     'L0_attn_basis_v': 8.0,
     'L0_attn_phase_v': 8.0,
     'L0_attn_basis_o': 8.0,
     'L0_attn_phase_o': 8.0,
     'L0_ffn_w12': 4.442,
     'L0_ffn_w3': 4.453,
     'L0_ffn_router_w': 7.026,
     'L0_ffn_shared_w1': 3.656,
     'L0_ffn_shared_w2': 3.624,
     'L0_ffn_shared_w3': 3.604}
    for name, (base, spread) in spreads.items():
        noise = np.random.default_rng([zlib.crc32(name.encode()), seed]).standard_normal(out[name].shape)
        drawn = base * np.exp(spread * noise) if base else spread * noise
        out[name] = jnp.asarray(drawn.astype(out[name].dtype))
    for name, factor in factors.items():
        out[name] = (out[name] * factor).astype(out[name].dtype)
    return out
```

```python
from contextlib import ExitStack

import numpy as np

import concourse.bass as bass
from concourse import mybir

F32 = mybir.dt.float32
F32R = mybir.dt.float32r
U8 = mybir.dt.uint8
ALU = mybir.AluOpType
ACT = mybir.ActivationFunctionType
AX_X = mybir.AxisListType.X

B, C, L, H = 32, 64, 256, 4
D = C * H
P = 128
LT = L // P
FT = D // P
NH, HD, HARM = 16, 16, 32
SLOT = 32
G = NH * SLOT // P
HPG = NH // G
N = L + 1
CLS = L
NE = 8
UH = 256
NS = 1024 // UH
NU = NS + NE
EPS = 1e-5
TWO_PI_1 = 6.28125
TWO_PI_2 = float(np.float32(0.0019350051879882812))
TWO_PI_3 = float(2 * np.pi - TWO_PI_1 - TWO_PI_2)
ROUND = 12582912.0


def build(nc, a, out):
    with ExitStack() as whole:
        def sem(name):
            return whole.enter_context(nc.semaphore(name))

        hscr = nc.dram_tensor("hscr", [B + 1, P, LT, D], F32, kind="Internal").ap()
        mv3 = whole.enter_context(nc.sbuf_tensor("mv3", [P, (B + 1) * LT, 2], F32))
        rs3 = whole.enter_context(nc.sbuf_tensor("rs3", [P, (B + 1) * LT], F32))
        eye = whole.enter_context(nc.sbuf_tensor("eye", [P, P], F32))
        mhalf = whole.enter_context(nc.sbuf_tensor("mhalf", [P, 2], F32))
        ps = whole.enter_context(nc.psum_tensor("ps", [P, 8, 512], F32))
        with ExitStack() as ctx:
            stage_a(nc, ctx, sem, a, hscr, mv3, rs3, eye, mhalf, ps)
        with ExitStack() as ctx:
            stage_b(nc, ctx, sem, a, out, hscr, mv3, rs3, eye, ps)


def stage_a(nc, ctx, sem, a, hscr, mv3, rs3, eye, mhalf, ps):
    def sb(name, shape, dt=F32):
        return ctx.enter_context(nc.sbuf_tensor(name, shape, dt))

    xs = sb("xs", [C + 1, L * H])
    wkv = sb("wkv", [C + 1, 2 * C])
    wq = sb("wq", [C + 1, C])
    idn = sb("idn", [C + 1, D])
    wbT = sb("wbT", [P, LT, L])
    mskT = sb("mskT", [P, LT, L], U8)
    mskf = sb("mskf", [P, LT, L])
    ewT = sb("ewT", [P, LT, L])
    outw = sb("outw", [P, FT, D])
    lng = sb("lng", [P, LT * D])
    lnb = sb("lnb", [P, LT * D])
    basT = sb("basT", [P, FT, 3 * HARM])
    basoT = sb("basoT", [P, FT, HARM])
    phs = sb("phs", [P, 512])
    amp = sb("amp", [P, 512])
    W = sb("W", [P, 512])
    tr = sb("tr", [P, 512])
    tn = sb("tn", [P, 512])
    kone = sb("kone", [P, 1])
    selm = sb("selm", [NH, G, P])
    bdm = sb("bdm", [P, G, NH])
    vbdm = sb("vbdm", [NH, D])
    clsr = sb("clsr", [1, D])
    cls32 = sb("cls32", [P, D])
    clsst = sb("clsst", [1, 6])
    clsmv = sb("clsmv", [1, 2])
    clsrs = sb("clsrs", [1, 1])
    clsz = sb("clsz", [1, D])
    one1 = sb("one1", [1, 1])
    zeros = sb("zeros", [P, LT * D])
    tick = sb("tick", [P, 1])
    clskt = sb("clskt", [P, G])
    mvb = sb("mvb", [P, LT, 2])
    mh65 = sb("mh65", [P, (B + 1) * LT])
    hres = sb("hres", [P, LT, D])
    h2 = sb("h2", [P, LT, D])
    rbc = sb("rbc", [3 * HARM, NH])
    ek = sb("ek", [P, LT, D])
    ekv = sb("ekv", [P, LT, D])
    tq = sb("tq", [P, FT, L])
    rden = sb("rden", [P, FT, L])
    y1 = sb("y1", [P, FT, L])
    yT = sb("yT", [P, FT, L])
    hn = sb("hn", [P, LT, D])
    hg = sb("hg", [P, LT, D])
    z = sb("z", [P, LT, D])
    st = sb("st", [P, LT, 6])
    mv = sb("mv", [P, LT, 2])
    rs = sb("rs", [P, LT])
    st2 = sb("st2", [P, LT, 6])
    mv2 = sb("mv2", [P, LT, 2])
    rs2 = sb("rs2", [P, LT])
    st3 = sb("st3", [P, LT, 6])
    zT = sb("zT", [P, FT, N])
    rT = sb("rT", [3 * HARM, N])
    qs = sb("qs", [P, G, N])
    ka = sb("ka", [P, G, N])
    qa = sb("qa", [P, G, N])
    qr = sb("qr", [P, G, N + 1], F32R)
    kr = sb("kr", [P, G, N + 1], F32R)
    kbd = sb("kbd", [P, G, NH])
    qbd = sb("qbd", [P, G, NH])
    vbd = sb("vbd", [NH, NH, SLOT])
    va = sb("va", [P, LT, NH, SLOT])
    mx = sb("mx", [P, LT, NH])
    negm = sb("negm", [NH, N])
    pT = sb("pT", [P, NH, LT, N])
    pc = sb("pc", [NH, N])
    og = sb("og", [P, G, N])
    rc = sb("rc", [P, LT * NH])
    on = sb("on", [P, LT, D])
    onT = sb("onT", [P, FT, L])
    ro = sb("ro", [P, L])
    clso = sb("clso", [P, G, B])

    (c_load, c_set, d_step, half_ok, mask_ok, wb_ok, ew_ok, arg_ok, cos_ok, w_ok, clsvar_ok, clsrs_ok, clsz_ok, clsT_ps,
     clsT_ok, clsr_ps, clsr_ok, clsqkv_ps, spread_ok) = (
        sem(x) for x in ("c_load", "c_set", "d_step", "half_ok", "mask_ok", "wb_ok", "ew_ok", "arg_ok", "cos_ok", "w_ok",
                         "clsvar_ok", "clsrs_ok", "clsz_ok", "clsT_ps", "clsT_ok", "clsr_ps", "clsr_ok", "clsqkv_ps",
                         "spread_ok"))
    x_in, h2_out, hres_ok = sem("x_in"), sem("h2_out"), sem("hres_ok")
    kvq_ps, ek_ok, tq_ok, ekv_ok, nd_ps = (sem(x) for x in ("kvq_ps", "ek_ok", "tq_ok", "ekv_ok", "nd_ps"))
    y_step, y_ok, h_ps, ln1, hn_ok, h_st, ln2, z_ok, zt_ps, zt_ok = (
        sem(x) for x in ("y_step", "y_ok", "h_ps", "ln1", "hn_ok", "h_st", "ln2", "z_ok", "zt_ps", "zt_ok"))
    p1, p2, hg_ok = sem("p1"), sem("p2"), sem("hg_ok")
    r_ps, r_ok, q_ps, q_ok, k_ps, k_ok, v_ps, v_ok, qk_r = (
        sem(x) for x in ("r_ps", "r_ok", "q_ps", "q_ok", "k_ps", "k_ok", "v_ps", "v_ok", "qk_r"))
    mx_ps, mx_ok, mt_ps, negm_ok, sel_ps, qa_ok = (
        sem(x) for x in ("mx_ps", "mx_ok", "mt_ps", "negm_ok", "sel_ps", "qa_ok"))
    s_ps, s_ok, pv_ps, og_ok, ot_ps, rc_ok, on_ok, onT_ps, onT_ok, ro_ps, ro_ok, o_ps, h2_ok, ln3, clso_ok = (
        sem(x) for x in ("s_ps", "s_ok", "pv_ps", "og_ok", "ot_ps", "rc_ok", "on_ok", "onT_ps", "onT_ok",
                         "ro_ps", "ro_ok", "o_ps", "h2_ok", "ln3", "clso_ok"))

    loads = [(wkv, a["wkv"]), (wq, a["wq"]), (idn, a["idn"]), (wbT, a["wbT"]), (mskT, a["mskT"]),
             (outw, a["outw"]), (lng, a["lng"]), (lnb, a["lnb"]), (basT, a["basT"]), (basoT, a["basoT"]),
             (phs, a["phs"]), (amp, a["amp"]), (kone, a["kone"]), (selm, a["selm"]), (bdm, a["bdm"]),
             (vbdm, a["vbdm"]), (eye, a["eye"]), (clsr, a["clsr"]), (cls32, a["cls32"])]
    LOADED = 16 * len(loads)

    def bank(n, w=512):
        return ps[:, n, 0:w]

    def xcol(t, h):
        return xs[:, h:L * H:H] if t is None else xs[:, t * P * H + h:(t + 1) * P * H:H]

    block = ctx.enter_context(nc.Block())

    @block.sync
    def _(sp):
        for dst, src in loads:
            sp.dma_start(dst[:], src).then_inc(c_load, 16)
        sp.dma_start(xs[0:C, :], a["x"][0].rearrange("c l h -> c (l h)")).then_inc(x_in, 16)
        sp.wait_ge(half_ok, 1)
        sp.dma_start(hscr[B], h2[:]).then_inc(h2_out, 16)
        with sp.Fori(1, B) as b:
            sp.wait_ge(h_ps, b)
            sp.dma_start(xs[0:C, :], a["x"][bass.ds(b, 1)].rearrange("n c l h -> (n c) (l h)")).then_inc(x_in, 16)
            sp.wait_ge(h2_ok, b)
            sp.dma_start(hscr[bass.ds(b - 1, 1)].rearrange("n p t d -> p (n t) d"), h2[:]).then_inc(h2_out, 16)
        for b in (B - 1, B):
            sp.wait_ge(h2_ok, b + 1)
            sp.dma_start(hscr[b], h2[:]).then_inc(h2_out, 16)
        sp.wait_ge(h2_out, 16 * (B + 2))

    @block.tensor
    def _(pe):
        def mixer_kvq(b):
            pe.wait_ge(x_in, b * 16 + 16)
            if not isinstance(b, int) or b > 0:
                pe.wait_ge(zt_ok, b)
            for t in range(LT):
                for h in range(H):
                    pe.matmul(ps[:, t, h * 2 * C:(h + 1) * 2 * C], xcol(t, h), wkv[:], start=True, stop=True)
            for f in range(FT):
                for hh in range(2):
                    last = pe.matmul(ps[hh * C:(hh + 1) * C, 2, f * L:(f + 1) * L], wq[:], xcol(None, 2 * f + hh),
                                     start=True, stop=True)
            last.then_inc(kvq_ps, 1)

        def mixer_sums(b):
            pe.wait_ge(ek_ok, b + 1)
            pe.wait_ge(ekv_ok, b + 1)
            for n, src in ((0, ekv), (1, ek)):
                for f in range(FT):
                    for s in range(LT):
                        last = pe.matmul(ps[:, n, f * L:(f + 1) * L], src[:, s, f * P:(f + 1) * P], ewT[:, s, :],
                                         start=(s == 0), stop=(s == LT - 1))
            last.then_inc(nd_ps, 1)

        def mixer_out(b):
            pe.wait_ge(y_ok, b + 1)
            pe.wait_ge(tq_ok, b + 1)
            for t in range(LT):
                o = ps[:, 2, t * D:(t + 1) * D]
                for f in range(FT):
                    pe.matmul(o, yT[:, f, t * P:(t + 1) * P], outw[:, f, :], start=(f == 0), stop=False)
                for h in range(H):
                    last = pe.matmul(o[:, h * C:(h + 1) * C], xcol(t, h), idn[:, h * C:(h + 1) * C],
                                     start=False, stop=(h == H - 1))
            last.then_inc(h_ps, 1)

        def mixer_turn(b):
            pe.wait_ge(z_ok, b + 1)
            for f in range(FT):
                for t in range(LT):
                    last = pe.transpose(ps[:, 0, f * L + t * P:f * L + (t + 1) * P], z[:, t, f * P:(f + 1) * P], eye[:])
            last.then_inc(zt_ps, 1)

        def resonances(b):
            pe.wait_ge(zt_ok, b + 1)
            if not isinstance(b, int) or b > 0:
                pe.wait_ge(h2_ok, b)
            for f in range(FT):
                last = pe.matmul(ps[0:3 * HARM, 7, 0:N], basT[:, f, :], zT[:, f, :], start=(f == 0), stop=(f == FT - 1))
            last.then_inc(r_ps, 1)

        def heads_qkv(b):
            pe.wait_ge(r_ok, b + 1)
            for g in range(G):
                last = pe.matmul(ps[:, 3 + g, 0:N], W[0:HARM, g * P:(g + 1) * P], rT[0:HARM, :], start=True, stop=True)
            last.then_inc(q_ps, 1)
            for t in range(LT):
                last = pe.matmul(ps[:, 7, t * D:(t + 1) * D], rT[2 * HARM:, t * P:(t + 1) * P], W[2 * HARM:3 * HARM, 0:D],
                                 start=True, stop=True)
            last.then_inc(v_ps, 1)
            pe.wait_ge(q_ok, b + 1)
            for g in range(G):
                last = pe.matmul(ps[:, 3 + g, 0:N], W[HARM:2 * HARM, g * P:(g + 1) * P], rT[HARM:2 * HARM, :],
                                 start=True, stop=True)
            last.then_inc(k_ps, 1)

        def slot(t, h, w0, w1):
            p = SLOT * (h % HPG)
            return t[p:p + SLOT, h // HPG, w0:w1]

        MXN = LT * NH // 2 + 1

        def maxima(b):
            pe.wait_ge(qk_r, 2 * b + 2)
            pe.wait_ge(v_ok, b + 1)
            for g in range(G):
                last = pe.matmul(ps[0:NH, 7, 0:N], qbd[:, g, :], ka[:, g, :], start=(g == 0), stop=(g == G - 1))
            last.then_inc(mx_ps, 1)
            n = 0
            for t in range(LT):
                for h in range(0, NH, 2):
                    if n >= 2:
                        pe.wait_ge(mx_ok, b * MXN + n)
                    for k in range(2):
                        last = pe.matmul(ps[:, 3 + 2 * (n % 2) + k, 0:N + 1], slot(qr, h + k, t * P, (t + 1) * P),
                                         slot(kr, h + k, 0, N + 1), start=True, stop=True)
                    last.then_inc(mx_ps, 1)
                    n += 1

        def shift_q(b):
            pe.wait_ge(mx_ok, b * MXN + MXN)
            for t in range(LT):
                last = pe.transpose(ps[0:NH, 7, t * P:(t + 1) * P], mx[:, t, :], eye[:])
            last.then_inc(mt_ps, 1)
            pe.wait_ge(negm_ok, b + 1)
            for g in range(G):
                last = pe.matmul(ps[:, 3 + g, 0:N], selm[:, g, :], negm[:], start=True, stop=True)
            last.then_inc(sel_ps, 1)

        SN = NH + 1

        def scores(b, h):
            if h == 0:
                pe.wait_ge(qa_ok, b + 1)
            else:
                if h >= 2:
                    pe.wait_ge(s_ok, b * SN + h)
            for t in range(LT):
                last = pe.matmul(ps[:, 3 + 2 * (h % 2) + t, 0:N], slot(ka, h, t * P, (t + 1) * P), slot(qa, h, 0, N),
                                 start=True, stop=True)
            last.then_inc(s_ps, 1)

        def cls_scores(b):
            pe.wait_ge(qa_ok, b + 1)
            for g in range(G):
                last = pe.matmul(ps[0:NH, 7, 0:N], kbd[:, g, :], qa[:, g, :], start=(g == 0), stop=(g == G - 1))
            last.then_inc(s_ps, 1)

        def values(b, g):
            pe.wait_ge(s_ok, b * SN + 1 + HPG * (g + 1))
            if g > 0:
                pe.wait_ge(og_ok, b * G + g)
            pe.matmul(ps[:, 7, 0:N], vbd[:, g * HPG:(g + 1) * HPG, :].rearrange("p h s -> p (h s)"), pc[:], start=True,
                      stop=False, skip_group_check=True)
            for j in range(HPG):
                h = g * HPG + j
                for t in range(LT):
                    last = pe.matmul(ps[SLOT * j:SLOT * (j + 1), 7, 0:N], va[:, t, h, :], pT[:, h, t, :], start=False,
                                     stop=(t == LT - 1), skip_group_check=True)
            last.then_inc(pv_ps, 1)

        def attend_out(b):
            pe.wait_ge(og_ok, b * G + G)
            pe.wait_ge(s_ok, b * SN + SN)
            for t in range(LT):
                for g in range(G):
                    last = pe.transpose(ps[:, 3 + t, g * P:(g + 1) * P], og[:, g, t * P:(t + 1) * P], eye[:])
            last.then_inc(ot_ps, 1)
            pe.wait_ge(on_ok, b + 1)
            for f in range(FT):
                for t in range(LT):
                    last = pe.transpose(ps[:, 5, f * L + t * P:f * L + (t + 1) * P], on[:, t, f * P:(f + 1) * P], eye[:])
            last.then_inc(onT_ps, 1)
            pe.wait_ge(onT_ok, b + 1)
            for f in range(FT):
                last = pe.matmul(ps[96:P, 6, 0:L], basoT[:, f, :], onT[:, f, :], start=(f == 0), stop=(f == FT - 1))
            last.then_inc(ro_ps, 1)
            pe.wait_ge(ro_ok, b + 1)
            for t in range(LT):
                last = pe.matmul(ps[:, 7, t * D:(t + 1) * D], ro[96:P, t * P:(t + 1) * P], W[96:P, 0:D], start=True,
                                 stop=True)
            last.then_inc(o_ps, 1)

        pe.wait_ge(c_load, LOADED)
        pe.wait_ge(c_set, 1)
        pe.wait_ge(clsz_ok, 1)
        for f in range(FT):
            last = pe.matmul(ps[:, 6, f:f + 1], clsz[:, f * P:(f + 1) * P], one1[:], start=True, stop=True)
        last.then_inc(clsT_ps, 1)
        pe.wait_ge(clsT_ok, 1)
        for f in range(FT):
            last = pe.matmul(ps[0:3 * HARM, 5, 16:17], basT[:, f, :], zT[:, f, CLS:N], start=(f == 0), stop=(f == FT - 1))
        last.then_inc(clsr_ps, 1)
        pe.wait_ge(clsr_ok, 2)
        pe.wait_ge(w_ok, 1)
        for g in range(G):
            pe.matmul(ps[:, 4, g:g + 1], W[0:HARM, g * P:(g + 1) * P], rT[0:HARM, CLS:N], start=True, stop=True)
            pe.matmul(ps[:, 5, g:g + 1], W[HARM:2 * HARM, g * P:(g + 1) * P], rT[HARM:2 * HARM, CLS:N], start=True,
                      stop=True)
        pe.matmul(ps[0:NH, 3, 0:D], rbc[2 * HARM:, :], W[2 * HARM:3 * HARM, 0:D], start=True,
                  stop=True).then_inc(clsqkv_ps, 1)
        mixer_kvq(0)
        pe.wait_ge(ew_ok, 1)
        mixer_sums(0)
        mixer_out(0)
        mixer_turn(0)
        pe.wait_ge(spread_ok, 1)
        resonances(0)

        def image(b, nxt):
            if nxt:
                mixer_kvq(b + 1)
            heads_qkv(b)
            maxima(b)
            if nxt:
                mixer_sums(b + 1)
            shift_q(b)
            cls_scores(b)
            for h in range(NH):
                scores(b, h)
                if h % HPG == HPG - 1 and h > HPG:
                    values(b, h // HPG - 1)
                if h == 9 and nxt:
                    mixer_out(b + 1)
            values(b, G - 1)
            if nxt:
                mixer_turn(b + 1)
            attend_out(b)
            if nxt:
                resonances(b + 1)

        with pe.Fori(0, B - 1) as b:
            image(b, True)
        image(B - 1, False)
        pe.wait_ge(clso_ok, B + 1)
        for g in range(G):
            last = pe.transpose(ps[0:B, 3, g * P:(g + 1) * P], clso[:, g, :], eye[:])
        last.then_inc(ot_ps, 1)
        pe.wait_ge(on_ok, B + 1)
        for f in range(FT):
            last = pe.transpose(ps[:, 5, f * B:(f + 1) * B], on[0:B, 0, f * P:(f + 1) * P], eye[0:B, 0:B])
        last.then_inc(onT_ps, 1)
        pe.wait_ge(onT_ok, B + 1)
        for f in range(FT):
            last = pe.matmul(ps[96:P, 6, 0:B], basoT[:, f, :], onT[:, f, 0:B], start=(f == 0), stop=(f == FT - 1))
        last.then_inc(ro_ps, 1)
        pe.wait_ge(ro_ok, B + 1)
        pe.wait_ge(h2_ok, B)
        pe.matmul(ps[0:B, 7, 0:D], ro[96:P, 0:B], W[96:P, 0:D], start=True, stop=True).then_inc(o_ps, 1)

    @block.scalar
    def _(act):
        def mixer_exps(b):
            act.wait_ge(kvq_ps, b + 1)
            kv = ps[:, 0:LT, :].rearrange("p t (h w) -> p t h w", h=H)
            act.activation(ek[:].rearrange("p t (h w) -> p t h w", h=H), kv[:, :, :, 0:C], ACT.Exp).then_inc(ek_ok, 1)
            act.activation(tq[:].rearrange("p f l -> p (f l)"), bank(2), ACT.Tanh, scale=0.5).then_inc(tq_ok, 1)

        def mixer_turned(b):
            act.wait_ge(zt_ps, b + 1)
            act.activation(zT[:, :, 0:L], bank(0).rearrange("p (f l) -> p f l", f=FT), ACT.Copy).then_inc(zt_ok, 1)

        def rest(b, nxt):
            act.wait_ge(r_ps, b + 1)
            act.activation(rT[:], ps[0:3 * HARM, 7, 0:N], ACT.Copy).then_inc(r_ok, 1)
            act.wait_ge(q_ps, b + 1)
            act.activation(qs[:], ps[:, 3:7, 0:N], ACT.Copy).then_inc(q_ok, 1)
            act.wait_ge(v_ps, b + 1)
            act.activation(va[:, :, :, 0:HD], bank(7).rearrange("p (t h d) -> p t h d", t=LT, h=NH),
                           ACT.Copy).then_inc(v_ok, 1)
            act.wait_ge(k_ps, b + 1)
            act.activation(ka[:], ps[:, 3:7, 0:N], ACT.Identity, bias=kone[:, 0:1]).then_inc(k_ok, 1)
            if nxt:
                mixer_exps(b + 1)
            act.wait_ge(s_ps, b * (NH + 1) + 1)
            act.activation(pc[:], ps[0:NH, 7, 0:N], ACT.Exp, scale=HD ** -0.5).then_inc(s_ok, 1)
            for h in range(NH):
                act.wait_ge(s_ps, b * (NH + 1) + h + 2)
                n = 3 + 2 * (h % 2)
                act.activation(pT[:, h, :, :], ps[:, n:n + LT, 0:N], ACT.Exp, scale=HD ** -0.5).then_inc(s_ok, 1)
                if h % HPG == HPG - 1 and h > HPG:
                    take_group(b, h // HPG - 1)
            take_group(b, G - 1)
            if nxt:
                mixer_turned(b + 1)
            act.wait_ge(onT_ps, b + 1)
            act.activation(onT[:].rearrange("p f l -> p (f l)"), bank(5), ACT.Copy).then_inc(onT_ok, 1)
            act.wait_ge(ro_ps, b + 1)
            act.activation(ro[96:P, :], ps[96:P, 6, 0:L], ACT.Copy).then_inc(ro_ok, 1)

        def take_group(b, g):
            act.wait_ge(pv_ps, b * G + g + 1)
            if g == 0:
                act.wait_ge(clso_ok, b + 1)
            act.activation(og[:, g, :], ps[:, 7, 0:N], ACT.Copy).then_inc(og_ok, 1)

        act.wait_ge(arg_ok, 1)
        act.activation(tr[:], tn[:], ACT.Sin).then_inc(cos_ok, 1)
        act.wait_ge(wb_ok, 1)
        act.activation(ewT[:], wbT[:], ACT.Exp).then_inc(ew_ok, 1)
        act.wait_ge(clsT_ps, 1)
        act.activation(zT[:, :, CLS:N], ps[:, 6, 0:FT].rearrange("p (f o) -> p f o", o=1), ACT.Copy).then_inc(clsT_ok, 1)
        act.wait_ge(clsr_ps, 1)
        act.activation(rT[:, CLS:N], ps[0:3 * HARM, 5, 16:17], ACT.Copy).then_inc(clsr_ok, 1)
        mixer_exps(0)
        mixer_turned(0)
        with act.Fori(0, B - 1) as b:
            rest(b, True)
        rest(B - 1, False)
        act.wait_ge(onT_ps, B + 1)
        act.activation(onT[:, :, 0:B], ps[:, 5, 0:FT * B].rearrange("p (f b) -> p f b", f=FT), ACT.Copy).then_inc(onT_ok, 1)
        act.wait_ge(ro_ps, B + 1)
        act.activation(ro[96:P, 0:B], ps[96:P, 6, 0:B], ACT.Copy).then_inc(ro_ok, 1)

    @block.vector
    def _(dve):
        MXN = LT * NH // 2 + 1

        def mixer_ekv(b):
            dve.wait_ge(ek_ok, b + 1)
            kv = ps[:, 0:LT, :].rearrange("p t (h w) -> p t h w", h=H)
            dve.tensor_tensor(ekv[:].rearrange("p t (h w) -> p t h w", h=H), kv[:, :, :, C:2 * C],
                              ek[:].rearrange("p t (h w) -> p t h w", h=H), ALU.mult).then_inc(ekv_ok, 1)

        def mixer_y(b):
            dve.wait_ge(nd_ps, b + 1)
            dve.wait_ge(tq_ok, b + 1)
            flat = lambda t: t[:].rearrange("p f l -> p (f l)")
            dve.reciprocal(flat(rden), bank(1)).then_inc(y_step, 1)
            dve.scalar_tensor_tensor(out=flat(y1), in0=flat(tq), scalar=1.0, in1=bank(0), op0=ALU.add,
                                     op1=ALU.mult).then_inc(y_step, 1)
            dve.wait_ge(y_step, 2 * b + 2)
            dve.scalar_tensor_tensor(out=flat(yT), in0=flat(y1), scalar=0.5, in1=flat(rden), op0=ALU.mult,
                                     op1=ALU.mult).then_inc(y_ok, 1)

        def mixer_norm(b):
            dve.wait_ge(h_ps, b + 1)
            for t in range(LT):
                dve.bn_stats(st[:, t, :], ps[:, 2, t * D:(t + 1) * D]).then_inc(ln1, 1)
            dve.wait_ge(ln1, b * 5 + 2)
            dve.memset(tick[:], 0.0)
            for t in range(LT):
                dve.bn_aggr(mv[:, t, :], st[:, t, :]).then_inc(ln1, 1)
            dve.wait_ge(ln1, b * 5 + 4)
            dve.tensor_scalar(rs[:], mv[:, :, 1], EPS, None, ALU.add).then_inc(ln1, 1)
            dve.wait_ge(p1, b + 1)
            for t in range(LT):
                dve.tensor_scalar(hn[:, t, :], ps[:, 2, t * D:(t + 1) * D], mv[:, t, 0:1], rs[:, t:t + 1],
                                  ALU.subtract, ALU.mult).then_inc(hn_ok, 1)

        def attn_norm(b):
            dve.wait_ge(h_st, b + 1)
            for t in range(LT):
                dve.bn_stats(st2[:, t, :], hg[:, t, :]).then_inc(ln2, 1)
            dve.wait_ge(ln2, b * 5 + 2)
            dve.memset(tick[:], 0.0)
            for t in range(LT):
                dve.bn_aggr(mv2[:, t, :], st2[:, t, :]).then_inc(ln2, 1)
            dve.wait_ge(ln2, b * 5 + 4)
            dve.tensor_scalar(rs2[:], mv2[:, :, 1], EPS, None, ALU.add).then_inc(ln2, 1)
            dve.wait_ge(p2, b + 1)
            for t in range(LT):
                last = dve.tensor_scalar(z[:, t, :], hg[:, t, :], mv2[:, t, 0:1], rs2[:, t:t + 1], ALU.subtract,
                                         ALU.mult)
            last.then_inc(z_ok, 1)

        def rest(b, nxt):
            dve.wait_ge(q_ok, b + 1)
            dve.tensor_copy(qr[:, :, 0:N], qs[:]).then_inc(qk_r, 1)
            dve.wait_ge(k_ok, b + 1)
            dve.tensor_copy(kr[:, :, 0:N], ka[:]).then_inc(qk_r, 1)
            if nxt:
                mixer_ekv(b + 1)
            dve.wait_ge(mx_ps, b * MXN + 1)
            dve.tensor_reduce(negm[:, CLS:N], ps[0:NH, 7, 0:N], AX_X, ALU.max, negate=True).then_inc(mx_ok, 1)
            n = 0
            for t in range(LT):
                for h in range(0, NH, 2):
                    dve.wait_ge(mx_ps, b * MXN + n + 2)
                    k = 3 + 2 * (n % 2)
                    dve.tensor_reduce(mx[:, t, h:h + 2], ps[:, k:k + 2, 0:N], AX_X, ALU.max).then_inc(mx_ok, 1)
                    n += 1
            dve.wait_ge(mt_ps, b + 1)
            dve.tensor_scalar(negm[:, 0:L], ps[0:NH, 7, 0:L], -1.0, None, ALU.mult).then_inc(negm_ok, 1)
            dve.wait_ge(sel_ps, b + 1)
            dve.tensor_tensor(qa[:], ps[:, 3:7, 0:N], qs[:], ALU.add).then_inc(qa_ok, 1)
            if nxt:
                mixer_y(b + 1)
                mixer_norm(b + 1)
                attn_norm(b + 1)
            dve.wait_ge(ot_ps, b + 1)
            o = ps[:, 3:3 + LT, :].rearrange("p t (h s) -> p (t h) s", s=SLOT)
            dve.reciprocal(rc[:], o[:, :, HD]).then_inc(rc_ok, 1)
            dve.wait_ge(rc_ok, b + 1)
            dve.tensor_tensor(on[:].rearrange("p t (h d) -> p (t h) d", d=HD), o[:, :, 0:HD],
                              rc[:].rearrange("p (x o) -> p x o", o=1).broadcast_to([P, LT * NH, HD]),
                              ALU.mult).then_inc(on_ok, 1)
            dve.tensor_copy(clso[:, :, bass.ds(b, 1)], og[:, :, CLS:N]).then_inc(clso_ok, 1)
            dve.wait_ge(o_ps, b + 1)
            dve.wait_ge(hres_ok, b + 1)
            dve.wait_ge(h2_out, 16 * b + 16)
            flat = lambda t: t[:].rearrange("p t d -> p (t d)")
            dve.tensor_tensor(flat(h2), bank(7), flat(hres), ALU.add).then_inc(h2_ok, 1)
            dve.wait_ge(h2_ok, b + 1)
            for t in range(LT):
                dve.bn_stats(st3[:, t, :], h2[:, t, :]).then_inc(ln3, 1)
            dve.wait_ge(ln3, b * 5 + 2)
            dve.memset(tick[:], 0.0)
            for t in range(LT):
                dve.bn_aggr(mvb[:, t, :], st3[:, t, :]).then_inc(ln3, 1)
            dve.wait_ge(ln3, b * 5 + 4)
            dve.tensor_copy(mv3[:, bass.ds(b * LT, LT), :].rearrange("p t m -> p (t m)"),
                            mvb[:].rearrange("p t m -> p (t m)")).then_inc(ln3, 1)

        dve.memset(h2[:], 0.0)
        dve.memset(mh65[:], -0.5)
        dve.memset(zeros[:], 0.0)
        dve.memset(mhalf[:], -0.5).then_inc(half_ok, 1)
        dve.memset(clso[:], 0.0).then_inc(clso_ok, 1)
        dve.memset(xs[C:C + 1, :], 1.0)
        dve.memset(one1[:], 1.0)
        dve.memset(qr[:].bitcast(F32), 0.0)
        dve.memset(kr[:].bitcast(F32), 0.0)
        dve.memset(mv3[:, B * LT:, :], 0.0)
        dve.memset(vbd[:], 0.0)
        dve.memset(va[:], 0.0).then_inc(d_step, 1)
        dve.wait_ge(d_step, 1)
        dve.memset(va[:, :, :, HD:HD + 1], 1.0).then_inc(c_set, 1)
        dve.wait_ge(c_load, LOADED)
        steps = [1]

        def chain(ins):
            steps[0] += 1
            ins.then_inc(d_step, 1)
            dve.wait_ge(d_step, steps[0])

        dve.tensor_copy(mskf[:], mskT[:]).then_inc(mask_ok, 1)
        chain(dve.tensor_scalar(tn[:], phs[:], 1.0 / (2 * np.pi), ROUND, ALU.mult, ALU.add))
        chain(dve.tensor_scalar(tr[:], tn[:], ROUND, None, ALU.subtract))
        chain(dve.scalar_tensor_tensor(out=tn[:], in0=tr[:], scalar=-TWO_PI_1, in1=phs[:], op0=ALU.mult, op1=ALU.add))
        chain(dve.scalar_tensor_tensor(out=W[:], in0=tr[:], scalar=-TWO_PI_2, in1=tn[:], op0=ALU.mult, op1=ALU.add))
        chain(dve.scalar_tensor_tensor(out=tn[:], in0=tr[:], scalar=-TWO_PI_3, in1=W[:], op0=ALU.mult, op1=ALU.add))
        chain(dve.scalar_tensor_tensor(out=W[:], in0=tn[:], scalar=-1.0, in1=tn[:], op0=ALU.mult, op1=ALU.max))
        dve.tensor_scalar(tn[:], W[:], -1.0, float(np.pi / 2), ALU.mult, ALU.add).then_inc(arg_ok, 1)
        chain(dve.bn_stats(clsst[:], clsr[:]))
        chain(dve.bn_aggr(clsmv[:], clsst[:]))
        dve.tensor_scalar(clsrs[:], clsmv[:, 1:2], EPS, None, ALU.add).then_inc(clsvar_ok, 1)
        dve.wait_ge(clsrs_ok, 1)
        dve.tensor_scalar(clsz[:], clsr[:], clsmv[:, 0:1], clsrs[:], ALU.subtract, ALU.mult).then_inc(clsz_ok, 1)
        dve.wait_ge(cos_ok, 1)
        dve.tensor_tensor(W[:], tr[:], amp[:], ALU.mult).then_inc(w_ok, 1)
        dve.wait_ge(clsr_ok, 1)
        dve.tensor_copy(rbc[:], rT[:, CLS:N].broadcast_to([3 * HARM, NH])).then_inc(clsr_ok, 1)
        dve.wait_ge(clsqkv_ps, 1)
        for g in range(G):
            dve.tensor_scalar(qbd[:, g, :], bdm[:, g, :], ps[:, 4, g:g + 1], None, ALU.mult)
        chain(dve.tensor_scalar(clskt[:], ps[:, 5, 0:G], kone[:, 0:1], None, ALU.add))
        for g in range(G):
            dve.tensor_scalar(kbd[:, g, :], bdm[:, g, :], clskt[:, g:g + 1], None, ALU.mult)
        dve.tensor_copy(vbd[:, :, HD], eye[0:NH, 0:NH])
        dve.tensor_tensor(vbd[:, :, 0:HD], ps[0:NH, 3, 0:D].rearrange("p (h d) -> p h d", d=HD),
                          vbdm[:].rearrange("p (h d) -> p h d", d=HD), ALU.mult).then_inc(spread_ok, 1)
        mixer_ekv(0)
        mixer_y(0)
        mixer_norm(0)
        attn_norm(0)
        with dve.Fori(0, B - 1) as b:
            rest(b, True)
        rest(B - 1, False)
        dve.wait_ge(ot_ps, B + 1)
        o = ps[0:B, 3, :].rearrange("p (h s) -> p h s", s=SLOT)
        dve.reciprocal(rc[0:B, 0:NH], o[:, :, HD]).then_inc(rc_ok, 1)
        dve.wait_ge(rc_ok, B + 1)
        dve.tensor_tensor(on[0:B, 0, :].rearrange("p (h d) -> p h d", d=HD), o[:, :, 0:HD],
                          rc[0:B, 0:NH].rearrange("p (x o) -> p x o", o=1).broadcast_to([B, NH, HD]),
                          ALU.mult).then_inc(on_ok, 1)
        dve.wait_ge(o_ps, B + 1)
        dve.wait_ge(h2_out, 16 * B + 16)
        dve.memset(h2[:], 0.0).then_inc(d_step, 1)
        dve.wait_ge(d_step, steps[0] + 1)
        dve.tensor_tensor(h2[0:B, 0, :], ps[0:B, 7, 0:D], cls32[0:B, :], ALU.add).then_inc(h2_ok, 1)
        dve.wait_ge(h2_ok, B + 1)
        dve.bn_stats(st3[:, 0, :], h2[:, 0, :]).then_inc(ln3, 1)
        dve.wait_ge(ln3, 5 * B + 1)
        dve.bn_aggr(mv3[:, B * LT, :], st3[:, 0, :]).then_inc(ln3, 1)
        dve.wait_ge(ln3, 5 * B + 2)
        dve.tensor_scalar(rs3[:], mv3[:, :, 1], EPS, None, ALU.add).then_inc(ln3, 1)

    @block.gpsimd
    def _(pool):
        flat = lambda t: t[:].rearrange("p t d -> p (t d)")

        def mixer_affine(b):
            pool.wait_ge(ln1, b * 5 + 5)
            pool.tensor_tensor(rs[:], rs[:], mhalf[:], ALU.pow).then_inc(p1, 1)
            pool.wait_ge(hn_ok, b * 2 + 2)
            pool.tensor_tensor(flat(hn), flat(hn), lng[:], ALU.mult).then_inc(hg_ok, 1)
            pool.wait_ge(hg_ok, b + 1)
            pool.tensor_tensor(flat(hg), flat(hn), lnb[:], ALU.add).then_inc(h_st, 1)
            pool.wait_ge(ln2, b * 5 + 5)
            pool.tensor_tensor(rs2[:], rs2[:], mhalf[:], ALU.pow).then_inc(p2, 1)

        def keep_residual(b):
            pool.wait_ge(h_st, b + 1)
            if not isinstance(b, int) or b > 0:
                pool.wait_ge(h2_ok, b)
            pool.tensor_tensor(flat(hres), flat(hg), zeros[:], ALU.add).then_inc(hres_ok, 1)

        pool.wait_ge(mask_ok, 1)
        pool.wait_ge(c_load, LOADED)
        pool.tensor_tensor(wbT[:], wbT[:], mskf[:], ALU.mult).then_inc(wb_ok, 1)
        pool.wait_ge(half_ok, 1)
        pool.wait_ge(clsvar_ok, 1)
        pool.tensor_tensor(clsrs[:], clsrs[:], mhalf[0:1, 0:1], ALU.pow).then_inc(clsrs_ok, 1)
        mixer_affine(0)
        keep_residual(0)
        with pool.Fori(0, B - 1) as b:
            mixer_affine(b + 1)
            keep_residual(b + 1)
        pool.wait_ge(ln3, 5 * B + 3)
        pool.tensor_tensor(rs3[:], rs3[:], mh65[:], ALU.pow)


def stage_b(nc, ctx, sem, a, out, hscr, mv3, rs3, eye, ps):
    def sb(name, shape, dt=F32):
        return ctx.enter_context(nc.sbuf_tensor(name, shape, dt))

    UW = FT * 2 * UH + 2 * D
    whi = sb("whi", [P, NU, UW], F32R)
    wlo = sb("wlo", [P, NU, UW], F32R)
    rwr = sb("rwr", [P, FT * NE])
    rwh = sb("rwh", [P, FT, NE], F32R)
    rwl = sb("rwl", [P, FT, NE], F32R)
    ebias = sb("ebias", [P, LT * NE])
    before = sb("before", [P, LT * NE, NE])
    hb = sb("hb", [P, LT, D])
    z3 = sb("z3", [P, LT, D])
    zhi = sb("zhi", [P, FT, L], F32R)
    zlo = sb("zlo", [P, FT, L], F32R)
    sil = sb("sil", [P, 2, 2 * L])
    uu = sb("uu", [P, 3, 2 * L])
    hhi = sb("hhi", [P, 3, 2 * L], F32R)
    hlo = sb("hlo", [P, 3, 2 * L], F32R)
    acc = sb("acc", [P, LT, D])
    th = sb("th", [P, LT * NE])
    sc = sb("sc", [P, LT * NE])
    key = sb("key", [P, LT * NE])
    gt = sb("gt", [P, LT * NE, NE])
    eq = sb("eq", [P, LT * NE, NE])
    rank = sb("rank", [P, LT * NE])
    gate = sb("gate", [P, LT * NE])

    w_hi, w_lo, b_load, r_hi, r_lo = (sem(x) for x in ("w_hi", "w_lo", "b_load", "r_hi", "r_lo"))
    w_in = [sem("w_in0"), sem("w_in1")]
    hb_in, z3_ok, zt3_ps, zhi_ok, zlo_ok, hid_ps, sil_ok, uu_ok, hhi_ok, hlo_ok, out_ps, acc_ok, lg_ps, th_ok, gt_step, out_d = (
        sem(x) for x in ("hb_in", "z3_ok", "zt3_ps", "zhi_ok", "zlo_ok", "hid_ps", "sil_ok", "uu_ok", "hhi_ok", "hlo_ok",
                         "out_ps", "acc_ok", "lg_ps", "th_ok", "gt_step", "out_d"))
    gate_ok = sem("gate_ok")
    K = B + 1
    AN = 1 + NE
    GS = 6

    RAW = 2
    raw = [uu[:].rearrange("p a b -> p (a b)"), None]
    raw2 = sb("raw2", [P, UW])
    raw[1] = raw2[:]
    assert UW == 3 * 2 * L

    block = ctx.enter_context(nc.Block())

    @block.sync
    def _(sp):
        sp.dma_start(rwr[:], a["routerT"]).then_inc(b_load, 16)
        sp.dma_start(ebias[:], a["ebias"]).then_inc(b_load, 16)
        sp.dma_start(before[:], a["before"]).then_inc(b_load, 16)
        sp.dma_start(hb[:], hscr[0]).then_inc(hb_in, 16)
        for u in range(NU):
            if u >= RAW:
                sp.wait_ge(w_lo, u - RAW + 1)
            sp.dma_start(raw[u % RAW], a["wu"][u]).then_inc(w_in[u % RAW], 16)
        with sp.Fori(0, K - 1) as k:
            sp.wait_ge(acc_ok, k * AN + 1)
            sp.dma_start(hb[:], hscr[bass.ds(k + 1, 1)].rearrange("n p t d -> p (n t) d")).then_inc(hb_in, 16)
            sp.wait_ge(acc_ok, k * AN + AN)
            sp.dma_start(out[bass.ds(k, 1), 1:N, :].rearrange("n (t p) d -> p (n t) d", p=P), acc[:]).then_inc(out_d, 16)
        sp.wait_ge(acc_ok, K * AN)
        sp.dma_start(out[:, 0, :], acc[0:B, 0, :]).then_inc(out_d, 16)
        sp.wait_ge(out_d, 16 * K)

    @block.tensor
    def _(pe):
        def turn(k):
            pe.wait_ge(z3_ok, k + 1)
            for f in range(FT):
                for t in range(LT):
                    last = pe.transpose(ps[:, 6, f * L + t * P:f * L + (t + 1) * P], z3[:, t, f * P:(f + 1) * P], eye[:])
            last.then_inc(zt3_ps, 1)

        def router(k, nt):
            if not isinstance(k, int) or k > 0:
                pe.wait_ge(th_ok, k)
            for t in range(nt):
                mm = [(z_, w_, f) for z_, w_ in ((zhi, rwh), (zlo, rwh), (zhi, rwl)) for f in range(FT)]
                for n, (z_, w_, f) in enumerate(mm):
                    last = pe.matmul(ps[:, 7, t * NE:(t + 1) * NE], z_[:, f, t * P:(t + 1) * P], w_[:, f, :],
                                     start=(n == 0), stop=(n == len(mm) - 1))
            last.then_inc(lg_ps, 1)

        def hidden(k, u, w):
            if u == 0:
                pe.wait_ge(zhi_ok, k + 1)
                pe.wait_ge(zlo_ok, k + 1)
            if u >= 2 or not isinstance(k, int) or k > 0:
                pe.wait_ge(uu_ok, k * NU + u - 1)
            for c in range(2):
                for m in range(2):
                    mm = [(w_, z_, f) for w_, z_ in ((whi, zhi), (wlo, zhi), (whi, zlo)) for f in range(FT)]
                    for n, (w_, z_, f) in enumerate(mm):
                        at = f * 2 * UH + m * UH + c * P
                        last = pe.matmul(ps[:, 2 * (u % 2) + c, m * L:m * L + w], w_[:, u, at:at + P], z_[:, f, 0:w],
                                         start=(n == 0), stop=(n == len(mm) - 1))
            last.then_inc(hid_ps, 1)

        def output(k, u, nt):
            pe.wait_ge(hhi_ok, k * NU + u + 1)
            pe.wait_ge(hlo_ok, k * NU + u + 1)
            e = u - NS
            if u == 0 and (not isinstance(k, int) or k > 0):
                pe.wait_ge(acc_ok, k * AN)
            if e >= 1:
                pe.wait_ge(acc_ok, k * AN + e)
            n_bank = 4 if e < 0 else 4 + (e + 1) % 2
            for t in range(nt):
                mm = [(h_, w_, c) for h_, w_ in ((hhi, whi), (hlo, whi), (hhi, wlo)) for c in range(2)]
                for n, (h_, w_, c) in enumerate(mm):
                    at = FT * 2 * UH + c * D
                    start = (n == 0) if e >= 0 else (n == 0 and u == 0 and t == 0)
                    stop = n == len(mm) - 1 and (e >= 0 or u == NS - 1)
                    last = pe.matmul(ps[:, n_bank, t * D:(t + 1) * D], h_[:, u % 3, c * L + t * P:c * L + (t + 1) * P],
                                     w_[:, u, at:at + D], start=start, stop=stop, skip_group_check=True)
            last.then_inc(out_ps, 1)

        def blk(k, nt, nxt):
            for u in range(NU):
                hidden(k, u, nt * P)
                if u == 1:
                    router(k, nt)
                if u >= 2:
                    output(k, u - 2, nt)
                if u == 9 and nxt:
                    turn(k + 1)
            output(k, NU - 2, nt)
            output(k, NU - 1, nt)

        pe.wait_ge(w_lo, NU)
        pe.wait_ge(w_hi, NU)
        pe.wait_ge(r_lo, 1)
        pe.wait_ge(r_hi, 1)
        turn(0)
        blk(0, LT, True)
        with pe.Fori(1, K - 1) as k:
            blk(k, LT, True)
        blk(K - 1, 1, False)

    @block.scalar
    def _(act):
        def silu(k, u, w):
            act.wait_ge(hid_ps, k * NU + u + 1)
            if u >= 2 or not isinstance(k, int) or k > 0:
                act.wait_ge(uu_ok, k * NU + u - 1)
            act.activation(sil[:, u % 2, :].rearrange("p (c l) -> p c l", c=2)[:, :, 0:w],
                           ps[:, 2 * (u % 2):2 * (u % 2) + 2, 0:w], ACT.Silu).then_inc(sil_ok, 1)

        def head(k, u, w):
            act.wait_ge(uu_ok, k * NU + u + 1)
            if u >= 3 or not isinstance(k, int) or k > 0:
                act.wait_ge(out_ps, k * NU + u - 2)
            v = lambda t: t[:, u % 3, :].rearrange("p (c l) -> p c l", c=2)[:, :, 0:w]
            act.activation(v(hhi), v(uu), ACT.Copy).then_inc(hhi_ok, 1)

        def z_high(k):
            act.wait_ge(zt3_ps, k + 1)
            if not isinstance(k, int) or k > 0:
                act.wait_ge(hid_ps, k * NU)
            act.activation(zhi[:].rearrange("p f l -> p (f l)"), ps[:, 6, :], ACT.Copy).then_inc(zhi_ok, 1)

        def blk(k, nt, nxt):
            w = nt * P
            for u in range(NU):
                silu(k, u, w)
                if u == 2:
                    act.wait_ge(lg_ps, k + 1)
                    act.activation(th[:, 0:nt * NE], ps[:, 7, 0:nt * NE], ACT.Tanh, scale=0.5).then_inc(th_ok, 1)
                if u >= 1:
                    head(k, u - 1, w)
            if nxt:
                z_high(k + 1)
            head(k, NU - 1, w)

        act.wait_ge(b_load, 48)
        act.activation(rwh[:].rearrange("p f e -> p (f e)"), rwr[:], ACT.Copy).then_inc(r_hi, 1)
        for u in range(NU):
            act.wait_ge(w_in[u % RAW], 16 * (u // RAW) + 16)
            act.activation(whi[:, u, :], raw[u % RAW], ACT.Copy).then_inc(w_hi, 1)
        z_high(0)
        blk(0, LT, True)
        with act.Fori(1, K - 1) as k:
            blk(k, LT, True)
        blk(K - 1, 1, False)

    @block.vector
    def _(dve):
        def norm(k):
            dve.wait_ge(hb_in, k * 16 + 16)
            for t in range(LT):
                c = k * LT + t
                mean = mv3[:, bass.ds(c, 1), 0:1].rearrange("p t m -> p (t m)")
                root = rs3[:, bass.ds(c, 1)]
                last = dve.tensor_scalar(z3[:, t, :], hb[:, t, :], mean, root, ALU.subtract, ALU.mult)
            last.then_inc(z3_ok, 1)

        def z_low(k):
            dve.wait_ge(zhi_ok, k + 1)
            dve.tensor_tensor(zlo[:].rearrange("p f l -> p (f l)"), ps[:, 6, :],
                              zhi[:].rearrange("p f l -> p (f l)"), ALU.subtract).then_inc(zlo_ok, 1)

        def gates(k, nt):
            n = nt * NE
            dve.wait_ge(th_ok, k + 1)
            dve.tensor_scalar(sc[:, 0:n], th[:, 0:n], 0.5, 0.5, ALU.mult, ALU.add).then_inc(gt_step, 1)
            dve.wait_ge(gt_step, k * GS + 1)
            dve.tensor_tensor(key[:, 0:n], sc[:, 0:n], ebias[:, 0:n], ALU.add).then_inc(gt_step, 1)
            dve.wait_ge(gt_step, k * GS + 2)
            for t in range(nt):
                row = key[:, t * NE:(t + 1) * NE]
                other = row.rearrange("p (o e) -> p o e", o=1).broadcast_to([P, NE, NE])
                own = row.rearrange("p (e o) -> p e o", o=1).broadcast_to([P, NE, NE])
                dve.tensor_tensor(gt[:, t * NE:(t + 1) * NE, :], other, own, ALU.is_gt)
                last = dve.tensor_tensor(eq[:, t * NE:(t + 1) * NE, :], other, own, ALU.is_equal)
            last.then_inc(gt_step, 1)
            dve.wait_ge(gt_step, k * GS + 3)
            f = lambda t: t[:, 0:n, :].rearrange("p a b -> p (a b)")
            dve.tensor_tensor(f(eq), f(eq), f(before), ALU.mult).then_inc(gt_step, 1)
            dve.wait_ge(gt_step, k * GS + 4)
            dve.tensor_tensor(f(gt), f(gt), f(eq), ALU.add).then_inc(gt_step, 1)
            dve.wait_ge(gt_step, k * GS + 5)
            dve.tensor_reduce(rank[:, 0:n], gt[:, 0:n, :], AX_X, ALU.add).then_inc(gt_step, 1)
            dve.wait_ge(gt_step, k * GS + 6)
            dve.scalar_tensor_tensor(out=gate[:, 0:n], in0=rank[:, 0:n], scalar=1.5, in1=sc[:, 0:n], op0=ALU.is_lt,
                                     op1=ALU.mult).then_inc(gate_ok, 1)

        def product(k, u, w):
            dve.wait_ge(sil_ok, k * NU + u + 1)
            if u >= 3 or not isinstance(k, int) or k > 0:
                dve.wait_ge(hlo_ok, k * NU + u - 2)
            v = lambda t, s: t[:, s, :].rearrange("p (c l) -> p c l", c=2)[:, :, 0:w]
            dve.tensor_tensor(v(uu, u % 3), ps[:, 2 * (u % 2):2 * (u % 2) + 2, L:L + w], v(sil, u % 2),
                              ALU.mult).then_inc(uu_ok, 1)

        def gather(k, u, nt):
            e = u - NS
            if e < 0 and u < NS - 1:
                return
            dve.wait_ge(out_ps, k * NU + u + 1)
            fl = lambda t: t[:, 0:nt, :].rearrange("p t d -> p (t d)")
            if e < 0:
                if not isinstance(k, int) or k > 0:
                    dve.wait_ge(out_d, 16 * k)
                dve.tensor_tensor(fl(acc), ps[:, 4, 0:nt * D], fl(hb), ALU.add).then_inc(acc_ok, 1)
                return
            if e == 0:
                dve.wait_ge(gate_ok, k + 1)
            dve.wait_ge(acc_ok, k * AN + e + 1)
            for t in range(nt):
                last = dve.scalar_tensor_tensor(out=acc[:, t, :], in0=ps[:, 4 + (e + 1) % 2, t * D:(t + 1) * D],
                                                scalar=gate[:, t * NE + e:t * NE + e + 1], in1=acc[:, t, :],
                                                op0=ALU.mult, op1=ALU.add)
            last.then_inc(acc_ok, 1)

        def blk(k, nt, nxt):
            for u in range(NU):
                product(k, u, nt * P)
                if u == 3:
                    gates(k, nt)
                if u >= 3:
                    gather(k, u - 3, nt)
                if u == 8 and nxt:
                    norm(k + 1)
            if nxt:
                z_low(k + 1)
            for u in range(NU - 3, NU):
                gather(k, u, nt)

        dve.wait_ge(r_hi, 1)
        dve.tensor_tensor(rwl[:].rearrange("p f e -> p (f e)"), rwr[:], rwh[:].rearrange("p f e -> p (f e)"),
                          ALU.subtract).then_inc(r_lo, 1)
        norm(0)
        for u in range(NU):
            dve.wait_ge(w_hi, u + 1)
            dve.tensor_tensor(wlo[:, u, :], raw[u % RAW], whi[:, u, :], ALU.subtract).then_inc(w_lo, 1)
        z_low(0)
        blk(0, LT, True)
        with dve.Fori(1, K - 1) as k:
            blk(k, LT, True)
        blk(K - 1, 1, False)

    @block.gpsimd
    def _(pool):
        def tail(k, u, w):
            pool.wait_ge(hhi_ok, k * NU + u + 1)
            v = lambda t: t[:, u % 3, :].rearrange("p (c l) -> p c l", c=2)[:, :, 0:w]
            pool.tensor_tensor(v(hlo), v(uu), v(hhi), ALU.subtract).then_inc(hlo_ok, 1)

        with pool.Fori(0, K - 1) as k:
            for u in range(NU):
                tail(k, u, L)
        for u in range(NU):
            tail(K - 1, u, P)


def layout(i):
    f = lambda x: np.ascontiguousarray(x)
    z = lambda *s: np.zeros(s, np.float32)
    t = {k[3:]: np.asarray(v) for k, v in i.items() if k.startswith("L0_")}
    o = {"x": f(i["x"])}
    tiles = lambda m: f(m.reshape(-1, P, m.shape[1]).transpose(1, 0, 2))
    wkv = z(C + 1, 2 * C)
    wkv[:C, :C], wkv[:C, C:] = t["tok_Wk_w"].T, t["tok_Wv_w"].T
    wkv[C, :C], wkv[C, C:] = t["tok_Wk_b"], t["tok_Wv_b"]
    o["wkv"] = wkv
    o["wq"] = f(np.concatenate([t["tok_Wq_w"].T, t["tok_Wq_b"][None]]))
    o["idn"] = f(np.concatenate([np.tile(np.eye(C, dtype=np.float32), (1, H)), t["tok_out_b"][None]]))
    o["wbT"] = tiles(t["tok_w_bias"].T)
    o["mskT"] = tiles(t["tok_local_mask"].T)
    o["outw"] = tiles(t["tok_out_w"])
    o["lng"] = f(np.tile(t["tok_ln_g"][None], (P, LT)))
    o["lnb"] = f(np.tile(t["tok_ln_b"][None], (P, LT)))
    o["basT"] = tiles(np.concatenate([t["attn_basis_" + n].T for n in "qkv"], axis=1))
    o["basoT"] = tiles(t["attn_basis_o"].T)
    for name, src in (("phs", "phase"), ("amp", "amp")):
        w = z(P, 512)
        for r, n in enumerate("qk"):
            w[r * HARM:(r + 1) * HARM].reshape(HARM, NH, SLOT)[:, :, :HD] = t[f"attn_{src}_{n}"].T.reshape(HARM, NH, HD)
        for r, n in ((2, "v"), (3, "o")):
            w[r * HARM:(r + 1) * HARM, :D] = t[f"attn_{src}_{n}"].T
        o[name] = w
    p = np.arange(P)
    heads = np.arange(NH)
    o["kone"] = f((p % SLOT == HD)[:, None].astype(np.float32))
    group_head = HPG * np.arange(G)[:, None] + p[None] // SLOT
    mine = (group_head[None] == heads[:, None, None]).astype(np.float32)
    o["selm"] = f(mine * (p % SLOT == HD))
    o["bdm"] = f(mine.transpose(2, 1, 0))
    o["vbdm"] = f((np.arange(D)[None] // HD == heads[:, None]).astype(np.float32))
    o["eye"] = np.eye(P, dtype=np.float32)
    cls = np.asarray(i["cls_tok"]).reshape(1, D)
    o["clsr"] = f(cls)
    o["cls32"] = f(np.tile(cls, (P, 1)))
    sw = [np.asarray(t["ffn_shared_w%d" % n]) for n in (1, 2, 3)]
    wu = z(NU, P, FT * 2 * UH + 2 * D)
    for u in range(NU):
        if u < NS:
            r = slice(u * UH, (u + 1) * UH)
            w_in, w_out = np.concatenate([sw[0][r], sw[1][r]]), sw[2][:, r]
        else:
            w_in, w_out = t["ffn_w12"][u - NS], t["ffn_w3"][u - NS]
        wu[u, :, :FT * 2 * UH] = tiles(w_in.T).reshape(P, -1)
        wu[u, :, FT * 2 * UH:] = tiles(w_out.T).reshape(P, -1)
    o["wu"] = wu
    o["routerT"] = tiles(t["ffn_router_w"].T).reshape(P, -1)
    o["ebias"] = f(np.tile(t["ffn_expert_bias"][None], (P, LT)))
    e = np.arange(NE)
    o["before"] = f(np.tile((e[None] < e[:, None]).astype(np.float32)[None], (P, LT, 1)))
    return o


def kernel(**inputs):
    import numpy as _np
    import concourse.bacc as _bacc
    from concourse import mybir as _mybir
    from concourse.bass_utils import run_bass_kernel_spmd as _run

    nc = _bacc.Bacc("TRN2", target_bir_lowering=False, num_devices=1)
    arrays = {"in_" + k: v for k, v in layout({k: _np.asarray(v) for k, v in inputs.items()}).items()}
    aps = {k[3:]: nc.dram_tensor(k, v.shape, _mybir.dt.from_np(v.dtype), kind="ExternalInput").ap()
           for k, v in arrays.items()}
    out = nc.dram_tensor("out", (B, N, D), F32, kind="ExternalOutput").ap()
    build(nc, aps, out)
    r = _run(nc, [arrays], core_ids=[0])
    return r.results[0]["out"]
```

```python
from contextlib import ExitStack

import numpy as np

import concourse.bass as bass
from concourse import mybir

F32 = mybir.dt.float32
F32R = mybir.dt.float32r
U8 = mybir.dt.uint8
ALU = mybir.AluOpType
ACT = mybir.ActivationFunctionType
AX_X = mybir.AxisListType.X

B, C, L, H = 32, 64, 256, 4
D = C * H
P = 128
LT = L // P
FT = D // P
NH, HD, HARM = 16, 16, 32
SLOT = 32
G = NH * SLOT // P
HPG = NH // G
HPF = P // HD
SLOT2 = 64
G2 = NH * SLOT2 // P
NP = L + 2
N = L + 1
CLS = L
NE = 8
UH = 256
NS = 1024 // UH
NU = NS + NE
EPS = 1e-5
TWO_PI_1 = 6.28125
TWO_PI_2 = float(np.float32(0.0019350051879882812))
TWO_PI_3 = float(2 * np.pi - TWO_PI_1 - TWO_PI_2)
ROUND = 12582912.0


def build(nc, a, out):
    with ExitStack() as whole:
        def sem(name):
            return whole.enter_context(nc.semaphore(name))

        hscr = nc.dram_tensor("hscr", [B + 1, P, LT, D], F32, kind="Internal").ap()
        mv3 = whole.enter_context(nc.sbuf_tensor("mv3", [P, (B + 1) * LT, 2], F32))
        rs3 = whole.enter_context(nc.sbuf_tensor("rs3", [P, (B + 1) * LT], F32))
        eye = whole.enter_context(nc.sbuf_tensor("eye", [P, P], F32))
        mhalf = whole.enter_context(nc.sbuf_tensor("mhalf", [P, 2], F32))
        ps = whole.enter_context(nc.psum_tensor("ps", [P, 8, 512], F32))
        with ExitStack() as ctx:
            stage_a(nc, ctx, sem, a, hscr, mv3, rs3, eye, mhalf, ps)
        with ExitStack() as ctx:
            stage_b(nc, ctx, sem, a, out, hscr, mv3, rs3, eye, ps)


def stage_a(nc, ctx, sem, a, hscr, mv3, rs3, eye, mhalf, ps):
    def sb(name, shape, dt=F32):
        return ctx.enter_context(nc.sbuf_tensor(name, shape, dt))

    xs = sb("xs", [P, L * H])
    wkv = sb("wkv", [P, 2 * C])
    wq = sb("wq", [P, C])
    idn = sb("idn", [P, D])
    wbT = sb("wbT", [P, LT, L])
    mskT = sb("mskT", [P, LT, L], U8)
    mskf = sb("mskf", [P, LT, L])
    ewT = sb("ewT", [P, LT, L])
    outw = sb("outw", [P, FT, D])
    lng = sb("lng", [P, LT * D])
    lnb = sb("lnb", [P, LT * D])
    basT = sb("basT", [P, FT, 3 * HARM])
    basoT = sb("basoT", [P, FT, HARM])
    phs = sb("phs", [P, D])
    amp = sb("amp", [P, D])
    W = sb("W", [P, D])
    Wz = sb("Wz", [3 * HARM, 3, D])
    tr = sb("tr", [P, D])
    tn = sb("tn", [P, D])
    selw = sb("selw", [P, 4, 4, P])
    sel = sb("sel", [P, 4, 4, P], F32R)
    bdm = sb("bdm", [P, FT, P])
    mones = sb("mones", [P, NH, P], F32R)
    eyer = sb("eyer", [P, P], F32R)
    vbdm = sb("vbdm", [NH, D])
    clsr = sb("clsr", [1, D])
    cls32 = sb("cls32", [P, D])
    clsst = sb("clsst", [1, 6])
    clsmv = sb("clsmv", [1, 2])
    clsrs = sb("clsrs", [1, 1])
    clsz = sb("clsz", [1, D])
    one1 = sb("one1", [1, 1])
    zeros = sb("zeros", [P, LT * D])
    tick = sb("tick", [P, 1])
    mvb = sb("mvb", [P, LT, 2])
    mh65 = sb("mh65", [P, (B + 1) * LT])
    hres = sb("hres", [P, LT, D])
    h2 = sb("h2", [P, LT, D])
    rbc = sb("rbc", [3 * HARM, NH])
    ek = sb("ek", [P, LT, D])
    ekv = sb("ekv", [P, LT, D])
    tq = sb("tq", [P, FT, L])
    rden = sb("rden", [P, FT, L])
    y1 = sb("y1", [P, FT, L])
    yT = sb("yT", [P, FT, L])
    hn = sb("hn", [P, LT, D])
    hg = sb("hg", [P, LT, D])
    z = sb("z", [P, LT, D])
    st = sb("st", [P, LT, 6])
    mv = sb("mv", [P, LT, 2])
    rs = sb("rs", [P, LT])
    st2 = sb("st2", [P, LT, 6])
    mv2 = sb("mv2", [P, LT, 2])
    rs2 = sb("rs2", [P, LT])
    st3 = sb("st3", [P, LT, 6])
    zT = sb("zT", [P, FT, N])
    rT = sb("rT", [3 * HARM, N])
    qhi = sb("qhi", [P, FT, NP], F32R)
    qlo = sb("qlo", [P, FT, NP], F32R)
    khi = sb("khi", [P, FT, NP], F32R)
    klo = sb("klo", [P, FT, NP], F32R)
    q2 = sb("q2", [P, G2, NP], F32R)
    km = sb("km", [P, G2, 2, NP], F32R)
    bdf = sb("bdf", [P, 2, FT, P])
    bdh = sb("bdh", [P, 2, FT, P], F32R)
    bdl = sb("bdl", [P, 2, FT, P], F32R)
    negr = sb("negr", [P, NP], F32R)
    negc_ok, x_rows = sem("negc_ok"), sem("x_rows")
    negc = sb("negc", [NH, 1])
    vbd = sb("vbd", [NH, NH, SLOT])
    va = sb("va", [P, LT, NH, SLOT])
    mx = sb("mx", [P, LT, NH])
    pT = sb("pT", [P, NH, LT, N])
    pc = sb("pc", [NH, N])
    og = sb("og", [P, G, N])
    rc = sb("rc", [P, LT * NH])
    on = sb("on", [P, LT, D])
    onT = sb("onT", [P, FT, L])
    ro = sb("ro", [P, L])
    clso = sb("clso", [P, G, B])

    (c_load, c_set, d_step, half_ok, mask_ok, wb_ok, ew_ok, arg_ok, cos_ok, w_ok, clsvar_ok, clsrs_ok, clsz_ok, clsT_ps,
     clsT_ok, clsr_ps, clsr_ok, clsqkv_ps, spread_ok) = (
        sem(x) for x in ("c_load", "c_set", "d_step", "half_ok", "mask_ok", "wb_ok", "ew_ok", "arg_ok", "cos_ok", "w_ok",
                         "clsvar_ok", "clsrs_ok", "clsz_ok", "clsT_ps", "clsT_ok", "clsr_ps", "clsr_ok", "clsqkv_ps",
                         "spread_ok"))
    x_in, h2_out, hres_ok = sem("x_in"), sem("h2_out"), sem("hres_ok")
    kvq_ps, ek_ok, tq_ok, ekv_ok, nd_ps = (sem(x) for x in ("kvq_ps", "ek_ok", "tq_ok", "ekv_ok", "nd_ps"))
    y_step, y_ok, h_ps, ln1, hn_ok, h_st, ln2, z_ok, zt_ps, zt_ok = (
        sem(x) for x in ("y_step", "y_ok", "h_ps", "ln1", "hn_ok", "h_st", "ln2", "z_ok", "zt_ps", "zt_ok"))
    p1, p2, hg_ok = sem("p1"), sem("p2"), sem("hg_ok")
    r_ps, r_ok, qk_ps, v_ps, v_ok, hi_ok, lo_ok, rep_ps, rep_ok, repd_ok = (
        sem(x) for x in ("r_ps", "r_ok", "qk_ps", "v_ps", "v_ok", "hi_ok", "lo_ok", "rep_ps", "rep_ok", "repd_ok"))
    mx_ps, mx_ok, mt_ps, negm_ok = (sem(x) for x in ("mx_ps", "mx_ok", "mt_ps", "negm_ok"))
    s_ps, s_ok, pv_ps, og_ok, ot_ps, rc_ok, on_ok, onT_ps, onT_ok, ro_ps, ro_ok, o_ps, h2_ok, ln3, clso_ok = (
        sem(x) for x in ("s_ps", "s_ok", "pv_ps", "og_ok", "ot_ps", "rc_ok", "on_ok", "onT_ps", "onT_ok",
                         "ro_ps", "ro_ok", "o_ps", "h2_ok", "ln3", "clso_ok"))

    loads = [(wkv, a["wkv"]), (wq, a["wq"]), (idn, a["idn"]), (wbT, a["wbT"]), (mskT, a["mskT"]),
             (outw, a["outw"]), (lng, a["lng"]), (lnb, a["lnb"]), (basT, a["basT"]), (basoT, a["basoT"]),
             (phs, a["phs"]), (amp, a["amp"]), (selw, a["sel"]), (bdm, a["bdm"]),
             (vbdm, a["vbdm"]), (eye, a["eye"]), (clsr, a["clsr"]), (cls32, a["cls32"])]
    LOADED = 16 * len(loads)

    def bank(n, w=512):
        return ps[:, n, 0:w]

    def xcol(t, h):
        return xs[:, h:L * H:H] if t is None else xs[:, t * P * H + h:(t + 1) * P * H:H]

    block = ctx.enter_context(nc.Block())

    @block.sync
    def _(sp):
        for dst, src in loads:
            sp.dma_start(dst[:], src).then_inc(c_load, 16)
        sp.dma_start(xs[0:C, :], a["x"][0].rearrange("c l h -> c (l h)")).then_inc(x_in, 16)
        sp.wait_ge(half_ok, 1)
        sp.dma_start(hscr[B], h2[:]).then_inc(h2_out, 16)
        with sp.Fori(1, B) as b:
            sp.wait_ge(h_ps, b)
            sp.dma_start(xs[0:C, :], a["x"][bass.ds(b, 1)].rearrange("n c l h -> (n c) (l h)")).then_inc(x_in, 16)
            sp.wait_ge(h2_ok, b)
            sp.dma_start(hscr[bass.ds(b - 1, 1)].rearrange("n p t d -> p (n t) d"), h2[:]).then_inc(h2_out, 16)
        for b in (B - 1, B):
            sp.wait_ge(h2_ok, b + 1)
            sp.dma_start(hscr[b], h2[:]).then_inc(h2_out, 16)
        sp.wait_ge(h2_out, 16 * (B + 2))

    @block.tensor
    def _(pe):
        def mixer_kvq(b):
            pe.wait_ge(x_in, b * 16 + 16)
            if not isinstance(b, int) or b > 0:
                pe.wait_ge(zt_ok, b)
            for t in range(LT):
                for h in range(H):
                    pe.matmul(ps[:, t, h * 2 * C:(h + 1) * 2 * C], xcol(t, h), wkv[:], start=True, stop=True)
            for f in range(FT):
                for hh in range(2):
                    last = pe.matmul(ps[hh * C:(hh + 1) * C, 2, f * L:(f + 1) * L], wq[:], xcol(None, 2 * f + hh),
                                     start=True, stop=True)
            last.then_inc(kvq_ps, 1)

        def mixer_sums(b):
            pe.wait_ge(ek_ok, b + 1)
            pe.wait_ge(ekv_ok, b + 1)
            for n, src in ((0, ekv), (1, ek)):
                for f in range(FT):
                    for s in range(LT):
                        last = pe.matmul(ps[:, n, f * L:(f + 1) * L], src[:, s, f * P:(f + 1) * P], ewT[:, s, :],
                                         start=(s == 0), stop=(s == LT - 1))
            last.then_inc(nd_ps, 1)

        def mixer_out(b):
            pe.wait_ge(y_ok, b + 1)
            pe.wait_ge(tq_ok, b + 1)
            for t in range(LT):
                o = ps[:, 2, t * D:(t + 1) * D]
                for f in range(FT):
                    pe.matmul(o, yT[:, f, t * P:(t + 1) * P], outw[:, f, :], start=(f == 0), stop=False)
                for h in range(H):
                    last = pe.matmul(o[:, h * C:(h + 1) * C], xcol(t, h), idn[:, h * C:(h + 1) * C],
                                     start=False, stop=(h == H - 1))
            last.then_inc(h_ps, 1)

        def mixer_turn(b):
            pe.wait_ge(z_ok, b + 1)
            for f in range(FT):
                for t in range(LT):
                    last = pe.transpose(ps[:, 0, f * L + t * P:f * L + (t + 1) * P], z[:, t, f * P:(f + 1) * P], eye[:])
            last.then_inc(zt_ps, 1)

        def resonances(b):
            pe.wait_ge(zt_ok, b + 1)
            if not isinstance(b, int) or b > 0:
                pe.wait_ge(h2_ok, b)
            for f in range(FT):
                last = pe.matmul(ps[0:3 * HARM, 7, 0:N], basT[:, f, :], zT[:, f, :], start=(f == 0), stop=(f == FT - 1))
            last.then_inc(r_ps, 1)

        def heads_qkv(b):
            pe.wait_ge(r_ok, b + 1)
            for n in range(2):
                for f in range(FT):
                    last = pe.matmul(ps[:, 3 + 2 * n + f, 0:N], Wz[:, n, f * P:(f + 1) * P], rT[:], start=True, stop=True)
            last.then_inc(qk_ps, 1)
            for t in range(LT):
                last = pe.matmul(ps[:, 7, t * D:(t + 1) * D], rT[:, t * P:(t + 1) * P], Wz[:, 2, :], start=True, stop=True)
            last.then_inc(v_ps, 1)

        def stack(b, n):
            if n == 0:
                pe.wait_ge(lo_ok, 2 * b + 2)
            else:
                pe.wait_ge(rep_ok, 4 * b + n)
            if n == 3:
                pe.wait_ge(repd_ok, 2 * b + 1)
            kind, f = 2 * (n // 2), n % 2
            hi, lo = (qhi, qlo) if n < 2 else (khi, klo)
            for g in range(4):
                pe.matmul(ps[:, 3 + g, 0:NP], sel[:, kind, g, :], hi[:, f, :], start=True, stop=False)
                last = pe.matmul(ps[:, 3 + g, 0:NP], sel[:, kind + 1, g, :], lo[:, f, :], start=False, stop=True)
            last.then_inc(rep_ps, 1)

        MXN = LT * NH // 2 + 1

        def maxima(b):
            pe.wait_ge(rep_ok, 4 * b + 4)
            pe.wait_ge(repd_ok, 2 * b + 2)
            pe.wait_ge(v_ok, b + 1)
            mm = [(x, y, f) for x, y in ((bdh, khi), (bdh, klo), (bdl, khi)) for f in range(FT)]
            for n, (x, y, f) in enumerate(mm):
                last = pe.matmul(ps[:, 7, 0:NP], x[:, 0, f, :], y[:, f, :], start=(n == 0), stop=(n == len(mm) - 1))
            last.then_inc(mx_ps, 1)
            n = 0
            for t in range(LT):
                for h in range(0, NH, 2):
                    if n >= 2:
                        pe.wait_ge(mx_ok, b * MXN + n)
                    for k in range(2):
                        last = pe.matmul(ps[:, 3 + 2 * (n % 2) + k, 0:NP], q2[:, h // 2, t * P:(t + 1) * P],
                                         km[:, h // 2, k, :], start=True, stop=True)
                    last.then_inc(mx_ps, 1)
                    n += 1

        def turn_maxima(b):
            pe.wait_ge(mx_ok, b * MXN + MXN)
            for t in range(LT):
                last = pe.transpose(ps[0:NH, 7, t * P:(t + 1) * P], mx[:, t, :], eye[:])
            last.then_inc(mt_ps, 1)

        SN = NH + 1

        def scores(b, h):
            if h >= 2:
                pe.wait_ge(s_ok, b * SN + h)
            for t in range(LT):
                o = ps[:, 3 + 2 * (h % 2) + t, 0:NP]
                pe.matmul(o, km[:, h // 2, h % 2, t * P:(t + 1) * P], q2[:, h // 2, :], start=True, stop=False)
                last = pe.matmul(o, mones[:, h, :], negr[:], start=False, stop=True)
            last.then_inc(s_ps, 1)

        def cls_scores(b):
            pe.wait_ge(negm_ok, b + 1)
            mm = [(x, y, f) for x, y in ((bdh, qhi), (bdh, qlo), (bdl, qhi)) for f in range(FT)]
            for n, (x, y, f) in enumerate(mm):
                pe.matmul(ps[:, 7, 0:NP], x[:, 1, f, :], y[:, f, :], start=(n == 0), stop=False)
            pe.matmul(ps[:, 7, 0:NP], eyer[:], negr[:], start=False, stop=True).then_inc(s_ps, 1)

        def values(b, g):
            pe.wait_ge(s_ok, b * SN + 1 + HPG * (g + 1))
            if g > 0:
                pe.wait_ge(og_ok, b * G + g)
            pe.matmul(ps[:, 7, 0:N], vbd[:, g * HPG:(g + 1) * HPG, :].rearrange("p h s -> p (h s)"), pc[:], start=True,
                      stop=False, skip_group_check=True)
            for j in range(HPG):
                h = g * HPG + j
                for t in range(LT):
                    last = pe.matmul(ps[SLOT * j:SLOT * (j + 1), 7, 0:N], va[:, t, h, :], pT[:, h, t, :], start=False,
                                     stop=(t == LT - 1), skip_group_check=True)
            last.then_inc(pv_ps, 1)

        def attend_out(b):
            pe.wait_ge(og_ok, b * G + G)
            pe.wait_ge(s_ok, b * SN + SN)
            for t in range(LT):
                for g in range(G):
                    last = pe.transpose(ps[:, 3 + t, g * P:(g + 1) * P], og[:, g, t * P:(t + 1) * P], eye[:])
            last.then_inc(ot_ps, 1)
            pe.wait_ge(on_ok, b + 1)
            for f in range(FT):
                for t in range(LT):
                    last = pe.transpose(ps[:, 5, f * L + t * P:f * L + (t + 1) * P], on[:, t, f * P:(f + 1) * P], eye[:])
            last.then_inc(onT_ps, 1)
            pe.wait_ge(onT_ok, b + 1)
            for f in range(FT):
                last = pe.matmul(ps[96:P, 6, 0:L], basoT[:, f, :], onT[:, f, :], start=(f == 0), stop=(f == FT - 1))
            last.then_inc(ro_ps, 1)
            pe.wait_ge(ro_ok, b + 1)
            for t in range(LT):
                last = pe.matmul(ps[:, 7, t * D:(t + 1) * D], ro[96:P, t * P:(t + 1) * P], W[96:P, :], start=True,
                                 stop=True)
            last.then_inc(o_ps, 1)

        pe.wait_ge(c_load, LOADED)
        pe.wait_ge(c_set, 1)
        pe.wait_ge(clsz_ok, 1)
        for f in range(FT):
            last = pe.matmul(ps[:, 6, f:f + 1], clsz[:, f * P:(f + 1) * P], one1[:], start=True, stop=True)
        last.then_inc(clsT_ps, 1)
        pe.wait_ge(clsT_ok, 1)
        for f in range(FT):
            last = pe.matmul(ps[0:3 * HARM, 5, 16:17], basT[:, f, :], zT[:, f, CLS:N], start=(f == 0), stop=(f == FT - 1))
        last.then_inc(clsr_ps, 1)
        pe.wait_ge(clsr_ok, 2)
        pe.wait_ge(w_ok, 1)
        for n in range(2):
            for f in range(FT):
                pe.matmul(ps[:, 4, n * FT + f:n * FT + f + 1], Wz[:, n, f * P:(f + 1) * P], rT[:, CLS:N], start=True,
                          stop=True)
        pe.matmul(ps[0:NH, 3, 0:D], rbc[:], Wz[:, 2, :], start=True,
                  stop=True).then_inc(clsqkv_ps, 1)
        mixer_kvq(0)
        pe.wait_ge(ew_ok, 1)
        mixer_sums(0)
        mixer_out(0)
        mixer_turn(0)
        pe.wait_ge(spread_ok, 1)
        resonances(0)

        def image(b, nxt):
            heads_qkv(b)
            if nxt:
                mixer_kvq(b + 1)
            for n in range(4):
                stack(b, n)
            maxima(b)
            if nxt:
                mixer_sums(b + 1)
            turn_maxima(b)
            cls_scores(b)
            for h in range(NH):
                scores(b, h)
                if h % HPG == HPG - 1 and h > HPG:
                    values(b, h // HPG - 1)
                if h == 9 and nxt:
                    mixer_out(b + 1)
            values(b, G - 1)
            if nxt:
                mixer_turn(b + 1)
            attend_out(b)
            if nxt:
                resonances(b + 1)

        with pe.Fori(0, B - 1) as b:
            image(b, True)
        image(B - 1, False)
        pe.wait_ge(clso_ok, B + 1)
        for g in range(G):
            last = pe.transpose(ps[0:B, 3, g * P:(g + 1) * P], clso[:, g, :], eye[:])
        last.then_inc(ot_ps, 1)
        pe.wait_ge(on_ok, B + 1)
        for f in range(FT):
            last = pe.transpose(ps[:, 5, f * B:(f + 1) * B], on[0:B, 0, f * P:(f + 1) * P], eye[0:B, 0:B])
        last.then_inc(onT_ps, 1)
        pe.wait_ge(onT_ok, B + 1)
        for f in range(FT):
            last = pe.matmul(ps[96:P, 6, 0:B], basoT[:, f, :], onT[:, f, 0:B], start=(f == 0), stop=(f == FT - 1))
        last.then_inc(ro_ps, 1)
        pe.wait_ge(ro_ok, B + 1)
        pe.wait_ge(h2_ok, B)
        pe.matmul(ps[0:B, 7, 0:D], ro[96:P, 0:B], W[96:P, :], start=True, stop=True).then_inc(o_ps, 1)

    @block.scalar
    def _(act):
        def mixer_exps(b):
            act.wait_ge(kvq_ps, b + 1)
            kv = ps[:, 0:LT, :].rearrange("p t (h w) -> p t h w", h=H)
            act.activation(ek[:].rearrange("p t (h w) -> p t h w", h=H), kv[:, :, :, 0:C], ACT.Exp).then_inc(ek_ok, 1)
            act.activation(tq[:].rearrange("p f l -> p (f l)"), bank(2), ACT.Tanh, scale=0.5).then_inc(tq_ok, 1)

        def mixer_turned(b):
            act.wait_ge(zt_ps, b + 1)
            act.activation(zT[:, :, 0:L], bank(0).rearrange("p (f l) -> p f l", f=FT), ACT.Copy).then_inc(zt_ok, 1)

        def rest(b, nxt):
            act.wait_ge(r_ps, b + 1)
            act.activation(rT[:], ps[0:3 * HARM, 7, 0:N], ACT.Copy).then_inc(r_ok, 1)
            act.wait_ge(qk_ps, b + 1)
            for n, hi in ((0, qhi), (1, khi)):
                act.activation(hi[:, :, 0:N], ps[:, 3 + 2 * n:5 + 2 * n, 0:N], ACT.Copy).then_inc(hi_ok, 1)
            act.wait_ge(v_ps, b + 1)
            act.activation(va[:, :, :, 0:HD], bank(7).rearrange("p (t h d) -> p t h d", t=LT, h=NH),
                           ACT.Copy).then_inc(v_ok, 1)
            if nxt:
                mixer_exps(b + 1)
            for n in range(4):
                act.wait_ge(rep_ps, 4 * b + n + 1)
                if n < 2:
                    act.activation(q2[:, 4 * n:4 * n + 4, :], ps[:, 3:7, 0:NP], ACT.Copy).then_inc(rep_ok, 1)
                else:
                    g = 4 * (n - 2)
                    act.activation(km[0:SLOT2, g:g + 4, 0, :], ps[0:SLOT2, 3:7, 0:NP], ACT.Copy).then_inc(rep_ok, 1)
            act.wait_ge(mt_ps, b + 1)
            act.activation(negr[0:NH, 0:L], ps[0:NH, 7, 0:L], ACT.Copy).then_inc(negm_ok, 1)
            act.wait_ge(s_ps, b * (NH + 1) + 1)
            act.activation(pc[:], ps[0:NH, 7, 0:N], ACT.Exp, scale=HD ** -0.5).then_inc(s_ok, 1)
            for h in range(NH):
                act.wait_ge(s_ps, b * (NH + 1) + h + 2)
                n = 3 + 2 * (h % 2)
                act.activation(pT[:, h, :, :], ps[:, n:n + LT, 0:N], ACT.Exp, scale=HD ** -0.5).then_inc(s_ok, 1)
                if h % HPG == HPG - 1 and h > HPG:
                    take_group(b, h // HPG - 1)
            take_group(b, G - 1)
            if nxt:
                mixer_turned(b + 1)
            act.wait_ge(onT_ps, b + 1)
            act.activation(onT[:].rearrange("p f l -> p (f l)"), bank(5), ACT.Copy).then_inc(onT_ok, 1)
            act.wait_ge(ro_ps, b + 1)
            act.activation(ro[96:P, :], ps[96:P, 6, 0:L], ACT.Copy).then_inc(ro_ok, 1)

        def take_group(b, g):
            act.wait_ge(pv_ps, b * G + g + 1)
            if g == 0:
                act.wait_ge(clso_ok, b + 1)
            act.activation(og[:, g, :], ps[:, 7, 0:N], ACT.Copy).then_inc(og_ok, 1)

        act.wait_ge(arg_ok, 1)
        act.activation(tr[:], tn[:], ACT.Sin).then_inc(cos_ok, 1)
        act.wait_ge(wb_ok, 1)
        act.activation(ewT[:], wbT[:], ACT.Exp).then_inc(ew_ok, 1)
        act.wait_ge(clsT_ps, 1)
        act.activation(zT[:, :, CLS:N], ps[:, 6, 0:FT].rearrange("p (f o) -> p f o", o=1), ACT.Copy).then_inc(clsT_ok, 1)
        act.wait_ge(clsr_ps, 1)
        act.activation(rT[:, CLS:N], ps[0:3 * HARM, 5, 16:17], ACT.Copy).then_inc(clsr_ok, 1)
        mixer_exps(0)
        mixer_turned(0)
        with act.Fori(0, B - 1) as b:
            rest(b, True)
        rest(B - 1, False)
        act.wait_ge(onT_ps, B + 1)
        act.activation(onT[:, :, 0:B], ps[:, 5, 0:FT * B].rearrange("p (f b) -> p f b", f=FT), ACT.Copy).then_inc(onT_ok, 1)
        act.wait_ge(ro_ps, B + 1)
        act.activation(ro[96:P, 0:B], ps[96:P, 6, 0:B], ACT.Copy).then_inc(ro_ok, 1)

    @block.vector
    def _(dve):
        MXN = LT * NH // 2 + 1

        def mixer_ekv(b):
            dve.wait_ge(ek_ok, b + 1)
            kv = ps[:, 0:LT, :].rearrange("p t (h w) -> p t h w", h=H)
            dve.tensor_tensor(ekv[:].rearrange("p t (h w) -> p t h w", h=H), kv[:, :, :, C:2 * C],
                              ek[:].rearrange("p t (h w) -> p t h w", h=H), ALU.mult).then_inc(ekv_ok, 1)

        def mixer_y(b):
            dve.wait_ge(nd_ps, b + 1)
            dve.wait_ge(tq_ok, b + 1)
            flat = lambda t: t[:].rearrange("p f l -> p (f l)")
            dve.reciprocal(flat(rden), bank(1)).then_inc(y_step, 1)
            dve.scalar_tensor_tensor(out=flat(y1), in0=flat(tq), scalar=1.0, in1=bank(0), op0=ALU.add,
                                     op1=ALU.mult).then_inc(y_step, 1)
            dve.wait_ge(y_step, 2 * b + 2)
            dve.scalar_tensor_tensor(out=flat(yT), in0=flat(y1), scalar=0.5, in1=flat(rden), op0=ALU.mult,
                                     op1=ALU.mult).then_inc(y_ok, 1)

        def mixer_norm(b):
            dve.wait_ge(h_ps, b + 1)
            for t in range(LT):
                dve.bn_stats(st[:, t, :], ps[:, 2, t * D:(t + 1) * D]).then_inc(ln1, 1)
            dve.wait_ge(ln1, b * 5 + 2)
            dve.memset(tick[:], 0.0)
            for t in range(LT):
                dve.bn_aggr(mv[:, t, :], st[:, t, :]).then_inc(ln1, 1)
            dve.wait_ge(ln1, b * 5 + 4)
            dve.tensor_scalar(rs[:], mv[:, :, 1], EPS, None, ALU.add).then_inc(ln1, 1)
            dve.wait_ge(p1, b + 1)
            for t in range(LT):
                dve.tensor_scalar(hn[:, t, :], ps[:, 2, t * D:(t + 1) * D], mv[:, t, 0:1], rs[:, t:t + 1],
                                  ALU.subtract, ALU.mult).then_inc(hn_ok, 1)

        def attn_norm(b):
            dve.wait_ge(h_st, b + 1)
            for t in range(LT):
                dve.bn_stats(st2[:, t, :], hg[:, t, :]).then_inc(ln2, 1)
            dve.wait_ge(ln2, b * 5 + 2)
            dve.memset(tick[:], 0.0)
            for t in range(LT):
                dve.bn_aggr(mv2[:, t, :], st2[:, t, :]).then_inc(ln2, 1)
            dve.wait_ge(ln2, b * 5 + 4)
            dve.tensor_scalar(rs2[:], mv2[:, :, 1], EPS, None, ALU.add).then_inc(ln2, 1)
            dve.wait_ge(p2, b + 1)
            for t in range(LT):
                last = dve.tensor_scalar(z[:, t, :], hg[:, t, :], mv2[:, t, 0:1], rs2[:, t:t + 1], ALU.subtract,
                                         ALU.mult)
            last.then_inc(z_ok, 1)

        def rest(b, nxt):
            for n, (hi, lo) in enumerate(((qhi, qlo), (khi, klo))):
                dve.wait_ge(hi_ok, 2 * b + n + 1)
                dve.tensor_tensor(lo[:, :, 0:N], ps[:, 3 + 2 * n:5 + 2 * n, 0:N], hi[:, :, 0:N],
                                  ALU.subtract).then_inc(lo_ok, 1)
            if nxt:
                mixer_ekv(b + 1)
            for n in range(2):
                dve.wait_ge(rep_ps, 4 * b + n + 3)
                dve.tensor_copy(km[SLOT2:P, 4 * n:4 * n + 4, 1, :], ps[SLOT2:P, 3:7, 0:NP]).then_inc(repd_ok, 1)
            dve.wait_ge(mx_ps, b * MXN + 1)
            dve.tensor_reduce(negc[:], ps[0:NH, 7, 0:N], AX_X, ALU.max, negate=True).then_inc(negc_ok, 1)
            dve.wait_ge(negc_ok, b + 1)
            dve.tensor_copy(negr[0:NH, CLS:N], negc[:]).then_inc(mx_ok, 1)
            n = 0
            for t in range(LT):
                for h in range(0, NH, 2):
                    dve.wait_ge(mx_ps, b * MXN + n + 2)
                    k = 3 + 2 * (n % 2)
                    dve.tensor_reduce(mx[:, t, h:h + 2], ps[:, k:k + 2, 0:N], AX_X, ALU.max,
                                      negate=True).then_inc(mx_ok, 1)
                    n += 1
            if nxt:
                mixer_y(b + 1)
                mixer_norm(b + 1)
                attn_norm(b + 1)
            dve.wait_ge(ot_ps, b + 1)
            o = ps[:, 3:3 + LT, :].rearrange("p t (h s) -> p (t h) s", s=SLOT)
            dve.reciprocal(rc[:], o[:, :, HD]).then_inc(rc_ok, 1)
            dve.wait_ge(rc_ok, b + 1)
            dve.tensor_tensor(on[:].rearrange("p t (h d) -> p (t h) d", d=HD), o[:, :, 0:HD],
                              rc[:].rearrange("p (x o) -> p x o", o=1).broadcast_to([P, LT * NH, HD]),
                              ALU.mult).then_inc(on_ok, 1)
            dve.tensor_copy(clso[:, :, bass.ds(b, 1)], og[:, :, CLS:N]).then_inc(clso_ok, 1)
            dve.wait_ge(o_ps, b + 1)
            dve.wait_ge(hres_ok, b + 1)
            dve.wait_ge(h2_out, 16 * b + 16)
            flat = lambda t: t[:].rearrange("p t d -> p (t d)")
            dve.tensor_tensor(flat(h2), bank(7), flat(hres), ALU.add).then_inc(h2_ok, 1)
            dve.wait_ge(h2_ok, b + 1)
            for t in range(LT):
                dve.bn_stats(st3[:, t, :], h2[:, t, :]).then_inc(ln3, 1)
            dve.wait_ge(ln3, b * 5 + 2)
            dve.memset(tick[:], 0.0)
            for t in range(LT):
                dve.bn_aggr(mvb[:, t, :], st3[:, t, :]).then_inc(ln3, 1)
            dve.wait_ge(ln3, b * 5 + 4)
            dve.tensor_copy(mv3[:, bass.ds(b * LT, LT), :].rearrange("p t m -> p (t m)"),
                            mvb[:].rearrange("p t m -> p (t m)")).then_inc(ln3, 1)

        dve.memset(h2[:], 0.0)
        dve.memset(mh65[:], -0.5)
        dve.memset(zeros[:], 0.0)
        dve.memset(mhalf[:], -0.5).then_inc(half_ok, 1)
        dve.memset(clso[:], 0.0).then_inc(clso_ok, 1)
        dve.memset(xs[C:P, :], 0.0).then_inc(x_rows, 1)
        dve.wait_ge(x_rows, 1)
        dve.memset(xs[C:C + 1, :], 1.0)
        dve.memset(Wz[:], 0.0)
        dve.memset(one1[:], 1.0)
        for t in (qhi, qlo, khi, klo, q2, km, negr):
            dve.memset(t[:].bitcast(F32), 0.0)
        dve.memset(mv3[:, B * LT:, :], 0.0)
        dve.memset(vbd[:], 0.0)
        dve.memset(va[:], 0.0).then_inc(d_step, 1)
        dve.wait_ge(d_step, 1)
        dve.memset(va[:, :, :, HD:HD + 1], 1.0).then_inc(c_set, 1)
        dve.wait_ge(c_load, LOADED)
        steps = [1]

        def chain(ins):
            steps[0] += 1
            ins.then_inc(d_step, 1)
            dve.wait_ge(d_step, steps[0])

        dve.tensor_copy(mskf[:], mskT[:]).then_inc(mask_ok, 1)
        chain(dve.tensor_scalar(tn[:], phs[:], 1.0 / (2 * np.pi), ROUND, ALU.mult, ALU.add))
        chain(dve.tensor_scalar(tr[:], tn[:], ROUND, None, ALU.subtract))
        chain(dve.scalar_tensor_tensor(out=tn[:], in0=tr[:], scalar=-TWO_PI_1, in1=phs[:], op0=ALU.mult, op1=ALU.add))
        chain(dve.scalar_tensor_tensor(out=W[:], in0=tr[:], scalar=-TWO_PI_2, in1=tn[:], op0=ALU.mult, op1=ALU.add))
        chain(dve.scalar_tensor_tensor(out=tn[:], in0=tr[:], scalar=-TWO_PI_3, in1=W[:], op0=ALU.mult, op1=ALU.add))
        chain(dve.scalar_tensor_tensor(out=W[:], in0=tn[:], scalar=-1.0, in1=tn[:], op0=ALU.mult, op1=ALU.max))
        dve.tensor_scalar(tn[:], W[:], -1.0, float(np.pi / 2), ALU.mult, ALU.add).then_inc(arg_ok, 1)
        chain(dve.bn_stats(clsst[:], clsr[:]))
        chain(dve.bn_aggr(clsmv[:], clsst[:]))
        dve.tensor_scalar(clsrs[:], clsmv[:, 1:2], EPS, None, ALU.add).then_inc(clsvar_ok, 1)
        dve.wait_ge(clsrs_ok, 1)
        dve.tensor_scalar(clsz[:], clsr[:], clsmv[:, 0:1], clsrs[:], ALU.subtract, ALU.mult).then_inc(clsz_ok, 1)
        dve.wait_ge(cos_ok, 1)
        chain(dve.tensor_tensor(W[:], tr[:], amp[:], ALU.mult))
        for n in range(3):
            last = dve.tensor_copy(Wz[n * HARM:(n + 1) * HARM, n, :], W[n * HARM:(n + 1) * HARM, :])
        last.then_inc(w_ok, 1)
        dve.tensor_copy(sel[:], selw[:])
        dve.tensor_copy(eyer[:], eye[:])
        dve.tensor_copy(mones[:], eye[:, 0:NH].rearrange("p (h o) -> p h o", o=1).broadcast_to([P, NH, P]))
        dve.wait_ge(clsr_ok, 1)
        dve.tensor_copy(rbc[:], rT[:, CLS:N].broadcast_to([3 * HARM, NH])).then_inc(clsr_ok, 1)
        dve.wait_ge(clsqkv_ps, 1)
        for n in range(2):
            for f in range(FT):
                last = dve.tensor_scalar(bdf[:, n, f, :], bdm[:, f, :], ps[:, 4, n * FT + f:n * FT + f + 1], None, ALU.mult)
        chain(last)
        chain(dve.tensor_copy(bdh[:], bdf[:]))
        dve.tensor_tensor(bdl[:].rearrange("p a f h -> p (a f h)"), bdf[:].rearrange("p a f h -> p (a f h)"),
                          bdh[:].rearrange("p a f h -> p (a f h)"), ALU.subtract)
        dve.tensor_copy(vbd[:, :, HD], eye[0:NH, 0:NH])
        dve.tensor_tensor(vbd[:, :, 0:HD], ps[0:NH, 3, 0:D].rearrange("p (h d) -> p h d", d=HD),
                          vbdm[:].rearrange("p (h d) -> p h d", d=HD), ALU.mult).then_inc(spread_ok, 1)
        mixer_ekv(0)
        mixer_y(0)
        mixer_norm(0)
        attn_norm(0)
        with dve.Fori(0, B - 1) as b:
            rest(b, True)
        rest(B - 1, False)
        dve.wait_ge(ot_ps, B + 1)
        o = ps[0:B, 3, :].rearrange("p (h s) -> p h s", s=SLOT)
        dve.reciprocal(rc[0:B, 0:NH], o[:, :, HD]).then_inc(rc_ok, 1)
        dve.wait_ge(rc_ok, B + 1)
        dve.tensor_tensor(on[0:B, 0, :].rearrange("p (h d) -> p h d", d=HD), o[:, :, 0:HD],
                          rc[0:B, 0:NH].rearrange("p (x o) -> p x o", o=1).broadcast_to([B, NH, HD]),
                          ALU.mult).then_inc(on_ok, 1)
        dve.wait_ge(o_ps, B + 1)
        dve.wait_ge(h2_out, 16 * B + 16)
        dve.memset(h2[:], 0.0).then_inc(d_step, 1)
        dve.wait_ge(d_step, steps[0] + 1)
        dve.tensor_tensor(h2[0:B, 0, :], ps[0:B, 7, 0:D], cls32[0:B, :], ALU.add).then_inc(h2_ok, 1)
        dve.wait_ge(h2_ok, B + 1)
        dve.bn_stats(st3[:, 0, :], h2[:, 0, :]).then_inc(ln3, 1)
        dve.wait_ge(ln3, 5 * B + 1)
        dve.bn_aggr(mv3[:, B * LT, :], st3[:, 0, :]).then_inc(ln3, 1)
        dve.wait_ge(ln3, 5 * B + 2)
        dve.tensor_scalar(rs3[:], mv3[:, :, 1], EPS, None, ALU.add).then_inc(ln3, 1)

    @block.gpsimd
    def _(pool):
        flat = lambda t: t[:].rearrange("p t d -> p (t d)")

        def mixer_affine(b):
            pool.wait_ge(ln1, b * 5 + 5)
            pool.tensor_tensor(rs[:], rs[:], mhalf[:], ALU.pow).then_inc(p1, 1)
            pool.wait_ge(hn_ok, b * 2 + 2)
            pool.tensor_tensor(flat(hn), flat(hn), lng[:], ALU.mult).then_inc(hg_ok, 1)
            pool.wait_ge(hg_ok, b + 1)
            pool.tensor_tensor(flat(hg), flat(hn), lnb[:], ALU.add).then_inc(h_st, 1)
            pool.wait_ge(ln2, b * 5 + 5)
            pool.tensor_tensor(rs2[:], rs2[:], mhalf[:], ALU.pow).then_inc(p2, 1)

        def keep_residual(b):
            pool.wait_ge(h_st, b + 1)
            if not isinstance(b, int) or b > 0:
                pool.wait_ge(h2_ok, b)
            pool.tensor_tensor(flat(hres), flat(hg), zeros[:], ALU.add).then_inc(hres_ok, 1)

        pool.wait_ge(mask_ok, 1)
        pool.wait_ge(c_load, LOADED)
        pool.tensor_tensor(wbT[:], wbT[:], mskf[:], ALU.mult).then_inc(wb_ok, 1)
        pool.wait_ge(half_ok, 1)
        pool.wait_ge(clsvar_ok, 1)
        pool.tensor_tensor(clsrs[:], clsrs[:], mhalf[0:1, 0:1], ALU.pow).then_inc(clsrs_ok, 1)
        mixer_affine(0)
        keep_residual(0)
        with pool.Fori(0, B - 1) as b:
            mixer_affine(b + 1)
            keep_residual(b + 1)
        pool.wait_ge(ln3, 5 * B + 3)
        pool.tensor_tensor(rs3[:], rs3[:], mh65[:], ALU.pow)


def stage_b(nc, ctx, sem, a, out, hscr, mv3, rs3, eye, ps):
    def sb(name, shape, dt=F32):
        return ctx.enter_context(nc.sbuf_tensor(name, shape, dt))

    UW = FT * 2 * UH + 2 * D
    whi = sb("whi", [P, NU, UW], F32R)
    wlo = sb("wlo", [P, NU, UW], F32R)
    rwr = sb("rwr", [P, FT * NE])
    rwh = sb("rwh", [P, FT, NE], F32R)
    rwl = sb("rwl", [P, FT, NE], F32R)
    ebias = sb("ebias", [P, LT * NE])
    before = sb("before", [P, LT * NE, NE])
    hb = sb("hb", [P, LT, D])
    z3 = sb("z3", [P, LT, D])
    zhi = sb("zhi", [P, FT, L], F32R)
    zlo = sb("zlo", [P, FT, L], F32R)
    sil = sb("sil", [P, 2, 2 * L])
    uu = sb("uu", [P, 3, 2 * L])
    hhi = sb("hhi", [P, 3, 2 * L], F32R)
    hlo = sb("hlo", [P, 3, 2 * L], F32R)
    acc = sb("acc", [P, LT, D])
    th = sb("th", [P, LT * NE])
    sc = sb("sc", [P, LT * NE])
    key = sb("key", [P, LT * NE])
    gt = sb("gt", [P, LT * NE, NE])
    eq = sb("eq", [P, LT * NE, NE])
    rank = sb("rank", [P, LT * NE])
    gate = sb("gate", [P, LT * NE])

    w_hi, w_lo, b_load, r_hi, r_lo = (sem(x) for x in ("w_hi", "w_lo", "b_load", "r_hi", "r_lo"))
    w_in = [sem("w_in0"), sem("w_in1")]
    hb_in, z3_ok, zt3_ps, zhi_ok, zlo_ok, hid_ps, sil_ok, uu_ok, hhi_ok, hlo_ok, out_ps, acc_ok, lg_ps, th_ok, gt_step, out_d = (
        sem(x) for x in ("hb_in", "z3_ok", "zt3_ps", "zhi_ok", "zlo_ok", "hid_ps", "sil_ok", "uu_ok", "hhi_ok", "hlo_ok",
                         "out_ps", "acc_ok", "lg_ps", "th_ok", "gt_step", "out_d"))
    gate_ok = sem("gate_ok")
    K = B + 1
    AN = 1 + NE
    GS = 6

    RAW = 2
    raw = [uu[:].rearrange("p a b -> p (a b)"), None]
    raw2 = sb("raw2", [P, UW])
    raw[1] = raw2[:]
    assert UW == 3 * 2 * L

    block = ctx.enter_context(nc.Block())

    @block.sync
    def _(sp):
        sp.dma_start(rwr[:], a["routerT"]).then_inc(b_load, 16)
        sp.dma_start(ebias[:], a["ebias"]).then_inc(b_load, 16)
        sp.dma_start(before[:], a["before"]).then_inc(b_load, 16)
        sp.dma_start(hb[:], hscr[0]).then_inc(hb_in, 16)
        for u in range(NU):
            if u >= RAW:
                sp.wait_ge(w_lo, u - RAW + 1)
            sp.dma_start(raw[u % RAW], a["wu"][u]).then_inc(w_in[u % RAW], 16)
        with sp.Fori(0, K - 1) as k:
            sp.wait_ge(acc_ok, k * AN + 1)
            sp.dma_start(hb[:], hscr[bass.ds(k + 1, 1)].rearrange("n p t d -> p (n t) d")).then_inc(hb_in, 16)
            sp.wait_ge(acc_ok, k * AN + AN)
            sp.dma_start(out[bass.ds(k, 1), 1:N, :].rearrange("n (t p) d -> p (n t) d", p=P), acc[:]).then_inc(out_d, 16)
        sp.wait_ge(acc_ok, K * AN)
        sp.dma_start(out[:, 0, :], acc[0:B, 0, :]).then_inc(out_d, 16)
        sp.wait_ge(out_d, 16 * K)

    @block.tensor
    def _(pe):
        def turn(k):
            pe.wait_ge(z3_ok, k + 1)
            for f in range(FT):
                for t in range(LT):
                    last = pe.transpose(ps[:, 6, f * L + t * P:f * L + (t + 1) * P], z3[:, t, f * P:(f + 1) * P], eye[:])
            last.then_inc(zt3_ps, 1)

        def router(k, nt):
            if not isinstance(k, int) or k > 0:
                pe.wait_ge(th_ok, k)
            for t in range(nt):
                mm = [(z_, w_, f) for z_, w_ in ((zhi, rwh), (zlo, rwh), (zhi, rwl)) for f in range(FT)]
                for n, (z_, w_, f) in enumerate(mm):
                    last = pe.matmul(ps[:, 7, t * NE:(t + 1) * NE], z_[:, f, t * P:(t + 1) * P], w_[:, f, :],
                                     start=(n == 0), stop=(n == len(mm) - 1))
            last.then_inc(lg_ps, 1)

        def hidden(k, u, w):
            if u == 0:
                pe.wait_ge(zhi_ok, k + 1)
                pe.wait_ge(zlo_ok, k + 1)
            if u >= 2 or not isinstance(k, int) or k > 0:
                pe.wait_ge(uu_ok, k * NU + u - 1)
            for c in range(2):
                for m in range(2):
                    mm = [(w_, z_, f) for w_, z_ in ((whi, zhi), (wlo, zhi), (whi, zlo)) for f in range(FT)]
                    for n, (w_, z_, f) in enumerate(mm):
                        at = f * 2 * UH + m * UH + c * P
                        last = pe.matmul(ps[:, 2 * (u % 2) + c, m * L:m * L + w], w_[:, u, at:at + P], z_[:, f, 0:w],
                                         start=(n == 0), stop=(n == len(mm) - 1))
            last.then_inc(hid_ps, 1)

        def output(k, u, nt):
            pe.wait_ge(hhi_ok, k * NU + u + 1)
            pe.wait_ge(hlo_ok, k * NU + u + 1)
            e = u - NS
            if u == 0 and (not isinstance(k, int) or k > 0):
                pe.wait_ge(acc_ok, k * AN)
            if e >= 1:
                pe.wait_ge(acc_ok, k * AN + e)
            n_bank = 4 if e < 0 else 4 + (e + 1) % 2
            for t in range(nt):
                mm = [(h_, w_, c) for h_, w_ in ((hhi, whi), (hlo, whi), (hhi, wlo)) for c in range(2)]
                for n, (h_, w_, c) in enumerate(mm):
                    at = FT * 2 * UH + c * D
                    start = (n == 0) if e >= 0 else (n == 0 and u == 0 and t == 0)
                    stop = n == len(mm) - 1 and (e >= 0 or u == NS - 1)
                    last = pe.matmul(ps[:, n_bank, t * D:(t + 1) * D], h_[:, u % 3, c * L + t * P:c * L + (t + 1) * P],
                                     w_[:, u, at:at + D], start=start, stop=stop, skip_group_check=True)
            last.then_inc(out_ps, 1)

        def blk(k, nt, nxt):
            for u in range(NU):
                hidden(k, u, nt * P)
                if u == 1:
                    router(k, nt)
                if u >= 2:
                    output(k, u - 2, nt)
                if u == 9 and nxt:
                    turn(k + 1)
            output(k, NU - 2, nt)
            output(k, NU - 1, nt)

        pe.wait_ge(w_lo, NU)
        pe.wait_ge(w_hi, NU)
        pe.wait_ge(r_lo, 1)
        pe.wait_ge(r_hi, 1)
        turn(0)
        blk(0, LT, True)
        with pe.Fori(1, K - 1) as k:
            blk(k, LT, True)
        blk(K - 1, 1, False)

    @block.scalar
    def _(act):
        def silu(k, u, w):
            act.wait_ge(hid_ps, k * NU + u + 1)
            if u >= 2 or not isinstance(k, int) or k > 0:
                act.wait_ge(uu_ok, k * NU + u - 1)
            act.activation(sil[:, u % 2, :].rearrange("p (c l) -> p c l", c=2)[:, :, 0:w],
                           ps[:, 2 * (u % 2):2 * (u % 2) + 2, 0:w], ACT.Silu).then_inc(sil_ok, 1)

        def head(k, u, w):
            act.wait_ge(uu_ok, k * NU + u + 1)
            if u >= 3 or not isinstance(k, int) or k > 0:
                act.wait_ge(out_ps, k * NU + u - 2)
            v = lambda t: t[:, u % 3, :].rearrange("p (c l) -> p c l", c=2)[:, :, 0:w]
            act.activation(v(hhi), v(uu), ACT.Copy).then_inc(hhi_ok, 1)

        def z_high(k):
            act.wait_ge(zt3_ps, k + 1)
            if not isinstance(k, int) or k > 0:
                act.wait_ge(hid_ps, k * NU)
            act.activation(zhi[:].rearrange("p f l -> p (f l)"), ps[:, 6, :], ACT.Copy).then_inc(zhi_ok, 1)

        def blk(k, nt, nxt):
            w = nt * P
            for u in range(NU):
                silu(k, u, w)
                if u == 2:
                    act.wait_ge(lg_ps, k + 1)
                    act.activation(th[:, 0:nt * NE], ps[:, 7, 0:nt * NE], ACT.Tanh, scale=0.5).then_inc(th_ok, 1)
                if u >= 1:
                    head(k, u - 1, w)
            if nxt:
                z_high(k + 1)
            head(k, NU - 1, w)

        act.wait_ge(b_load, 48)
        act.activation(rwh[:].rearrange("p f e -> p (f e)"), rwr[:], ACT.Copy).then_inc(r_hi, 1)
        for u in range(NU):
            act.wait_ge(w_in[u % RAW], 16 * (u // RAW) + 16)
            act.activation(whi[:, u, :], raw[u % RAW], ACT.Copy).then_inc(w_hi, 1)
        z_high(0)
        blk(0, LT, True)
        with act.Fori(1, K - 1) as k:
            blk(k, LT, True)
        blk(K - 1, 1, False)

    @block.vector
    def _(dve):
        def norm(k):
            dve.wait_ge(hb_in, k * 16 + 16)
            for t in range(LT):
                c = k * LT + t
                mean = mv3[:, bass.ds(c, 1), 0:1].rearrange("p t m -> p (t m)")
                root = rs3[:, bass.ds(c, 1)]
                last = dve.tensor_scalar(z3[:, t, :], hb[:, t, :], mean, root, ALU.subtract, ALU.mult)
            last.then_inc(z3_ok, 1)

        def z_low(k):
            dve.wait_ge(zhi_ok, k + 1)
            dve.tensor_tensor(zlo[:].rearrange("p f l -> p (f l)"), ps[:, 6, :],
                              zhi[:].rearrange("p f l -> p (f l)"), ALU.subtract).then_inc(zlo_ok, 1)

        def gates(k, nt):
            n = nt * NE
            dve.wait_ge(th_ok, k + 1)
            dve.tensor_scalar(sc[:, 0:n], th[:, 0:n], 0.5, 0.5, ALU.mult, ALU.add).then_inc(gt_step, 1)
            dve.wait_ge(gt_step, k * GS + 1)
            dve.tensor_tensor(key[:, 0:n], sc[:, 0:n], ebias[:, 0:n], ALU.add).then_inc(gt_step, 1)
            dve.wait_ge(gt_step, k * GS + 2)
            for t in range(nt):
                row = key[:, t * NE:(t + 1) * NE]
                other = row.rearrange("p (o e) -> p o e", o=1).broadcast_to([P, NE, NE])
                own = row.rearrange("p (e o) -> p e o", o=1).broadcast_to([P, NE, NE])
                dve.tensor_tensor(gt[:, t * NE:(t + 1) * NE, :], other, own, ALU.is_gt)
                last = dve.tensor_tensor(eq[:, t * NE:(t + 1) * NE, :], other, own, ALU.is_equal)
            last.then_inc(gt_step, 1)
            dve.wait_ge(gt_step, k * GS + 3)
            f = lambda t: t[:, 0:n, :].rearrange("p a b -> p (a b)")
            dve.tensor_tensor(f(eq), f(eq), f(before), ALU.mult).then_inc(gt_step, 1)
            dve.wait_ge(gt_step, k * GS + 4)
            dve.tensor_tensor(f(gt), f(gt), f(eq), ALU.add).then_inc(gt_step, 1)
            dve.wait_ge(gt_step, k * GS + 5)
            dve.tensor_reduce(rank[:, 0:n], gt[:, 0:n, :], AX_X, ALU.add).then_inc(gt_step, 1)
            dve.wait_ge(gt_step, k * GS + 6)
            dve.scalar_tensor_tensor(out=gate[:, 0:n], in0=rank[:, 0:n], scalar=1.5, in1=sc[:, 0:n], op0=ALU.is_lt,
                                     op1=ALU.mult).then_inc(gate_ok, 1)

        def product(k, u, w):
            dve.wait_ge(sil_ok, k * NU + u + 1)
            if u >= 3 or not isinstance(k, int) or k > 0:
                dve.wait_ge(hlo_ok, k * NU + u - 2)
            v = lambda t, s: t[:, s, :].rearrange("p (c l) -> p c l", c=2)[:, :, 0:w]
            dve.tensor_tensor(v(uu, u % 3), ps[:, 2 * (u % 2):2 * (u % 2) + 2, L:L + w], v(sil, u % 2),
                              ALU.mult).then_inc(uu_ok, 1)

        def gather(k, u, nt):
            e = u - NS
            if e < 0 and u < NS - 1:
                return
            dve.wait_ge(out_ps, k * NU + u + 1)
            fl = lambda t: t[:, 0:nt, :].rearrange("p t d -> p (t d)")
            if e < 0:
                if not isinstance(k, int) or k > 0:
                    dve.wait_ge(out_d, 16 * k)
                dve.tensor_tensor(fl(acc), ps[:, 4, 0:nt * D], fl(hb), ALU.add).then_inc(acc_ok, 1)
                return
            if e == 0:
                dve.wait_ge(gate_ok, k + 1)
            dve.wait_ge(acc_ok, k * AN + e + 1)
            for t in range(nt):
                last = dve.scalar_tensor_tensor(out=acc[:, t, :], in0=ps[:, 4 + (e + 1) % 2, t * D:(t + 1) * D],
                                                scalar=gate[:, t * NE + e:t * NE + e + 1], in1=acc[:, t, :],
                                                op0=ALU.mult, op1=ALU.add)
            last.then_inc(acc_ok, 1)

        def blk(k, nt, nxt):
            for u in range(NU):
                product(k, u, nt * P)
                if u == 3:
                    gates(k, nt)
                if u >= 3:
                    gather(k, u - 3, nt)
                if u == 8 and nxt:
                    norm(k + 1)
            if nxt:
                z_low(k + 1)
            for u in range(NU - 3, NU):
                gather(k, u, nt)

        dve.wait_ge(r_hi, 1)
        dve.tensor_tensor(rwl[:].rearrange("p f e -> p (f e)"), rwr[:], rwh[:].rearrange("p f e -> p (f e)"),
                          ALU.subtract).then_inc(r_lo, 1)
        norm(0)
        for u in range(NU):
            dve.wait_ge(w_hi, u + 1)
            dve.tensor_tensor(wlo[:, u, :], raw[u % RAW], whi[:, u, :], ALU.subtract).then_inc(w_lo, 1)
        z_low(0)
        blk(0, LT, True)
        with dve.Fori(1, K - 1) as k:
            blk(k, LT, True)
        blk(K - 1, 1, False)

    @block.gpsimd
    def _(pool):
        def tail(k, u, w):
            pool.wait_ge(hhi_ok, k * NU + u + 1)
            v = lambda t: t[:, u % 3, :].rearrange("p (c l) -> p c l", c=2)[:, :, 0:w]
            pool.tensor_tensor(v(hlo), v(uu), v(hhi), ALU.subtract).then_inc(hlo_ok, 1)

        with pool.Fori(0, K - 1) as k:
            for u in range(NU):
                tail(k, u, L)
        for u in range(NU):
            tail(K - 1, u, P)


def layout(i):
    f = lambda x: np.ascontiguousarray(x)
    z = lambda *s: np.zeros(s, np.float32)
    t = {k[3:]: np.asarray(v) for k, v in i.items() if k.startswith("L0_")}
    o = {"x": f(i["x"])}
    tiles = lambda m: f(m.reshape(-1, P, m.shape[1]).transpose(1, 0, 2))
    wkv = z(P, 2 * C)
    wkv[:C, :C], wkv[:C, C:] = t["tok_Wk_w"].T, t["tok_Wv_w"].T
    wkv[C, :C], wkv[C, C:] = t["tok_Wk_b"], t["tok_Wv_b"]
    o["wkv"] = wkv
    o["wq"] = f(np.concatenate([t["tok_Wq_w"].T, t["tok_Wq_b"][None], z(P - C - 1, C)]))
    o["idn"] = f(np.concatenate([np.tile(np.eye(C, dtype=np.float32), (1, H)), t["tok_out_b"][None], z(P - C - 1, D)]))
    o["wbT"] = tiles(t["tok_w_bias"].T)
    o["mskT"] = tiles(t["tok_local_mask"].T)
    o["outw"] = tiles(t["tok_out_w"])
    o["lng"] = f(np.tile(t["tok_ln_g"][None], (P, LT)))
    o["lnb"] = f(np.tile(t["tok_ln_b"][None], (P, LT)))
    o["basT"] = tiles(np.concatenate([t["attn_basis_" + n].T for n in "qkv"], axis=1))
    o["basoT"] = tiles(t["attn_basis_o"].T)
    for name, src in (("phs", "phase"), ("amp", "amp")):
        o[name] = f(np.concatenate([t[f"attn_{src}_{n}"].T for n in "qkvo"]))
    heads = np.arange(NH)
    sel = z(P, 4, 4, P)
    for kind, places in enumerate(((0, 1), (2,), (0, 2), (1,))):
        for g in range(4):
            for j in range(2):
                for place in places:
                    to = SLOT2 * j + HD * place
                    sel[(2 * g + j) * HD:(2 * g + j + 1) * HD, kind, g, to:to + HD] = np.eye(HD)
    o["sel"] = sel
    col = np.arange(P)
    o["bdm"] = f((col[None, None] == HPF * np.arange(FT)[None, :, None] + col[:, None, None] // HD).astype(np.float32))
    o["vbdm"] = f((np.arange(D)[None] // HD == heads[:, None]).astype(np.float32))
    o["eye"] = np.eye(P, dtype=np.float32)
    cls = np.asarray(i["cls_tok"]).reshape(1, D)
    o["clsr"] = f(cls)
    o["cls32"] = f(np.tile(cls, (P, 1)))
    sw = [np.asarray(t["ffn_shared_w%d" % n]) for n in (1, 2, 3)]
    wu = z(NU, P, FT * 2 * UH + 2 * D)
    for u in range(NU):
        if u < NS:
            r = slice(u * UH, (u + 1) * UH)
            w_in, w_out = np.concatenate([sw[0][r], sw[1][r]]), sw[2][:, r]
        else:
            w_in, w_out = t["ffn_w12"][u - NS], t["ffn_w3"][u - NS]
        wu[u, :, :FT * 2 * UH] = tiles(w_in.T).reshape(P, -1)
        wu[u, :, FT * 2 * UH:] = tiles(w_out.T).reshape(P, -1)
    o["wu"] = wu
    o["routerT"] = tiles(t["ffn_router_w"].T).reshape(P, -1)
    o["ebias"] = f(np.tile(t["ffn_expert_bias"][None], (P, LT)))
    e = np.arange(NE)
    o["before"] = f(np.tile((e[None] < e[:, None]).astype(np.float32)[None], (P, LT, 1)))
    return o


def kernel(**inputs):
    import numpy as _np
    import concourse.bacc as _bacc
    from concourse import mybir as _mybir
    from concourse.bass_utils import run_bass_kernel_spmd as _run

    nc = _bacc.Bacc("TRN2", target_bir_lowering=False, num_devices=1)
    arrays = {"in_" + k: v for k, v in layout({k: _np.asarray(v) for k, v in inputs.items()}).items()}
    aps = {k[3:]: nc.dram_tensor(k, v.shape, _mybir.dt.from_np(v.dtype), kind="ExternalInput").ap()
           for k, v in arrays.items()}
    out = nc.dram_tensor("out", (B, N, D), F32, kind="ExternalOutput").ap()
    build(nc, aps, out)
    r = _run(nc, [arrays], core_ids=[0])
    return r.results[0]["out"]
```

```python
from contextlib import ExitStack

import numpy as np

import concourse.bass as bass
from concourse import mybir

F32 = mybir.dt.float32
F32R = mybir.dt.float32r
U8 = mybir.dt.uint8
ALU = mybir.AluOpType
ACT = mybir.ActivationFunctionType
AX_X = mybir.AxisListType.X

B, C, L, H = 32, 64, 256, 4
D = C * H
P = 128
LT = L // P
FT = D // P
NH, HD, HARM = 16, 16, 32
SLOT = 32
G = NH * SLOT // P
HPG = NH // G
HPF = P // HD
SLOT2 = 64
STACKED = 3 * HD
G2 = NH * SLOT2 // P
NP = L + 2
N = L + 1
CLS = L
NE = 8
UH = 256
NS = 1024 // UH
NU = NS + NE
EPS = 1e-5
TWO_PI_1 = 6.28125
TWO_PI_2 = float(np.float32(0.0019350051879882812))
TWO_PI_3 = float(2 * np.pi - TWO_PI_1 - TWO_PI_2)
ROUND = 12582912.0


def build(nc, a, out):
    with ExitStack() as whole:
        def sem(name):
            return whole.enter_context(nc.semaphore(name))

        hscr = nc.dram_tensor("hscr", [B + 1, P, LT, D], F32, kind="Internal").ap()
        mv3 = whole.enter_context(nc.sbuf_tensor("mv3", [P, (B + 1) * LT, 2], F32))
        rs3 = whole.enter_context(nc.sbuf_tensor("rs3", [P, (B + 1) * LT], F32))
        eye = whole.enter_context(nc.sbuf_tensor("eye", [P, P], F32))
        mhalf = whole.enter_context(nc.sbuf_tensor("mhalf", [P, 2], F32))
        ps = whole.enter_context(nc.psum_tensor("ps", [P, 8, 512], F32))
        with ExitStack() as ctx:
            stage_a(nc, ctx, sem, a, hscr, mv3, rs3, eye, mhalf, ps)
        with ExitStack() as ctx:
            stage_b(nc, ctx, sem, a, out, hscr, mv3, rs3, eye, ps)


def stage_a(nc, ctx, sem, a, hscr, mv3, rs3, eye, mhalf, ps):
    def sb(name, shape, dt=F32):
        return ctx.enter_context(nc.sbuf_tensor(name, shape, dt))

    pT = sb("pT", [P, NH, LT, N])

    spare = pT[:].rearrange("p h t l -> p (h t l)")
    at = [0]

    def temp(*shape):
        at[0] += int(np.prod(shape))
        assert at[0] <= NH * LT * N
        names = "abc"[:len(shape)]
        return spare[:, at[0] - int(np.prod(shape)):at[0]].rearrange(
            "p (%s) -> p %s" % (" ".join(names), " ".join(names)), **dict(zip(names, shape)))

    wbT, mskf = temp(LT, L), temp(LT, L)
    phs, amp, tr, tn = temp(D), temp(D), temp(D), temp(D)
    selw = temp(4, 4, P)
    bdf = temp(2, FT, P)

    xs = sb("xs", [P, L * H])
    wkv = sb("wkv", [P, 2 * C])
    wq = sb("wq", [P, C])
    idn = sb("idn", [P, D])
    mskT = sb("mskT", [P, LT, L], U8)
    ewT = sb("ewT", [P, LT, L])
    outw = sb("outw", [P, FT, D])
    lng = sb("lng", [P, LT * D])
    lnb = sb("lnb", [P, LT * D])
    basT = sb("basT", [P, FT, 3 * HARM])
    basoT = sb("basoT", [P, FT, HARM])
    W = sb("W", [P, D])
    Wz = sb("Wz", [3 * HARM, 3, D])
    sel = sb("sel", [P, 4, 4, P], F32R)
    bdm = sb("bdm", [P, FT, P])
    eyer = sb("eyer", [P, P], F32R)
    vbdm = sb("vbdm", [NH, D])
    clsr = sb("clsr", [1, D])
    cls32 = sb("cls32", [P, D])
    clsst = sb("clsst", [1, 6])
    clsmv = sb("clsmv", [1, 2])
    clsrs = sb("clsrs", [1, 1])
    clsz = sb("clsz", [1, D])
    one1 = sb("one1", [1, 1])
    tick = sb("tick", [P, 1])
    mvb = sb("mvb", [P, LT, 2])
    mh65 = sb("mh65", [P, (B + 1) * LT])
    hres = [sb("hres%d" % p, [P, LT, D]) for p in range(4)]
    h2 = sb("h2", [P, LT, D])
    rbc = sb("rbc", [3 * HARM, NH])
    ek = sb("ek", [P, LT, D])
    ekv = sb("ekv", [P, LT, D])
    tq = sb("tq", [P, FT, L])
    rden = sb("rden", [P, FT, L])
    y1 = sb("y1", [P, FT, L])
    yT = sb("yT", [P, FT, L])
    hn = sb("hn", [P, LT, D])
    z = sb("z", [P, LT, D])
    st = sb("st", [P, LT, 6])
    mv = sb("mv", [P, LT, 2])
    rs = sb("rs", [P, LT])
    st2 = sb("st2", [P, LT, 6])
    mv2 = sb("mv2", [P, LT, 2])
    rs2 = sb("rs2", [P, LT])
    st3 = sb("st3", [P, LT, 6])
    zT = sb("zT", [P, FT, N])
    rT = sb("rT", [3 * HARM, N])
    qhi = [sb("qhi%d" % p, [P, FT, NP], F32R) for p in range(2)]
    qlo = [sb("qlo%d" % p, [P, FT, NP], F32R) for p in range(2)]
    khi = [sb("khi%d" % p, [P, FT, NP], F32R) for p in range(2)]
    klo = [sb("klo%d" % p, [P, FT, NP], F32R) for p in range(2)]
    q2 = [sb("q2_%d" % p, [P, G2, NP], F32R) for p in range(2)]
    km = [sb("km_%d" % p, [P, G2, 2, NP], F32R) for p in range(2)]
    bdh = sb("bdh", [P, 2, FT, P], F32R)
    bdl = sb("bdl", [P, 2, FT, P], F32R)
    negr = [sb("negr%d" % p, [P, NP], F32R) for p in range(2)]
    negc_ok, x_rows = sem("negc_ok"), sem("x_rows")
    negc = sb("negc", [NH, 1])
    vbd = sb("vbd", [NH, NH, SLOT])
    va = [sb("va%d" % p, [P, LT, NH, SLOT]) for p in range(2)]
    mx = sb("mx", [P, LT, NH])
    pc = [sb("pc%d" % p, [NH, N]) for p in range(2)]
    pcr = [sb("pcr%d" % p, [NH, N]) for p in range(2)]
    og = sb("og", [P, G, N])
    rc = sb("rc", [P, LT * NH])
    on = sb("on", [P, LT, D])
    onT = sb("onT", [P, FT, L])
    ro = sb("ro", [P, L])
    clso = sb("clso", [P, G, B])

    (c_load, c_set, d_step, half_ok, mask_ok, wb_ok, ew_ok, arg_ok, cos_ok, w_ok, clsvar_ok, clsrs_ok, clsz_ok, clsT_ps,
     clsT_ok, clsr_ps, clsr_ok, clsqkv_ps, spread_ok) = (
        sem(x) for x in ("c_load", "c_set", "d_step", "half_ok", "mask_ok", "wb_ok", "ew_ok", "arg_ok", "cos_ok", "w_ok",
                         "clsvar_ok", "clsrs_ok", "clsz_ok", "clsT_ps", "clsT_ok", "clsr_ps", "clsr_ok", "clsqkv_ps",
                         "spread_ok"))
    x_in, h2_out = sem("x_in"), sem("h2_out")
    q_ps, kv_ps, ek_ok, tq_ok, ekv_ok, sum_ps = (sem(x) for x in ("q_ps", "kv_ps", "ek_ok", "tq_ok", "ekv_ok", "sum_ps"))
    y_step, y_ok, h_ps, ln1, hn_ok, h_st, ln2, z_ok, zt_ps, zt_ok = (
        sem(x) for x in ("y_step", "y_ok", "h_ps", "ln1", "hn_ok", "h_st", "ln2", "z_ok", "zt_ps", "zt_ok"))
    p1, p2, hg_ok = sem("p1"), sem("p2"), sem("hg_ok")
    r_ps, r_ok, qk_ps, v_ps, v_ok, hi_ok, lo_ok, rep_ps, rep_ok, repd_ok = (
        sem(x) for x in ("r_ps", "r_ok", "qk_ps", "v_ps", "v_ok", "hi_ok", "lo_ok", "rep_ps", "rep_ok", "repd_ok"))
    negm_in = sem("negm_in")
    mx_ps, mx_ok, mt_ps, negm_ok = (sem(x) for x in ("mx_ps", "mx_ok", "mt_ps", "negm_ok"))
    pcr_ok, pc_ok = sem("pcr_ok"), sem("pc_ok")
    s_ps, s_ok, pv_ps, og_ok, ot_ps, rc_ok, on_ok, onT_ps, onT_ok, ro_ps, ro_ok, o_ps, h2_ok, ln3, clso_ok = (
        sem(x) for x in ("s_ps", "s_ok", "pv_ps", "og_ok", "ot_ps", "rc_ok", "on_ok", "onT_ps", "onT_ok",
                         "ro_ps", "ro_ok", "o_ps", "h2_ok", "ln3", "clso_ok"))

    loads = [(wkv, a["wkv"]), (wq, a["wq"]), (idn, a["idn"]), (wbT, a["wbT"]), (mskT, a["mskT"]),
             (outw, a["outw"]), (lng, a["lng"]), (lnb, a["lnb"]), (basT, a["basT"]), (basoT, a["basoT"]),
             (phs, a["phs"]), (amp, a["amp"]), (selw, a["sel"]), (bdm, a["bdm"]),
             (vbdm, a["vbdm"]), (eye, a["eye"]), (clsr, a["clsr"]), (cls32, a["cls32"])]
    LOADED = 16 * len(loads)

    def bank(n, w=512):
        return ps[:, n, 0:w]

    def xcol(t, h):
        return xs[:, h:L * H:H] if t is None else xs[:, t * P * H + h:(t + 1) * P * H:H]

    def later(i):
        return not isinstance(i, int) or i > 0

    SN = LT * NH
    MXN = SN + 2
    RN = 2 * G2
    LAG = 4
    U = 4
    VALUES_AT = (9, 12, 14)
    MX_AT = [3, 3, 3, 2, 3, 3, 3, 2, 2, 2, 2, 2, 2, 0, 0, 0]
    mx_upto = [sum(MX_AT[:n]) for n in range(NH + 1)]
    assert mx_upto[NH] == SN

    def has(i):
        return not isinstance(i, int) or 0 <= i < B

    def steps_of(eng, step):
        for b in range(-3, 1):
            step(b, b % U)
        with eng.Fori(0, (B - U) // U) as i:
            for p in range(1, U + 1):
                step(U * i + p, p % U)
        for b in range(B - 3, B + 1):
            step(b, b % U)

    block = ctx.enter_context(nc.Block())

    @block.sync
    def _(sp):
        for dst, src in loads:
            sp.dma_start(dst[:], src).then_inc(c_load, 16)
        sp.wait_ge(half_ok, 1)
        sp.dma_start(hscr[B], h2[:]).then_inc(h2_out, 16)

        def step(b, p):
            if has(b + 3):
                if later(b + 3):
                    sp.wait_ge(h_ps, b + 3)
                sp.dma_start(xs[0:C, :], a["x"][bass.ds(b + 3, 1)].rearrange("n c l h -> (n c) (l h)")).then_inc(x_in, 16)
            if has(b - 1):
                sp.wait_ge(h2_ok, b)
                sp.dma_start(hscr[bass.ds(b - 1, 1)].rearrange("n p t d -> p (n t) d"), h2[:]).then_inc(h2_out, 16)
            if has(b + 1):
                sp.wait_ge(negm_ok, b + 2)
                for k in range(2):
                    row = SLOT2 * k + STACKED
                    sp.dma_start(q2[(p + 1) % 2][row:row + 1, :, :].bitcast(F32),
                                 negr[(p + 1) % 2][k:NH:2, :].bitcast(F32)).then_inc(negm_in, 16)

        steps_of(sp, step)
        sp.wait_ge(h2_ok, B + 1)
        sp.dma_start(hscr[B], h2[:]).then_inc(h2_out, 16)
        sp.wait_ge(h2_out, 16 * (B + 2))

    @block.tensor
    def _(pe):
        def mixer_q(j):
            pe.wait_ge(x_in, j * 16 + 16)
            if later(j):
                pe.wait_ge(lo_ok, 2 * j)
            for f in range(FT):
                for hh in range(2):
                    last = pe.matmul(ps[hh * C:(hh + 1) * C, 2, f * L:(f + 1) * L], wq[:], xcol(None, 2 * f + hh),
                                     start=True, stop=True)
            last.then_inc(q_ps, 1)

        def mixer_kv(j, t):
            if t == 1:
                pe.wait_ge(tq_ok, j + 1)
            for h in range(H):
                last = pe.matmul(ps[:, 3 - t, h * 2 * C:(h + 1) * 2 * C], xcol(t, h), wkv[:], start=True, stop=True)
            last.then_inc(kv_ps, 1)

        def mixer_sum(j, n):
            pe.wait_ge(ek_ok, 2 * j + 2)
            pe.wait_ge(ekv_ok, 2 * j + 1 + n)
            for f in range(FT):
                for s in range(LT):
                    last = pe.matmul(ps[:, 3 - n, f * L:(f + 1) * L], (ek, ekv)[n][:, s, f * P:(f + 1) * P],
                                     ewT[:, s, :], start=(s == 0), stop=(s == LT - 1))
            last.then_inc(sum_ps, 1)

        def mixer_out(j, t):
            if t == 0:
                pe.wait_ge(y_ok, j + 1)
            o = ps[:, 3, t * D:(t + 1) * D]
            for f in range(FT):
                pe.matmul(o, yT[:, f, t * P:(t + 1) * P], outw[:, f, :], start=(f == 0), stop=False)
            for h in range(H):
                last = pe.matmul(o[:, h * C:(h + 1) * C], xcol(t, h), idn[:, h * C:(h + 1) * C],
                                 start=False, stop=(h == H - 1))
            if t == LT - 1:
                last.then_inc(h_ps, 1)

        def turn(j):
            pe.wait_ge(z_ok, j + 1)
            for f in range(FT):
                for t in range(LT):
                    last = pe.transpose(ps[:, 2, f * L + t * P:f * L + (t + 1) * P], z[:, t, f * P:(f + 1) * P], eye[:])
            last.then_inc(zt_ps, 1)

        def resonances(j):
            pe.wait_ge(zt_ok, j + 1)
            for f in range(FT):
                last = pe.matmul(ps[0:3 * HARM, 3, 0:N], basT[:, f, :], zT[:, f, :], start=(f == 0), stop=(f == FT - 1))
            last.then_inc(r_ps, 1)

        def heads_qk(j, n):
            if n == 0:
                pe.wait_ge(r_ok, j + 1)
                if later(j):
                    pe.wait_ge(v_ok, j)
            else:
                pe.wait_ge(lo_ok, 2 * j + 1)
            for f in range(FT):
                last = pe.matmul(ps[:, 2 + f, 0:N], Wz[:, n, f * P:(f + 1) * P], rT[:], start=True, stop=True)
            last.then_inc(qk_ps, 1)

        def heads_v(m):
            for t in range(LT):
                last = pe.matmul(ps[:, 2, t * D:(t + 1) * D], rT[:, t * P:(t + 1) * P], Wz[:, 2, :], start=True, stop=True)
            last.then_inc(v_ps, 1)

        def stack(j, p, r):
            g, kind = r // 2, r % 2
            pe.wait_ge(lo_ok, 2 * j + 1 + (r > 0))
            if r > 0 or later(j):
                pe.wait_ge(rep_ok, RN * j + r)
            if r > 1 or later(j):
                pe.wait_ge(repd_ok, G2 * j + g)
            hi, lo = ((qhi, qlo), (khi, klo))[kind]
            f = g // (G2 // FT)
            pe.matmul(ps[:, 6, 0:NP], sel[:, 2 * kind, g % 4, :], hi[p % 2][:, f, :], start=True, stop=False)
            pe.matmul(ps[:, 6, 0:NP], sel[:, 2 * kind + 1, g % 4, :], lo[p % 2][:, f, :], start=False,
                      stop=True).then_inc(rep_ps, 1)

        def cls_tiles(m, p):
            if later(m):
                pe.wait_ge(negm_ok, m)
            for n, (hi, lo) in enumerate(((khi, klo), (qhi, qlo))):
                mm = [(x, y, f) for x, y in ((bdh, hi), (bdh, lo), (bdl, hi)) for f in range(FT)]
                for i, (x, y, f) in enumerate(mm):
                    last = pe.matmul(ps[:, n, 0:NP], x[:, n, f, :], y[p % 2][:, f, :], start=(i == 0),
                                     stop=(i == len(mm) - 1))
                last.then_inc(mx_ps, 1)

        def maxima(m, p, n):
            t, h = n // NH, n % NH
            if n == 0:
                pe.wait_ge(rep_ok, RN * m + RN - LAG)
                pe.wait_ge(repd_ok, G2 * m + G2 - LAG // 2)
            if n == NH - LAG:
                pe.wait_ge(rep_ok, RN * m + RN)
                pe.wait_ge(repd_ok, G2 * m + G2)
            pe.wait_ge(mx_ok, m * MXN + n + 1)
            pe.matmul(ps[:, n % 2, 0:NP], q2[p % 2][:, h // 2, t * P:(t + 1) * P], km[p % 2][:, h // 2, h % 2, :],
                      start=True, stop=True).then_inc(mx_ps, 1)

        def turn_maxima(m):
            pe.wait_ge(mx_ok, m * MXN + MXN)
            for t in range(LT):
                last = pe.transpose(ps[0:NH, 0, t * P:(t + 1) * P], mx[:, t, :], eye[:])
            last.then_inc(mt_ps, 1)

        def scores(b, p, n):
            h, t = n // LT, n % LT
            if n == 0:
                pe.wait_ge(negm_in, 32 * b + 32)
            if n >= 2 or later(b):
                pe.wait_ge(s_ok, b * SN + n - 1)
            o = ps[:, 4 + n % 2, 0:NP]
            pe.matmul(o, km[p % 2][:, h // 2, h % 2, t * P:(t + 1) * P], q2[p % 2][:, h // 2, :], start=True,
                      stop=True).then_inc(s_ps, 1)

        def values(b, p, g):
            pe.wait_ge(s_ok, b * SN + LT * HPG * (g + 1))
            if g == 0:
                if later(b):
                    pe.wait_ge(h2_ok, b)
                pe.wait_ge(pc_ok, b + 1)
                pe.wait_ge(v_ok, b + 1)
            else:
                pe.wait_ge(og_ok, b * G + g)
            pe.matmul(ps[:, 7, 0:N], vbd[:, g * HPG:(g + 1) * HPG, :].rearrange("p h s -> p (h s)"), pc[p % 2][:], start=True,
                      stop=False, skip_group_check=True)
            for j in range(HPG):
                h = g * HPG + j
                for t in range(LT):
                    last = pe.matmul(ps[SLOT * j:SLOT * (j + 1), 7, 0:N], va[p % 2][:, t, h, :], pT[:, h, t, :],
                                     start=False, stop=(t == LT - 1), skip_group_check=True)
            last.then_inc(pv_ps, 1)

        def turn_values(b, t):
            if t == 0:
                pe.wait_ge(og_ok, b * G + G)
            else:
                pe.wait_ge(on_ok, b * LT + t)
            for g in range(G):
                last = pe.transpose(ps[:, 7, g * P:(g + 1) * P], og[:, g, t * P:(t + 1) * P], eye[:])
            last.then_inc(ot_ps, 1)

        def turn_back(b):
            pe.wait_ge(on_ok, b * LT + LT)
            for f in range(FT):
                for t in range(LT):
                    last = pe.transpose(ps[:, 7, f * L + t * P:f * L + (t + 1) * P], on[:, t, f * P:(f + 1) * P], eye[:])
            last.then_inc(onT_ps, 1)

        def out_resonances(b):
            pe.wait_ge(onT_ok, b + 1)
            for f in range(FT):
                last = pe.matmul(ps[96:P, 7, 0:L], basoT[:, f, :], onT[:, f, :], start=(f == 0), stop=(f == FT - 1))
            last.then_inc(ro_ps, 1)

        def attend_out(b):
            pe.wait_ge(ro_ok, b + 1)
            for t in range(LT):
                last = pe.matmul(ps[:, 7, t * D:(t + 1) * D], ro[96:P, t * P:(t + 1) * P], W[96:P, :], start=True,
                                 stop=True)
            last.then_inc(o_ps, 1)

        pe.wait_ge(c_load, LOADED)
        pe.wait_ge(c_set, 1)
        pe.wait_ge(clsz_ok, 1)
        for f in range(FT):
            last = pe.matmul(ps[:, 6, f:f + 1], clsz[:, f * P:(f + 1) * P], one1[:], start=True, stop=True)
        last.then_inc(clsT_ps, 1)
        pe.wait_ge(clsT_ok, 1)
        for f in range(FT):
            last = pe.matmul(ps[0:3 * HARM, 5, 16:17], basT[:, f, :], zT[:, f, CLS:N], start=(f == 0), stop=(f == FT - 1))
        last.then_inc(clsr_ps, 1)
        pe.wait_ge(clsr_ok, 2)
        pe.wait_ge(w_ok, 1)
        for n in range(2):
            for f in range(FT):
                pe.matmul(ps[:, 4, n * FT + f:n * FT + f + 1], Wz[:, n, f * P:(f + 1) * P], rT[:, CLS:N], start=True,
                          stop=True)
        pe.matmul(ps[0:NH, 3, 0:D], rbc[:], Wz[:, 2, :], start=True,
                  stop=True).then_inc(clsqkv_ps, 1)

        def step(b, p):
            for n in range(NH):
                todo = list(range(mx_upto[n], mx_upto[n + 1])) if has(b + 1) else []
                if todo:
                    maxima(b + 1, p + 1, todo[0])
                if has(b):
                    scores(b, p, 2 * n)
                if len(todo) > 1:
                    maxima(b + 1, p + 1, todo[1])
                if has(b):
                    scores(b, p, 2 * n + 1)
                if n == 1 and has(b + 2):
                    turn(b + 2)
                if n == 2 and has(b + 2):
                    heads_qk(b + 2, 0)
                if n < LAG and has(b + 1):
                    stack(b + 1, p + 1, RN - LAG + n)
                if n > LAG and has(b + 2):
                    stack(b + 2, p + 2, n - LAG)
                if len(todo) > 2:
                    maxima(b + 1, p + 1, todo[2])
                if has(b - 1):
                    if n == 0:
                        values(b - 1, p - 1, G - 1)
                    if n in (1, 2):
                        turn_values(b - 1, n - 1)
                    if n == 3:
                        turn_back(b - 1)
                    if n == 4:
                        out_resonances(b - 1)
                    if n == 5:
                        attend_out(b - 1)
                if has(b) and n in VALUES_AT:
                    values(b, p, VALUES_AT.index(n))
                if has(b + 1):
                    if n == 1:
                        if has(b + 2):
                            pe.wait_ge(zt_ok, b + 3)
                        heads_v(b + 1)
                    if n == 13:
                        turn_maxima(b + 1)
                if has(b + 2):
                    if n == 1:
                        resonances(b + 2)
                    if n == 3:
                        heads_qk(b + 2, 1)
                    if n == LAG:
                        stack(b + 2, p + 2, 0)
                    if n == 15:
                        cls_tiles(b + 2, p + 2)
                if has(b + 3):
                    if n == 4:
                        mixer_q(b + 3)
                    if n in (5, 6):
                        mixer_kv(b + 3, n - 5)
                    if n in (7, 8):
                        mixer_sum(b + 3, n - 7)
                    if n in (10, 11):
                        mixer_out(b + 3, n - 10)

        pe.wait_ge(ew_ok, 1)
        pe.wait_ge(spread_ok, 1)
        steps_of(pe, step)
        pe.wait_ge(clso_ok, B + 1)
        for g in range(G):
            last = pe.transpose(ps[0:B, 3, g * P:(g + 1) * P], clso[:, g, :], eye[:])
        last.then_inc(ot_ps, 1)
        pe.wait_ge(on_ok, LT * B + 1)
        for f in range(FT):
            last = pe.transpose(ps[:, 5, f * B:(f + 1) * B], on[0:B, 0, f * P:(f + 1) * P], eye[0:B, 0:B])
        last.then_inc(onT_ps, 1)
        pe.wait_ge(onT_ok, B + 1)
        for f in range(FT):
            last = pe.matmul(ps[96:P, 6, 0:B], basoT[:, f, :], onT[:, f, 0:B], start=(f == 0), stop=(f == FT - 1))
        last.then_inc(ro_ps, 1)
        pe.wait_ge(ro_ok, B + 1)
        pe.wait_ge(h2_ok, B)
        pe.matmul(ps[0:B, 7, 0:D], ro[96:P, 0:B], W[96:P, :], start=True, stop=True).then_inc(o_ps, 1)

    @block.scalar
    def _(act):
        def mixer_gate(j):
            act.wait_ge(q_ps, j + 1)
            act.activation(tq[:].rearrange("p f l -> p (f l)"), bank(2), ACT.Tanh, scale=0.5).then_inc(tq_ok, 1)

        def mixer_exp(j, t):
            act.wait_ge(kv_ps, 2 * j + t + 1)
            kv = bank(3 - t).rearrange("p (h w) -> p h w", h=H)
            act.activation(ek[:, t, :].rearrange("p (h w) -> p h w", h=H), kv[:, :, 0:C], ACT.Exp).then_inc(ek_ok, 1)

        def turned(j):
            act.wait_ge(zt_ps, j + 1)
            act.activation(zT[:, :, 0:L], bank(2).rearrange("p (f l) -> p f l", f=FT), ACT.Copy).then_inc(zt_ok, 1)

        def high(j, p, n):
            act.wait_ge(qk_ps, 2 * j + n + 1)
            act.activation((qhi, khi)[n][p % 2][:, :, 0:N], ps[:, 2:4, 0:N], ACT.Copy).then_inc(hi_ok, 1)

        def take_stack(j, p, r):
            act.wait_ge(rep_ps, RN * j + r + 1)
            if r % 2 == 0:
                act.activation(q2[p % 2][:, r // 2, :], ps[:, 6, 0:NP], ACT.Copy).then_inc(rep_ok, 1)
            else:
                act.activation(km[p % 2][0:STACKED, r // 2, 0, :], ps[0:STACKED, 6, 0:NP], ACT.Copy).then_inc(rep_ok, 1)

        def exps(b, n):
            act.wait_ge(s_ps, b * SN + n + 1)
            act.activation(pT[:, n // LT, n % LT, :], ps[:, 4 + n % 2, 0:N], ACT.Exp, scale=HD ** -0.5).then_inc(s_ok, 1)

        def take_group(b, g):
            act.wait_ge(pv_ps, b * G + g + 1)
            if g == 0:
                act.wait_ge(clso_ok, b + 1)
            act.activation(og[:, g, :], ps[:, 7, 0:N], ACT.Copy).then_inc(og_ok, 1)

        def step(b, p):
            for n in range(NH):
                if has(b):
                    exps(b, 2 * n)
                    exps(b, 2 * n + 1)
                if n == 1 and has(b + 2):
                    turned(b + 2)
                if n == 2 and has(b + 2):
                    high(b + 2, p + 2, 0)
                if n < LAG and has(b + 1):
                    take_stack(b + 1, p + 1, RN - LAG + n)
                if n > LAG and has(b + 2):
                    take_stack(b + 2, p + 2, n - LAG)
                if has(b - 1):
                    if n == 0:
                        take_group(b - 1, G - 1)
                    if n == 3:
                        act.wait_ge(onT_ps, b)
                        act.activation(onT[:].rearrange("p f l -> p (f l)"), bank(7), ACT.Copy).then_inc(onT_ok, 1)
                    if n == 4:
                        act.wait_ge(ro_ps, b)
                        act.activation(ro[96:P, :], ps[96:P, 7, 0:L], ACT.Copy).then_inc(ro_ok, 1)
                if has(b) and n in VALUES_AT:
                    take_group(b, VALUES_AT.index(n))
                if has(b + 1):
                    if n == 1:
                        act.wait_ge(v_ps, b + 2)
                        act.activation(va[(p + 1) % 2][:, :, :, 0:HD],
                                       bank(2).rearrange("p (t h d) -> p t h d", t=LT, h=NH), ACT.Copy).then_inc(v_ok, 1)
                    if n == 13:
                        act.wait_ge(mt_ps, b + 2)
                        act.activation(negr[(p + 1) % 2][0:NH, 0:L], ps[0:NH, 0, 0:L], ACT.Copy).then_inc(negm_ok, 1)
                    if n == 15:
                        act.wait_ge(pcr_ok, b + 2)
                        act.activation(pc[(p + 1) % 2][:], pcr[(p + 1) % 2][:], ACT.Exp, scale=HD ** -0.5).then_inc(pc_ok, 1)
                if has(b + 2):
                    if n == 1:
                        act.wait_ge(r_ps, b + 3)
                        act.activation(rT[:], ps[0:3 * HARM, 3, 0:N], ACT.Copy).then_inc(r_ok, 1)
                    if n == 3:
                        high(b + 2, p + 2, 1)
                    if n == LAG:
                        take_stack(b + 2, p + 2, 0)
                if has(b + 3):
                    if n == 4:
                        mixer_gate(b + 3)
                    if n in (5, 6):
                        mixer_exp(b + 3, n - 5)

        act.wait_ge(arg_ok, 1)
        act.activation(tr[:], tn[:], ACT.Sin).then_inc(cos_ok, 1)
        act.wait_ge(wb_ok, 1)
        act.activation(ewT[:], wbT[:], ACT.Exp).then_inc(ew_ok, 1)
        act.wait_ge(clsT_ps, 1)
        act.activation(zT[:, :, CLS:N], ps[:, 6, 0:FT].rearrange("p (f o) -> p f o", o=1), ACT.Copy).then_inc(clsT_ok, 1)
        act.wait_ge(clsr_ps, 1)
        act.activation(rT[:, CLS:N], ps[0:3 * HARM, 5, 16:17], ACT.Copy).then_inc(clsr_ok, 1)
        steps_of(act, step)
        act.wait_ge(onT_ps, B + 1)
        act.activation(onT[:, :, 0:B], ps[:, 5, 0:FT * B].rearrange("p (f b) -> p f b", f=FT), ACT.Copy).then_inc(onT_ok, 1)
        act.wait_ge(ro_ps, B + 1)
        act.activation(ro[96:P, 0:B], ps[96:P, 6, 0:B], ACT.Copy).then_inc(ro_ok, 1)

    @block.vector
    def _(dve):
        def mixer_ekv(j, t):
            dve.wait_ge(ek_ok, 2 * j + t + 1)
            kv = bank(3 - t).rearrange("p (h w) -> p h w", h=H)
            dve.tensor_tensor(ekv[:, t, :].rearrange("p (h w) -> p h w", h=H), kv[:, :, C:2 * C],
                              ek[:, t, :].rearrange("p (h w) -> p h w", h=H), ALU.mult).then_inc(ekv_ok, 1)

        def mixer_inverse(j, f):
            if f == 0:
                dve.wait_ge(sum_ps, 2 * j + 1)
            dve.reciprocal(rden[:, f, :], ps[:, 3, f * L:(f + 1) * L]).then_inc(y_step, 1)

        def mixer_y(j):
            dve.wait_ge(sum_ps, 2 * j + 2)
            dve.wait_ge(tq_ok, j + 1)
            flat = lambda t: t[:].rearrange("p f l -> p (f l)")
            dve.scalar_tensor_tensor(out=flat(y1), in0=flat(tq), scalar=1.0, in1=bank(2), op0=ALU.add,
                                     op1=ALU.mult).then_inc(y_step, 1)
            dve.wait_ge(y_step, 3 * j + 3)
            dve.scalar_tensor_tensor(out=flat(yT), in0=flat(y1), scalar=0.5, in1=flat(rden), op0=ALU.mult,
                                     op1=ALU.mult).then_inc(y_ok, 1)

        def mixer_stats(b):
            dve.wait_ge(h_ps, b + 1)
            for t in range(LT):
                dve.bn_stats(st[:, t, :], ps[:, 3, t * D:(t + 1) * D]).then_inc(ln1, 1)
            dve.wait_ge(ln1, b * 5 + 2)
            dve.memset(tick[:], 0.0)
            for t in range(LT):
                dve.bn_aggr(mv[:, t, :], st[:, t, :]).then_inc(ln1, 1)
            dve.wait_ge(ln1, b * 5 + 4)
            dve.tensor_scalar(rs[:], mv[:, :, 1], EPS, None, ALU.add).then_inc(ln1, 1)

        def mixer_norm(b):
            dve.wait_ge(p1, b + 1)
            for t in range(LT):
                dve.tensor_scalar(hn[:, t, :], ps[:, 3, t * D:(t + 1) * D], mv[:, t, 0:1], rs[:, t:t + 1],
                                  ALU.subtract, ALU.mult).then_inc(hn_ok, 1)

        def attn_stats(b, p):
            dve.wait_ge(h_st, b + 1)
            for t in range(LT):
                dve.bn_stats(st2[:, t, :], hres[p % U][:, t, :]).then_inc(ln2, 1)
            dve.wait_ge(ln2, b * 5 + 2)
            dve.memset(tick[:], 0.0)
            for t in range(LT):
                dve.bn_aggr(mv2[:, t, :], st2[:, t, :]).then_inc(ln2, 1)
            dve.wait_ge(ln2, b * 5 + 4)
            dve.tensor_scalar(rs2[:], mv2[:, :, 1], EPS, None, ALU.add).then_inc(ln2, 1)

        def attn_norm(b, p):
            dve.wait_ge(p2, b + 1)
            for t in range(LT):
                last = dve.tensor_scalar(z[:, t, :], hres[p % U][:, t, :], mv2[:, t, 0:1], rs2[:, t:t + 1], ALU.subtract,
                                         ALU.mult)
            last.then_inc(z_ok, 1)

        def low(j, p, n):
            dve.wait_ge(hi_ok, 2 * j + n + 1)
            hi, lo = ((qhi, qlo), (khi, klo))[n]
            dve.tensor_tensor(lo[p % 2][:, :, 0:N], ps[:, 2:4, 0:N], hi[p % 2][:, :, 0:N], ALU.subtract).then_inc(lo_ok, 1)

        def take_stack(j, p, r):
            dve.wait_ge(rep_ps, RN * j + r + 1)
            dve.tensor_copy(km[p % 2][SLOT2:SLOT2 + STACKED, r // 2, 1, :], ps[SLOT2:SLOT2 + STACKED, 6, 0:NP]).then_inc(repd_ok, 1)

        def cls_tiles(m, p):
            dve.wait_ge(mx_ps, m * MXN + 1)
            dve.tensor_reduce(negc[:], ps[0:NH, 0, 0:N], AX_X, ALU.max, negate=True).then_inc(negc_ok, 1)
            dve.wait_ge(negc_ok, m + 1)
            dve.tensor_copy(negr[p % 2][0:NH, CLS:N], negc[:]).then_inc(mx_ok, 1)
            dve.wait_ge(mx_ps, m * MXN + 2)
            if later(m - 1):
                dve.wait_ge(pc_ok, m - 1)
            dve.tensor_copy(pcr[p % 2][:], ps[0:NH, 1, 0:N]).then_inc(mx_ok, 1)

        def maxima(m, n):
            dve.wait_ge(mx_ps, m * MXN + n + 3)
            t, h = n // NH, n % NH
            dve.tensor_reduce(mx[:, t, h:h + 1], ps[:, n % 2, 0:N], AX_X, ALU.max, negate=True).then_inc(mx_ok, 1)

        def cls_shift(m, p):
            dve.wait_ge(negm_ok, m + 1)
            dve.tensor_tensor(pcr[p % 2][:], pcr[p % 2][:], negr[p % 2][0:NH, 0:N], ALU.add).then_inc(pcr_ok, 1)

        def normalise(b, t):
            dve.wait_ge(ot_ps, b * LT + t + 1)
            o = ps[:, 7, :].rearrange("p (h s) -> p h s", s=SLOT)
            dve.reciprocal(rc[:, t * NH:(t + 1) * NH], o[:, :, HD]).then_inc(rc_ok, 1)
            dve.wait_ge(rc_ok, b * LT + t + 1)
            dve.tensor_tensor(on[:, t, :].rearrange("p (h d) -> p h d", d=HD), o[:, :, 0:HD],
                              rc[:, t * NH:(t + 1) * NH].rearrange("p (x o) -> p x o", o=1).broadcast_to([P, NH, HD]),
                              ALU.mult).then_inc(on_ok, 1)
            if t == LT - 1:
                dve.tensor_copy(clso[:, :, bass.ds(b, 1)], og[:, :, CLS:N]).then_inc(clso_ok, 1)

        def residual(b, p):
            dve.wait_ge(o_ps, b + 1)
            dve.wait_ge(h2_out, 16 * b + 16)
            flat = lambda t: t[:].rearrange("p t d -> p (t d)")
            dve.tensor_tensor(flat(h2), bank(7), flat(hres[p % U]), ALU.add).then_inc(h2_ok, 1)

        def ffn_stats(b):
            dve.wait_ge(h2_ok, b + 1)
            for t in range(LT):
                dve.bn_stats(st3[:, t, :], h2[:, t, :]).then_inc(ln3, 1)
            dve.wait_ge(ln3, b * 5 + 2)
            dve.memset(tick[:], 0.0)
            for t in range(LT):
                dve.bn_aggr(mvb[:, t, :], st3[:, t, :]).then_inc(ln3, 1)
            dve.wait_ge(ln3, b * 5 + 4)
            dve.tensor_copy(mv3[:, bass.ds(b * LT, LT), :].rearrange("p t m -> p (t m)"),
                            mvb[:].rearrange("p t m -> p (t m)")).then_inc(ln3, 1)

        def step(b, p):
            for n in range(NH):
                if has(b + 1):
                    for i in range(mx_upto[n], mx_upto[n + 1]):
                        maxima(b + 1, i)
                if has(b + 2) and n == 4:
                    low(b + 2, p + 2, 1)
                if n == 0 and has(b + 2):
                    attn_norm(b + 2, p + 2)
                if n < LAG and n % 2 == 1 and has(b + 1):
                    take_stack(b + 1, p + 1, RN - LAG + n)
                if n > LAG and n % 2 == 1 and has(b + 2):
                    take_stack(b + 2, p + 2, n - LAG)
                if has(b - 1):
                    if n in (1, 2):
                        normalise(b - 1, n - 1)
                    if n == 5:
                        residual(b - 1, p - 1)
                    if n == 6:
                        ffn_stats(b - 1)
                if has(b + 1) and n == 14:
                    cls_shift(b + 1, p + 1)
                if has(b + 2) and n == 2:
                    low(b + 2, p + 2, 0)
                if has(b + 2) and n == 15:
                    cls_tiles(b + 2, p + 2)
                if has(b + 3):
                    if n in (5, 6):
                        mixer_ekv(b + 3, n - 5)
                    if n in (7, 8):
                        mixer_inverse(b + 3, n - 7)
                    if n == 9:
                        mixer_y(b + 3)
                    if n == 11:
                        mixer_stats(b + 3)
                    if n == 12:
                        mixer_norm(b + 3)
                    if n == 14:
                        attn_stats(b + 3, p + 3)

        dve.memset(h2[:], 0.0)
        dve.memset(mh65[:], -0.5)
        dve.memset(mhalf[:], -0.5).then_inc(half_ok, 1)
        dve.memset(clso[:], 0.0).then_inc(clso_ok, 1)
        dve.memset(xs[C:P, :], 0.0).then_inc(x_rows, 1)
        dve.wait_ge(x_rows, 1)
        dve.memset(xs[C:C + 1, :], 1.0)
        dve.memset(Wz[:], 0.0)
        dve.memset(one1[:], 1.0)
        for t in (*qhi, *qlo, *khi, *klo, *q2, *km, *negr):
            dve.memset(t[:].bitcast(F32), 0.0)
        dve.memset(mv3[:, B * LT:, :], 0.0)
        dve.memset(vbd[:], 0.0)
        dve.memset(va[0][:], 0.0)
        dve.memset(va[1][:], 0.0).then_inc(d_step, 1)
        dve.wait_ge(d_step, 1)
        for t in km:
            for k in range(2):
                dve.memset(t[SLOT2 * k + 32:SLOT2 * (k + 1), :, k, :].bitcast(F32), 1.0)
        dve.memset(va[0][:, :, :, HD:HD + 1], 1.0)
        dve.memset(va[1][:, :, :, HD:HD + 1], 1.0).then_inc(c_set, 1)
        dve.wait_ge(c_load, LOADED)
        steps = [1]

        def chain(ins):
            steps[0] += 1
            ins.then_inc(d_step, 1)
            dve.wait_ge(d_step, steps[0])

        dve.tensor_copy(mskf[:], mskT[:]).then_inc(mask_ok, 1)
        chain(dve.tensor_scalar(tn[:], phs[:], 1.0 / (2 * np.pi), ROUND, ALU.mult, ALU.add))
        chain(dve.tensor_scalar(tr[:], tn[:], ROUND, None, ALU.subtract))
        chain(dve.scalar_tensor_tensor(out=tn[:], in0=tr[:], scalar=-TWO_PI_1, in1=phs[:], op0=ALU.mult, op1=ALU.add))
        chain(dve.scalar_tensor_tensor(out=W[:], in0=tr[:], scalar=-TWO_PI_2, in1=tn[:], op0=ALU.mult, op1=ALU.add))
        chain(dve.scalar_tensor_tensor(out=tn[:], in0=tr[:], scalar=-TWO_PI_3, in1=W[:], op0=ALU.mult, op1=ALU.add))
        chain(dve.scalar_tensor_tensor(out=W[:], in0=tn[:], scalar=-1.0, in1=tn[:], op0=ALU.mult, op1=ALU.max))
        dve.tensor_scalar(tn[:], W[:], -1.0, float(np.pi / 2), ALU.mult, ALU.add).then_inc(arg_ok, 1)
        chain(dve.bn_stats(clsst[:], clsr[:]))
        chain(dve.bn_aggr(clsmv[:], clsst[:]))
        dve.tensor_scalar(clsrs[:], clsmv[:, 1:2], EPS, None, ALU.add).then_inc(clsvar_ok, 1)
        dve.wait_ge(clsrs_ok, 1)
        dve.tensor_scalar(clsz[:], clsr[:], clsmv[:, 0:1], clsrs[:], ALU.subtract, ALU.mult).then_inc(clsz_ok, 1)
        dve.wait_ge(cos_ok, 1)
        chain(dve.tensor_tensor(W[:], tr[:], amp[:], ALU.mult))
        for n in range(3):
            last = dve.tensor_copy(Wz[n * HARM:(n + 1) * HARM, n, :], W[n * HARM:(n + 1) * HARM, :])
        last.then_inc(w_ok, 1)
        dve.tensor_copy(sel[:], selw[:])
        dve.tensor_copy(eyer[:], eye[:])
        dve.wait_ge(clsr_ok, 1)
        dve.tensor_copy(rbc[:], rT[:, CLS:N].broadcast_to([3 * HARM, NH])).then_inc(clsr_ok, 1)
        dve.wait_ge(clsqkv_ps, 1)
        for n in range(2):
            for f in range(FT):
                last = dve.tensor_scalar(bdf[:, n, f, :], bdm[:, f, :], ps[:, 4, n * FT + f:n * FT + f + 1], None, ALU.mult)
        chain(last)
        chain(dve.tensor_copy(bdh[:], bdf[:]))
        dve.tensor_tensor(bdl[:].rearrange("p a f h -> p (a f h)"), bdf[:].rearrange("p a f h -> p (a f h)"),
                          bdh[:].rearrange("p a f h -> p (a f h)"), ALU.subtract)
        dve.tensor_copy(vbd[:, :, HD], eye[0:NH, 0:NH])
        dve.tensor_tensor(vbd[:, :, 0:HD], ps[0:NH, 3, 0:D].rearrange("p (h d) -> p h d", d=HD),
                          vbdm[:].rearrange("p (h d) -> p h d", d=HD), ALU.mult).then_inc(spread_ok, 1)
        steps_of(dve, step)
        dve.wait_ge(ot_ps, LT * B + 1)
        o = ps[0:B, 3, :].rearrange("p (h s) -> p h s", s=SLOT)
        dve.reciprocal(rc[0:B, 0:NH], o[:, :, HD]).then_inc(rc_ok, 1)
        dve.wait_ge(rc_ok, LT * B + 1)
        dve.tensor_tensor(on[0:B, 0, :].rearrange("p (h d) -> p h d", d=HD), o[:, :, 0:HD],
                          rc[0:B, 0:NH].rearrange("p (x o) -> p x o", o=1).broadcast_to([B, NH, HD]),
                          ALU.mult).then_inc(on_ok, 1)
        dve.wait_ge(o_ps, B + 1)
        dve.wait_ge(h2_out, 16 * B + 16)
        dve.memset(h2[:], 0.0).then_inc(d_step, 1)
        dve.wait_ge(d_step, steps[0] + 1)
        dve.tensor_tensor(h2[0:B, 0, :], ps[0:B, 7, 0:D], cls32[0:B, :], ALU.add).then_inc(h2_ok, 1)
        dve.wait_ge(h2_ok, B + 1)
        dve.bn_stats(st3[:, 0, :], h2[:, 0, :]).then_inc(ln3, 1)
        dve.wait_ge(ln3, 5 * B + 1)
        dve.bn_aggr(mv3[:, B * LT, :], st3[:, 0, :]).then_inc(ln3, 1)
        dve.wait_ge(ln3, 5 * B + 2)
        dve.tensor_scalar(rs3[:], mv3[:, :, 1], EPS, None, ALU.add).then_inc(ln3, 1)

    @block.gpsimd
    def _(pool):
        flat = lambda t: t[:].rearrange("p t d -> p (t d)")

        def mixer_affine(b, p):
            pool.wait_ge(ln1, b * 5 + 5)
            pool.tensor_tensor(rs[:], rs[:], mhalf[:], ALU.pow).then_inc(p1, 1)
            pool.wait_ge(hn_ok, b * 2 + 2)
            pool.tensor_tensor(flat(hn), flat(hn), lng[:], ALU.mult).then_inc(hg_ok, 1)
            pool.wait_ge(hg_ok, b + 1)
            if not isinstance(b, int) or b >= U:
                pool.wait_ge(h2_ok, b - U + 1)
            pool.tensor_tensor(flat(hres[p % U]), flat(hn), lnb[:], ALU.add).then_inc(h_st, 1)
            pool.wait_ge(ln2, b * 5 + 5)
            pool.tensor_tensor(rs2[:], rs2[:], mhalf[:], ALU.pow).then_inc(p2, 1)

        pool.wait_ge(mask_ok, 1)
        pool.wait_ge(c_load, LOADED)
        pool.tensor_tensor(wbT[:], wbT[:], mskf[:], ALU.mult).then_inc(wb_ok, 1)
        pool.wait_ge(half_ok, 1)
        pool.wait_ge(clsvar_ok, 1)
        pool.tensor_tensor(clsrs[:], clsrs[:], mhalf[0:1, 0:1], ALU.pow).then_inc(clsrs_ok, 1)
        for b in range(U):
            mixer_affine(b, b)
        with pool.Fori(0, B // U - 1) as i:
            for p in range(U):
                mixer_affine(U * i + U + p, p)
        pool.wait_ge(ln3, 5 * B + 3)
        pool.tensor_tensor(rs3[:], rs3[:], mh65[:], ALU.pow)


def stage_b(nc, ctx, sem, a, out, hscr, mv3, rs3, eye, ps):
    def sb(name, shape, dt=F32):
        return ctx.enter_context(nc.sbuf_tensor(name, shape, dt))

    I32 = mybir.dt.int32
    K = B + 1
    TOP = 2
    REG = K * L + P
    NT = (TOP * K * L + NE * (P - 1)) // P + 1
    assert NT % 2 == 0
    UW = FT * 2 * UH + 2 * D
    ONE = LT * NE
    zs = nc.dram_tensor("zs", [NE * REG, D], F32, kind="Internal").ap()
    ys = nc.dram_tensor("ys", [NT * P, D], F32, kind="Internal").ap()

    whi = sb("whi", [P, NU, UW], F32R)
    wlo = sb("wlo", [P, NU, UW], F32R)
    rwr = sb("rwr", [P, FT * NE])
    rwh = sb("rwh", [P, FT, NE], F32R)
    rwl = sb("rwl", [P, FT, NE], F32R)
    ebias = sb("ebias", [P, ONE])
    before = sb("before", [P, ONE, NE])
    earlierf = sb("earlierf", [P, P])
    earlier = sb("earlier", [P, P], F32R)
    ones = sb("ones", [P, P], F32R)
    region = sb("region", [P, ONE])
    rowid = sb("rowid", [P, 1])
    tileid = sb("tileid", [1, NT])
    hb = [sb("hb%d" % p, [P, LT, D]) for p in range(2)]
    z3 = [sb("z3_%d" % p, [P, LT, D]) for p in range(3)]
    zhi = [sb("zhi%d" % p, [P, FT, L], F32R) for p in range(2)]
    zlo = [sb("zlo%d" % p, [P, FT, L], F32R) for p in range(2)]
    sil = sb("sil", [P, 2, 2 * L])
    uu = sb("uu", [P, 3, 2 * L])
    raw2 = sb("raw2", [P, UW])
    RAW = 2
    raw = [uu[:].rearrange("p a b -> p (a b)"), raw2[:]]
    assert UW == 3 * 2 * L
    hhi = sb("hhi", [P, 2, 2 * L], F32R)
    hlo = sb("hlo", [P, 2, 2 * L], F32R)
    acc = sb("acc", [P, LT, D])
    th = sb("th", [P, ONE])
    sc = sb("sc", [P, ONE])
    key = sb("key", [P, ONE])
    gt = sb("gt", [P, ONE, NE])
    eq = sb("eq", [P, ONE, NE])
    rank = sb("rank", [P, ONE])
    gate = sb("gate", [P, ONE])
    mask = sb("mask", [P, ONE], F32R)
    filled = sb("filled", [P, ONE])
    slot = sb("slot", [P, ONE])
    smax = sb("smax", [P, LT])
    ssum = sb("ssum", [P, LT])
    hit = sb("hit", [P, TOP, ONE])
    two = sb("two", [P, LT, TOP])
    idx = [sb("idx%d" % p, [P, LT * TOP], I32) for p in range(3)]
    slots = sb("slots", [P, K * LT * TOP])
    offset = sb("offset", [P, K * LT * TOP])
    moved = sb("moved", [P, K * LT * TOP])
    shift = sb("shift", [P, NE])
    idxs = sb("idxs", [P, K * LT * TOP], I32)
    gates = sb("gates", [P, K * LT * TOP])
    gnow = sb("gnow", [P, LT * TOP])
    tail = sb("tail", [P, NE], I32)
    tailf = sb("tailf", [P, NE])
    rows = sb("rows", [1, NT], I32)
    units = sb("units", [1, NT], I32)
    turns = sb("turns", [1, NT], I32)
    count = sb("count", [P, NE])
    ntile = sb("ntile", [P, NE])
    upto = sb("upto", [P, NE])
    ti = sb("list_ti", [1, NT])
    te = sb("list_te", [1, NT])
    tp = sb("list_tp", [1, NT])
    tq = sb("list_tq", [1, NT])
    mark = sb("mark", [P, 1])

    w_hi, w_lo, b_load, r_hi, r_lo = (sem(x) for x in ("w_hi", "w_lo", "b_load", "r_hi", "r_lo"))
    w_in = [sem("w_in0"), sem("w_in1")]
    hb_in, z3_ok, zt3_ps, zhi_ok, zlo_ok, lg_ps, th_ok, gt_step, gate_ok, pos_ps, rt_step, idx_ok, base_ok, kept = (
        sem(x) for x in ("hb_in", "z3_ok", "zt3_ps", "zhi_ok", "zlo_ok", "lg_ps", "th_ok", "gt_step", "gate_ok",
                         "pos_ps", "rt_step", "idx_ok", "base_ok", "kept"))
    zs_out = [sem("zs_out%d" % p) for p in range(3)]
    seen, tail_ok = sem("seen"), sem("tail_ok")
    tail_out, tab_step, tab_ok = sem("tail_out"), sem("tab_step"), sem("tab_ok")
    GS = 6
    consts = [(rwr, a["routerT"]), (ebias, a["ebias"]), (before, a["before"]), (earlierf, a["earlier"]),
              (region, a["region"]), (rowid, a["rowid"]), (tileid, a["tileid"])]

    def later(k):
        return not isinstance(k, int) or k > 0

    def norm(dve, k, h, z, done):
        for t in range(LT):
            c = k * LT + t
            mean = mv3[:, bass.ds(c, 1), 0:1].rearrange("p t m -> p (t m)")
            root = rs3[:, bass.ds(c, 1)]
            last = dve.tensor_scalar(z[:, t, :], h[:, t, :], mean, root, ALU.subtract, ALU.mult)
        last.then_inc(done, 1)

    with nc.Block() as block:
        @block.sync
        def _(sp):
            for dst, src in consts:
                sp.dma_start(dst[:], src).then_inc(b_load, 16)
            sp.dma_start(hb[0][:], hscr[0]).then_inc(hb_in, 16)
            sp.wait_ge(z3_ok, 1)
            sp.dma_start(hb[0][:], hscr[1]).then_inc(hb_in, 16)
            for u in range(NU):
                if u >= RAW:
                    sp.wait_ge(w_lo, u - RAW + 1)
                sp.dma_start(raw[u % RAW], a["wu"][u]).then_inc(w_in[u % RAW], 16)
                sp.wait_ge(z3_ok, u + 2)
                sp.dma_start(hb[0][:], hscr[u + 2]).then_inc(hb_in, 16)
            with sp.Fori(NU + 2, K) as k:
                sp.wait_ge(z3_ok, k)
                sp.dma_start(hb[0][:], hscr[bass.ds(k, 1)].rearrange("n p t d -> p (n t) d")).then_inc(hb_in, 16)

        def blocks(eng, step):
            for k in range(NU):
                step(k, k % 3, k // 3)
            with eng.Fori(NU // 3, K // 3 - 1) as n:
                for p in range(3):
                    step(3 * n + p, p, n)
            for k in range(K - 3, K):
                step(k, k % 3, k // 3)

        def first(k, m):
            return isinstance(k, int) and k < m

        def last_(k, m):
            return isinstance(k, int) and k >= K - m

        @block.tensor
        def _(pe):
            def turn(k, p):
                pe.wait_ge(z3_ok, k + 1)
                if later(k):
                    pe.wait_ge(zlo_ok, k)
                for f in range(FT):
                    for t in range(LT):
                        last = pe.transpose(ps[:, 0, f * L + t * P:f * L + (t + 1) * P], z3[p][:, t, f * P:(f + 1) * P],
                                            eye[:])
                last.then_inc(zt3_ps, 1)

            def router(k):
                pe.wait_ge(zhi_ok, k + 1)
                pe.wait_ge(zlo_ok, k + 1)
                if later(k):
                    pe.wait_ge(th_ok, k)
                for t in range(LT):
                    mm = [(z_, w_, f) for z_, w_ in ((zhi[0], rwh), (zlo[0], rwh), (zhi[0], rwl)) for f in range(FT)]
                    for n, (z_, w_, f) in enumerate(mm):
                        last = pe.matmul(ps[:, 1, t * NE:(t + 1) * NE], z_[:, f, t * P:(t + 1) * P], w_[:, f, :],
                                         start=(n == 0), stop=(n == len(mm) - 1))
                last.then_inc(lg_ps, 1)

            def counts(k):
                pe.wait_ge(gate_ok, k + 1)
                if later(k):
                    pe.wait_ge(base_ok, k)
                m = [mask[:, t * NE:(t + 1) * NE] for t in range(LT)]
                pe.matmul(ps[:, 2, 0:NE], earlier[:], m[0], start=True, stop=True)
                pe.matmul(ps[:, 2, NE:2 * NE], earlier[:], m[1], start=True, stop=False)
                pe.matmul(ps[:, 2, NE:2 * NE], ones[:], m[0], start=False, stop=True)
                pe.matmul(ps[:, 2, 2 * NE:3 * NE], ones[:], m[0], start=True, stop=False)
                pe.matmul(ps[:, 2, 2 * NE:3 * NE], ones[:], m[1], start=False, stop=True).then_inc(pos_ps, 1)

            def step(k, p, n):
                if not last_(k, 1):
                    turn(k + 1, (p + 1) % 3)
                counts(k)
                if not last_(k, 1):
                    router(k + 1)

            pe.wait_ge(r_lo, 1)
            pe.wait_ge(r_hi, 1)
            turn(0, 0)
            router(0)
            blocks(pe, step)

        @block.scalar
        def _(act):
            def prepare(k):
                act.wait_ge(zt3_ps, k + 1)
                act.activation(zhi[0][:].rearrange("p f l -> p (f l)"), ps[:, 0, :], ACT.Copy).then_inc(zhi_ok, 1)
                act.wait_ge(lg_ps, k + 1)
                if later(k):
                    act.wait_ge(gate_ok, k)
                act.activation(th[:], ps[:, 1, 0:ONE], ACT.Tanh, scale=0.5).then_inc(th_ok, 1)

            def step(k, p, n):
                if first(k, NU):
                    act.wait_ge(w_in[k % RAW], 16 * (k // RAW) + 16)
                    act.activation(whi[:, k, :], raw[k % RAW], ACT.Copy).then_inc(w_hi, 1)
                if not last_(k, 1):
                    prepare(k + 1)

            act.wait_ge(b_load, 16 * len(consts))
            act.activation(rwh[:].rearrange("p f e -> p (f e)"), rwr[:], ACT.Copy).then_inc(r_hi, 1)
            prepare(0)
            blocks(act, step)

        @block.vector
        def _(dve):
            def scores(k):
                dve.wait_ge(th_ok, k + 1)
                dve.tensor_scalar(sc[:], th[:], 0.5, 0.5, ALU.mult, ALU.add).then_inc(gt_step, 1)
                dve.wait_ge(gt_step, k * GS + 1)
                dve.tensor_tensor(key[:], sc[:], ebias[:], ALU.add).then_inc(gt_step, 1)
                dve.wait_ge(gt_step, k * GS + 2)
                for t in range(LT):
                    row = key[:, t * NE:(t + 1) * NE]
                    other = row.rearrange("p (o e) -> p o e", o=1).broadcast_to([P, NE, NE])
                    own = row.rearrange("p (e o) -> p e o", o=1).broadcast_to([P, NE, NE])
                    dve.tensor_tensor(gt[:, t * NE:(t + 1) * NE, :], other, own, ALU.is_gt)
                    last = dve.tensor_tensor(eq[:, t * NE:(t + 1) * NE, :], other, own, ALU.is_equal)
                last.then_inc(gt_step, 1)
                dve.wait_ge(gt_step, k * GS + 3)
                f = lambda t: t[:].rearrange("p a b -> p (a b)")
                dve.tensor_tensor(f(eq), f(eq), f(before), ALU.mult).then_inc(gt_step, 1)
                dve.wait_ge(gt_step, k * GS + 4)
                dve.tensor_tensor(f(gt), f(gt), f(eq), ALU.add).then_inc(gt_step, 1)
                dve.wait_ge(gt_step, k * GS + 5)
                dve.tensor_reduce(rank[:], gt[:], AX_X, ALU.add).then_inc(gt_step, 1)
                dve.wait_ge(gt_step, k * GS + 6)
                dve.scalar_tensor_tensor(out=gate[:], in0=rank[:], scalar=1.5, in1=sc[:], op0=ALU.is_lt, op1=ALU.mult)
                dve.tensor_scalar(mask[:], rank[:], 1.5, None, ALU.is_lt).then_inc(gate_ok, 1)

            RS = 7

            def places(k, p, n):
                dve.wait_ge(pos_ps, k + 1)
                dve.tensor_tensor(slot[:], ps[:, 2, 0:ONE], filled[:], ALU.add).then_inc(rt_step, 1)
                dve.wait_ge(rt_step, k * RS + 1)
                dve.tensor_tensor(filled[:].rearrange("p (t e) -> p t e", t=LT),
                                  ps[:, 2, ONE:ONE + NE].rearrange("p (o e) -> p o e", o=1).broadcast_to([P, LT, NE]),
                                  filled[:].rearrange("p (t e) -> p t e", t=LT), ALU.add).then_inc(base_ok, 1)
                dve.tensor_tensor(slot[:], slot[:], mask[:].bitcast(F32), ALU.mult).then_inc(rt_step, 1)
                dve.wait_ge(rt_step, k * RS + 2)
                by_t = lambda t: t.rearrange("p (t e) -> p t e", e=NE)
                dve.tensor_reduce(smax[:], by_t(slot[:]), AX_X, ALU.max)
                dve.tensor_reduce(ssum[:], by_t(slot[:]), AX_X, ALU.add).then_inc(rt_step, 1)
                dve.wait_ge(rt_step, k * RS + 3)
                dve.tensor_copy(two[:, :, 0], smax[:])
                dve.tensor_tensor(two[:, :, 1], ssum[:], smax[:], ALU.subtract).then_inc(rt_step, 1)
                dve.wait_ge(rt_step, k * RS + 4)
                for c in range(TOP):
                    last = dve.tensor_tensor(by_t(hit[:, c, :]), by_t(slot[:]),
                                             two[:, :, c:c + 1].broadcast_to([P, LT, NE]), ALU.is_equal)
                last.then_inc(rt_step, 1)
                if later(k):
                    dve.wait_ge(seen, k)
                if not first(k, 3):
                    dve.wait_ge(zs_out[p], 64 * n)
                dve.tensor_scalar(idx[p][:], two[:].rearrange("p t c -> p (t c)"), 1.0, None,
                                  ALU.subtract).then_inc(idx_ok, 1)
                dve.wait_ge(rt_step, k * RS + 5)
                for c in range(TOP):
                    last = dve.tensor_tensor(hit[:, c, :], hit[:, c, :], gate[:], ALU.mult)
                last.then_inc(rt_step, 1)
                dve.wait_ge(idx_ok, k + 1)
                dve.tensor_copy(slots[:, bass.ds(k * LT * TOP, LT * TOP)], idx[p][:]).then_inc(kept, 1)
                dve.wait_ge(rt_step, k * RS + 6)
                for c in range(TOP):
                    last = dve.tensor_reduce(gnow[:, c * LT:(c + 1) * LT], by_t(hit[:, c, :]), AX_X, ALU.add)
                last.then_inc(rt_step, 1)
                dve.wait_ge(rt_step, k * RS + 7)
                dve.tensor_copy(gates[:, bass.ds(k * LT * TOP, LT * TOP)], gnow[:]).then_inc(kept, 1)

            def low(k):
                dve.wait_ge(zhi_ok, k + 1)
                dve.tensor_tensor(zlo[0][:].rearrange("p f l -> p (f l)"), ps[:, 0, :],
                                  zhi[0][:].rearrange("p f l -> p (f l)"), ALU.subtract).then_inc(zlo_ok, 1)

            def step(k, p, n):
                scores(k)
                if not last_(k, 1):
                    low(k + 1)
                places(k, p, n)
                if not last_(k, 2):
                    if not first(k, 1):
                        dve.wait_ge(zs_out[(p + 2) % 3], 64 * n + (64 if p > 0 else 0))
                    dve.wait_ge(hb_in, k * 16 + 48)
                    norm(dve, k + 2, hb[0], z3[(p + 2) % 3], z3_ok)

            dve.wait_ge(b_load, 16 * len(consts))
            dve.wait_ge(r_hi, 1)
            dve.tensor_tensor(rwl[:].rearrange("p f e -> p (f e)"), rwr[:], rwh[:].rearrange("p f e -> p (f e)"),
                              ALU.subtract).then_inc(r_lo, 1)
            dve.tensor_copy(filled[:], region[:])
            dve.memset(ones[:].bitcast(F32), 1.0)
            dve.tensor_copy(earlier[:], earlierf[:])
            for k in range(2):
                dve.wait_ge(hb_in, 16 * k + 16)
                norm(dve, k, hb[0], z3[k], z3_ok)
            low(0)
            blocks(dve, step)
            n = [0]

            def chain(ins):
                n[0] += 1
                ins.then_inc(tab_step, 1)
                dve.wait_ge(tab_step, n[0])

            dve.wait_ge(base_ok, K)
            dve.wait_ge(kept, 2 * K)
            chain(dve.tensor_scalar(tailf[:], filled[:, 0:NE], rowid[:, 0:1], 1.0, ALU.add, ALU.subtract))
            chain(dve.tensor_copy(tail[:], tailf[:]))
            dve.wait_ge(zs_out[0], 64 * (K // 3))
            dve.memset(z3[0][:], 0.0).then_inc(tail_ok, 1)
            chain(dve.tensor_tensor(count[:], filled[:, 0:NE], region[:, 0:NE], ALU.subtract))
            chain(dve.tensor_scalar(count[:], count[:], float(P - 1), 1.0 / P, ALU.add, ALU.mult))
            chain(dve.tensor_scalar(count[:], count[:], 0.5 - 0.5 / P, ROUND, ALU.subtract, ALU.add))
            chain(dve.tensor_scalar(ntile[:], count[:], ROUND, None, ALU.subtract))
            chain(dve.tensor_copy(upto[:], ntile[:]))
            for e in range(1, NE):
                chain(dve.tensor_tensor(upto[:, e:e + 1], upto[:, e - 1:e], ntile[:, e:e + 1], ALU.add))
            chain(dve.tensor_scalar(tq[:, 0:1], upto[0:1, NE - 1:NE], 1.0, None, ALU.subtract))
            chain(dve.tensor_scalar(ti[:], tileid[:], tq[:, 0:1], None, ALU.min))
            chain(dve.memset(te[:], 0.0))
            chain(dve.memset(tp[:], 0.0))
            for e in range(NE - 1):
                chain(dve.scalar_tensor_tensor(out=te[:], in0=ti[:], scalar=upto[0:1, e:e + 1], in1=te[:], op0=ALU.is_ge,
                                               op1=ALU.add))
                chain(dve.tensor_scalar(tq[:], ti[:], upto[0:1, e:e + 1], ntile[0:1, e:e + 1], ALU.is_ge, ALU.mult))
                chain(dve.tensor_tensor(tp[:], tp[:], tq[:], ALU.add))
            chain(dve.tensor_tensor(tp[:], ti[:], tp[:], ALU.subtract))
            chain(dve.tensor_scalar(tq[:], te[:], float(REG), None, ALU.mult))
            chain(dve.scalar_tensor_tensor(out=tp[:], in0=tp[:], scalar=float(P), in1=tq[:], op0=ALU.mult, op1=ALU.add))
            chain(dve.tensor_copy(rows[:], tp[:]))
            chain(dve.tensor_scalar(te[:], te[:], float(NS), None, ALU.add))
            chain(dve.tensor_copy(units[:], te[:]))
            chain(dve.memset(tp[:], 0.0))
            at = lambda j: te[:, j:NT - 3 + j]
            chain(dve.scalar_tensor_tensor(out=tp[:, 2:NT - 1], in0=at(3), scalar=float(NU), in1=at(2), op0=ALU.mult,
                                           op1=ALU.add))
            for j in (1, 0):
                chain(dve.scalar_tensor_tensor(out=tq[:, 2:NT - 1], in0=tp[:, 2:NT - 1], scalar=float(NU), in1=at(j),
                                               op0=ALU.mult, op1=ALU.add))
                chain(dve.tensor_copy(tp[:, 2:NT - 1], tq[:, 2:NT - 1]))
            dve.tensor_copy(turns[:], tp[:]).then_inc(tab_ok, 1)
            chain(dve.tensor_scalar(shift[:], ntile[:], float(P), float(REG), ALU.mult, ALU.subtract))
            for e in range(1, NE):
                chain(dve.tensor_scalar(moved[:], slots[:], float(e * REG), shift[:, e - 1:e], ALU.is_ge, ALU.mult))
                if e == 1:
                    chain(dve.tensor_copy(offset[:], moved[:]))
                else:
                    chain(dve.tensor_tensor(offset[:], offset[:], moved[:], ALU.add))
            chain(dve.tensor_tensor(slots[:], slots[:], offset[:], ALU.add))
            dve.tensor_copy(idxs[:], slots[:])

        @block.gpsimd
        def _(pool):
            def step(k, p, n):
                if first(k, NU):
                    pool.wait_ge(w_hi, k + 1)
                    pool.tensor_tensor(wlo[:, k, :], raw[k % RAW], whi[:, k, :], ALU.subtract).then_inc(w_lo, 1)
                pool.wait_ge(idx_ok, k + 1)
                pool.tensor_tensor(mark[:], rowid[:], rowid[:], ALU.add).then_inc(seen, 1)
                for t in range(LT):
                    for c in range(TOP):
                        at = t * TOP + c
                        pool.indirect_dma_start(zs, bass.IndirectOffsetOnAxis(idx[p][:, at:at + 1], 0), z3[p][:, t, :],
                                                None).then_inc(zs_out[p], 16)


            blocks(pool, step)
            pool.wait_ge(tail_ok, 1)
            for e in range(NE):
                pool.indirect_dma_start(zs, bass.IndirectOffsetOnAxis(tail[:, e:e + 1], 0), z3[0][:, 0, :],
                                        None).then_inc(tail_out, 16)
            pool.wait_ge(tail_out, 16 * NE)
            for p in range(3):
                pool.wait_ge(zs_out[p], 64 * (K // 3))

    z_in, y_out = [sem("z_in0"), sem("z_in1")], [sem("y_out0"), sem("y_out1")]
    xt_ps, xhi_ok, xlo_ok, x12_ps, xs_ok, xu_ok, xh_ps, xhh_ok, xhl_ok, xy_ps, xy_ok = (
        sem(x) for x in ("xt_ps", "xhi_ok", "xlo_ok", "x12_ps", "xs_ok", "xu_ok", "xh_ps", "xhh_ok", "xhl_ok",
                         "xy_ps", "xy_ok"))
    with nc.Block() as block:
        def valid(i):
            return not isinstance(i, int) or 0 <= i < NT

        def tiles(eng, step):
            for i in range(-1, 3):
                step(i, i % 2)
            with eng.Fori(0, (NT - 4) // 2) as i:
                step(2 * i + 3, 1)
                step(2 * i + 4, 0)
            for i in range(NT - 1, NT + 2):
                step(i, i % 2)

        zin = lambda p: z3[p % 2][:, 0, :]
        ysb = lambda p: z3[p % 2][:, 1, :]
        xsil = lambda p: sil[:, p % 2, 0:UH]
        xu = lambda p: uu[:, p % 2, 0:UH]

        @block.sync
        def _(sp):
            def load(i, p):
                row = sp.value_load(rows[0:1, bass.ds(i, 1)], min_val=0, max_val=NE * REG - P)
                sp.dma_start(zin(p), zs[bass.ds(row, P), :]).then_inc(z_in[p % 2], 16)

            def step(i, p):
                if valid(i + 3):
                    sp.wait_ge(xt_ps, i + 2)
                    load(i + 3, p + 3)
                if valid(i - 2):
                    sp.wait_ge(xy_ok, i - 1)
                    sp.dma_start(ys[bass.ds((i - 2) * P, P), :], ysb(p)).then_inc(y_out[p % 2], 16)

            load(0, 0)
            load(1, 1)
            for i in range(-1, 3):
                step(i, i % 2)
            with sp.Fori(0, (NT - 6) // 2) as i:
                step(2 * i + 3, 1)
                step(2 * i + 4, 0)
            for i in range(NT - 3, NT + 2):
                step(i, i % 2)
            for p in range(2):
                sp.wait_ge(y_out[p], 16 * (NT // 2))

        @block.tensor
        def _(pe):
            def unit_of(i):
                return pe.value_load(units[0:1, i:i + 1], min_val=NS, max_val=NU - 1) if valid(i) else None

            def step(i, p, unit_in, unit_out):
                if valid(i + 1):
                    q = (p + 1) % 2
                    pe.wait_ge(z_in[q], 8 * (i + 1 - q) + 16)
                    if not isinstance(i, int) or i + 1 >= 2:
                        pe.wait_ge(xlo_ok, i)
                    for f in range(FT):
                        last = pe.transpose(ps[:, q, f * P:(f + 1) * P], zin(q)[:, f * P:(f + 1) * P], eye[:])
                    last.then_inc(xt_ps, 1)
                if valid(i - 2):
                    pe.wait_ge(xhh_ok, i - 1)
                    pe.wait_ge(xhl_ok, i - 1)
                    if not isinstance(i, int) or i - 2 >= 2:
                        pe.wait_ge(xy_ok, i - 3)
                    mm = [(h_, w_, c) for h_, w_ in ((hhi, whi), (hlo, whi), (hhi, wlo)) for c in range(2)]
                    for n, (h_, w_, c) in enumerate(mm):
                        at = FT * 2 * UH + c * D
                        w = w_[:, bass.ds(unit_out, 1), at:at + D].rearrange("p u n -> p (u n)")
                        last = pe.matmul(ps[:, 6 + p, 0:D], h_[:, p, c * P:(c + 1) * P], w, start=(n == 0),
                                         stop=(n == len(mm) - 1))
                    last.then_inc(xy_ps, 1)
                if valid(i - 1):
                    q = (p + 1) % 2
                    pe.wait_ge(xu_ok, i)
                    if not isinstance(i, int) or i - 1 >= 2:
                        pe.wait_ge(xhl_ok, i - 2)
                    for c in range(2):
                        last = pe.transpose(ps[:, 4 + q, c * P:(c + 1) * P], xu(q)[:, c * P:(c + 1) * P], eye[:])
                    last.then_inc(xh_ps, 1)
                if valid(i):
                    pe.wait_ge(xhi_ok, i + 1)
                    pe.wait_ge(xlo_ok, i + 1)
                    if not isinstance(i, int) or i >= 2:
                        pe.wait_ge(xu_ok, i - 1)
                    mm = [(z_, w_, f) for z_, w_ in ((zhi, whi), (zlo, whi), (zhi, wlo)) for f in range(FT)]
                    for n, (z_, w_, f) in enumerate(mm):
                        w = w_[:, bass.ds(unit_in, 1), f * 2 * UH:(f + 1) * 2 * UH].rearrange("p u n -> p (u n)")
                        last = pe.matmul(ps[:, 2 + p, 0:2 * UH], z_[p][:, 0, f * P:(f + 1) * P], w,
                                         start=(n == 0), stop=(n == len(mm) - 1))
                    last.then_inc(x12_ps, 1)

            for i in range(-1, 3):
                step(i, i % 2, unit_of(i), unit_of(i - 2))
            with pe.Fori(0, (NT - 4) // 2) as i:
                code = pe.value_load(turns[0:1, bass.ds(2 * i + 3, 1)], min_val=0, max_val=NU ** 4 - 1)
                u = [(code // NU ** n) % NU for n in range(4)]
                step(2 * i + 3, 1, u[2], u[0])
                step(2 * i + 4, 0, u[3], u[1])
            for i in range(NT - 1, NT + 2):
                step(i, i % 2, unit_of(i), unit_of(i - 2))

        @block.scalar
        def _(act):
            def step(i, p):
                q = (p + 1) % 2
                if valid(i + 1):
                    act.wait_ge(xt_ps, i + 2)
                    if not isinstance(i, int) or i + 1 >= 2:
                        act.wait_ge(x12_ps, i)
                    act.activation(zhi[q][:, 0, :], ps[:, q, 0:D], ACT.Copy).then_inc(xhi_ok, 1)
                if valid(i - 2):
                    act.wait_ge(xy_ps, i - 1)
                    if not isinstance(i, int) or i - 2 >= 2:
                        act.wait_ge(y_out[p], 8 * (i - 2 - p))
                        act.wait_ge(xhl_ok, i - 3)
                    act.activation(ysb(p), ps[:, 6 + p, 0:D], ACT.Copy).then_inc(xy_ok, 1)
                if valid(i - 1):
                    act.wait_ge(xh_ps, i)
                    if not isinstance(i, int) or i - 1 >= 2:
                        act.wait_ge(xy_ps, i - 2)
                    act.activation(hhi[:, q, 0:UH], ps[:, 4 + q, 0:UH], ACT.Copy).then_inc(xhh_ok, 1)
                if valid(i):
                    act.wait_ge(x12_ps, i + 1)
                    if not isinstance(i, int) or i >= 2:
                        act.wait_ge(xu_ok, i - 1)
                    act.activation(xsil(p), ps[:, 2 + p, 0:UH], ACT.Silu).then_inc(xs_ok, 1)

            tiles(act, step)

        @block.vector
        def _(dve):
            def step(i, p):
                q = (p + 1) % 2
                if valid(i + 1):
                    dve.wait_ge(xhi_ok, i + 2)
                    dve.tensor_tensor(zlo[q][:, 0, :], ps[:, q, 0:D], zhi[q][:, 0, :], ALU.subtract).then_inc(xlo_ok, 1)
                if valid(i - 1):
                    dve.wait_ge(xhh_ok, i)
                    dve.tensor_tensor(hlo[:, q, 0:UH], ps[:, 4 + q, 0:UH], hhi[:, q, 0:UH],
                                      ALU.subtract).then_inc(xhl_ok, 1)
                if valid(i):
                    dve.wait_ge(xs_ok, i + 1)
                    if not isinstance(i, int) or i >= 2:
                        dve.wait_ge(xh_ps, i - 1)
                    dve.tensor_tensor(xu(p), ps[:, 2 + p, UH:2 * UH], xsil(p), ALU.mult).then_inc(xu_ok, 1)

            tiles(dve, step)

    hb3_in = [sem("hb3_in0"), sem("hb3_in1")]
    z_ok3, t3_ps, hi3_ok, lo3_ok, hid_ps, sil_ok, uu_ok, hhi_ok, hlo_ok, out_ps, acc_ok, out_d = (
        sem(x) for x in ("z_ok3", "t3_ps", "hi3_ok", "lo3_ok", "hid_ps", "sil_ok", "uu_ok", "hhi_ok", "hlo_ok",
                         "out_ps", "acc_ok", "out_d"))
    idx3_ok, y_in, seen3 = sem("idx3_ok"), sem("y_in"), sem("seen3")
    AN = 1 + TOP
    yg = raw2[:, 0:LT * TOP * D].rearrange("p (t c d) -> p t c d", t=LT, c=TOP)
    with nc.Block() as block:
        def blocks3(eng, blk):
            blk(0, 0)
            with eng.Fori(0, (K - 3) // 2) as i:
                blk(2 * i + 1, 1)
                blk(2 * i + 2, 0)
            for k in range(K - 2, K):
                blk(k, k % 2)

        @block.sync
        def _(sp):
            def step(k, p):
                if not isinstance(k, int) or k < K - 2:
                    sp.wait_ge(acc_ok, k * AN + 1)
                    sp.dma_start(hb[p][:], hscr[bass.ds(k + 2, 1)].rearrange("n p t d -> p (n t) d")).then_inc(hb3_in[p], 16)
                sp.wait_ge(acc_ok, k * AN + AN)
                if not isinstance(k, int) or k < K - 1:
                    sp.dma_start(out[bass.ds(k, 1), 1:N, :].rearrange("n (t p) d -> p (n t) d", p=P),
                                 acc[:]).then_inc(out_d, 16)

            for p in range(2):
                sp.dma_start(hb[p][:], hscr[p]).then_inc(hb3_in[p], 16)
            blocks3(sp, step)
            sp.dma_start(out[:, 0, :], acc[0:B, 0, :]).then_inc(out_d, 16)
            sp.wait_ge(out_d, 16 * K)

        @block.tensor
        def _(pe):
            def turn(k):
                pe.wait_ge(z_ok3, k + 1)
                if later(k):
                    pe.wait_ge(lo3_ok, k)
                for f in range(FT):
                    for t in range(LT):
                        last = pe.transpose(ps[:, 6, f * L + t * P:f * L + (t + 1) * P], z3[0][:, t, f * P:(f + 1) * P],
                                            eye[:])
                last.then_inc(t3_ps, 1)

            def hidden(k, p, u):
                if u == 0:
                    pe.wait_ge(hi3_ok, k + 1)
                    pe.wait_ge(lo3_ok, k + 1)
                if u >= 2 or later(k):
                    pe.wait_ge(uu_ok, k * NS + u - 1)
                for c in range(2):
                    for m in range(2):
                        mm = [(w_, z_, f) for w_, z_ in ((whi, zhi[p]), (wlo, zhi[p]), (whi, zlo[p])) for f in range(FT)]
                        for n, (w_, z_, f) in enumerate(mm):
                            at = f * 2 * UH + m * UH + c * P
                            last = pe.matmul(ps[:, 2 * (u % 2) + c, m * L:(m + 1) * L], w_[:, u, at:at + P], z_[:, f, :],
                                             start=(n == 0), stop=(n == len(mm) - 1))
                last.then_inc(hid_ps, 1)

            def output(k, u):
                pe.wait_ge(hhi_ok, k * NS + u + 1)
                pe.wait_ge(hlo_ok, k * NS + u + 1)
                if u == 0 and later(k):
                    pe.wait_ge(acc_ok, k * AN - AN + 1)
                for t in range(LT):
                    mm = [(h_, w_, c) for h_, w_ in ((hhi, whi), (hlo, whi), (hhi, wlo)) for c in range(2)]
                    for n, (h_, w_, c) in enumerate(mm):
                        at = FT * 2 * UH + c * D
                        last = pe.matmul(ps[:, 4, t * D:(t + 1) * D], h_[:, u % 2, c * L + t * P:c * L + (t + 1) * P],
                                         w_[:, u, at:at + D], start=(n == 0 and u == 0 and t == 0),
                                         stop=(n == len(mm) - 1 and u == NS - 1), skip_group_check=True)
                last.then_inc(out_ps, 1)

            def blk(k, p):
                nxt = not isinstance(k, int) or k < K - 1
                for u in range(NS):
                    hidden(k, p, u)
                    if u >= 1:
                        output(k, u - 1)
                    elif later(k):
                        output(k - 1, NS - 1)
                    if u == 2 and nxt:
                        turn(k + 1)

            turn(0)
            blocks3(pe, blk)
            output(K - 1, NS - 1)

        @block.scalar
        def _(act):
            def silu(k, u):
                act.wait_ge(hid_ps, k * NS + u + 1)
                if u >= 2 or later(k):
                    act.wait_ge(uu_ok, k * NS + u - 1)
                act.activation(sil[:, u % 2, :].rearrange("p (c l) -> p c l", c=2),
                               ps[:, 2 * (u % 2):2 * (u % 2) + 2, 0:L], ACT.Silu).then_inc(sil_ok, 1)

            def head(k, u):
                act.wait_ge(uu_ok, k * NS + u + 1)
                if u >= 2 or later(k):
                    act.wait_ge(out_ps, k * NS + u - 1)
                act.activation(hhi[:, u % 2, :], uu[:, u % 2, :], ACT.Copy).then_inc(hhi_ok, 1)

            def z_high(k, p):
                act.wait_ge(t3_ps, k + 1)
                act.activation(zhi[p][:].rearrange("p f l -> p (f l)"), ps[:, 6, :], ACT.Copy).then_inc(hi3_ok, 1)

            def blk(k, p):
                nxt = not isinstance(k, int) or k < K - 1
                for u in range(NS):
                    silu(k, u)
                    head(k, u)
                    if u == 2 and nxt:
                        z_high(k + 1, 1 - p)

            z_high(0, 0)
            blocks3(act, blk)

        @block.vector
        def _(dve):
            def z_low(k, p):
                dve.wait_ge(hi3_ok, k + 1)
                dve.tensor_tensor(zlo[p][:].rearrange("p f l -> p (f l)"), ps[:, 6, :],
                                  zhi[p][:].rearrange("p f l -> p (f l)"), ALU.subtract).then_inc(lo3_ok, 1)

            def product(k, u):
                dve.wait_ge(sil_ok, k * NS + u + 1)
                dve.tensor_tensor(uu[:, u % 2, :].rearrange("p (c l) -> p c l", c=2),
                                  ps[:, 2 * (u % 2):2 * (u % 2) + 2, L:2 * L],
                                  sil[:, u % 2, :].rearrange("p (c l) -> p c l", c=2), ALU.mult).then_inc(uu_ok, 1)

            def split(k, u):
                dve.wait_ge(hhi_ok, k * NS + u + 1)
                dve.tensor_tensor(hlo[:, u % 2, :], uu[:, u % 2, :], hhi[:, u % 2, :], ALU.subtract).then_inc(hlo_ok, 1)

            def pick(k):
                if later(k):
                    dve.wait_ge(y_in, 64 * k)
                    dve.wait_ge(seen3, k)
                dve.tensor_copy(idx[0][:], idxs[:, bass.ds(k * LT * TOP, LT * TOP)]).then_inc(idx3_ok, 1)

            def gather(k, p):
                dve.wait_ge(out_ps, k * NS + NS)
                fl = lambda t: t[:].rearrange("p t d -> p (t d)")
                if later(k):
                    dve.wait_ge(out_d, 16 * k)
                dve.tensor_copy(gnow[:], gates[:, bass.ds(k * LT * TOP, LT * TOP)])
                dve.tensor_tensor(fl(acc), ps[:, 4, :], fl(hb[p]), ALU.add).then_inc(acc_ok, 1)
                dve.wait_ge(y_in, 64 * k + 64)
                for c in range(TOP):
                    dve.wait_ge(acc_ok, k * AN + c + 1)
                    for t in range(LT):
                        last = dve.scalar_tensor_tensor(out=acc[:, t, :], in0=yg[:, t, c, :],
                                                        scalar=gnow[:, c * LT + t:c * LT + t + 1], in1=acc[:, t, :],
                                                        op0=ALU.mult, op1=ALU.add)
                    last.then_inc(acc_ok, 1)

            def blk(k, p):
                nxt = not isinstance(k, int) or k < K - 1
                for u in range(NS):
                    product(k, u)
                    split(k, u)
                    if u == 0 and later(k):
                        gather(k - 1, 1 - p)
                        pick(k)
                    if u == 1 and nxt:
                        dve.wait_ge(hb3_in[1 - p], 8 * (k + p) + 16)
                        norm(dve, k + 1, hb[1 - p], z3[0], z_ok3)
                    if u == 2 and nxt:
                        z_low(k + 1, 1 - p)

            dve.wait_ge(hb3_in[0], 16)
            norm(dve, 0, hb[0], z3[0], z_ok3)
            pick(0)
            z_low(0, 0)
            blocks3(dve, blk)
            gather(K - 1, (K - 1) % 2)

        @block.gpsimd
        def _(pool):
            with pool.Fori(0, K) as k:
                pool.wait_ge(idx3_ok, k + 1)
                pool.tensor_tensor(mark[:], rowid[:], rowid[:], ALU.add).then_inc(seen3, 1)
                for t in range(LT):
                    for c in range(TOP):
                        at = t * TOP + c
                        pool.indirect_dma_start(yg[:, t, c, :], None, ys,
                                                bass.IndirectOffsetOnAxis(idx[0][:, at:at + 1], 0)).then_inc(y_in, 16)


def layout(i):
    f = lambda x: np.ascontiguousarray(x)
    z = lambda *s: np.zeros(s, np.float32)
    t = {k[3:]: np.asarray(v) for k, v in i.items() if k.startswith("L0_")}
    o = {"x": f(i["x"])}
    tiles = lambda m: f(m.reshape(-1, P, m.shape[1]).transpose(1, 0, 2))
    wkv = z(P, 2 * C)
    wkv[:C, :C], wkv[:C, C:] = t["tok_Wk_w"].T, t["tok_Wv_w"].T
    wkv[C, :C], wkv[C, C:] = t["tok_Wk_b"], t["tok_Wv_b"]
    o["wkv"] = wkv
    o["wq"] = f(np.concatenate([t["tok_Wq_w"].T, t["tok_Wq_b"][None], z(P - C - 1, C)]))
    o["idn"] = f(np.concatenate([np.tile(np.eye(C, dtype=np.float32), (1, H)), t["tok_out_b"][None], z(P - C - 1, D)]))
    o["wbT"] = tiles(t["tok_w_bias"].T)
    o["mskT"] = tiles(t["tok_local_mask"].T)
    o["outw"] = tiles(t["tok_out_w"])
    o["lng"] = f(np.tile(t["tok_ln_g"][None], (P, LT)))
    o["lnb"] = f(np.tile(t["tok_ln_b"][None], (P, LT)))
    o["basT"] = tiles(np.concatenate([t["attn_basis_" + n].T for n in "qkv"], axis=1))
    o["basoT"] = tiles(t["attn_basis_o"].T)
    for name, src in (("phs", "phase"), ("amp", "amp")):
        o[name] = f(np.concatenate([t[f"attn_{src}_{n}"].T for n in "qkvo"]))
    heads = np.arange(NH)
    sel = z(P, 4, 4, P)
    for kind, places in enumerate(((0, 1), (2,), (0, 2), (1,))):
        for g in range(4):
            for j in range(2):
                for place in places:
                    to = SLOT2 * j + HD * place
                    sel[(2 * g + j) * HD:(2 * g + j + 1) * HD, kind, g, to:to + HD] = np.eye(HD)
    o["sel"] = sel
    col = np.arange(P)
    o["bdm"] = f((col[None, None] == HPF * np.arange(FT)[None, :, None] + col[:, None, None] // HD).astype(np.float32))
    o["vbdm"] = f((np.arange(D)[None] // HD == heads[:, None]).astype(np.float32))
    o["eye"] = np.eye(P, dtype=np.float32)
    cls = np.asarray(i["cls_tok"]).reshape(1, D)
    o["clsr"] = f(cls)
    o["cls32"] = f(np.tile(cls, (P, 1)))
    sw = [np.asarray(t["ffn_shared_w%d" % n]) for n in (1, 2, 3)]
    wu = z(NU, P, FT * 2 * UH + 2 * D)
    for u in range(NU):
        if u < NS:
            r = slice(u * UH, (u + 1) * UH)
            w_in, w_out = np.concatenate([sw[0][r], sw[1][r]]), sw[2][:, r]
        else:
            w_in, w_out = t["ffn_w12"][u - NS], t["ffn_w3"][u - NS]
        wu[u, :, :FT * 2 * UH] = tiles(w_in.T).reshape(P, -1)
        wu[u, :, FT * 2 * UH:] = tiles(w_out.T).reshape(P, -1)
    o["wu"] = wu
    o["routerT"] = tiles(t["ffn_router_w"].T).reshape(P, -1)
    o["ebias"] = f(np.tile(t["ffn_expert_bias"][None], (P, LT)))
    e = np.arange(NE)
    o["before"] = f(np.tile((e[None] < e[:, None]).astype(np.float32)[None], (P, LT, 1)))
    slots = (B + 1) * L + P
    o["earlier"] = f((np.arange(P)[:, None] < np.arange(P)[None]).astype(np.float32))
    o["region"] = f(np.tile((e * slots + 1).astype(np.float32)[None], (P, LT)))
    o["rowid"] = f(np.arange(P, dtype=np.float32)[:, None])
    o["tileid"] = f(np.arange((2 * (B + 1) * L + NE * (P - 1)) // P + 1, dtype=np.float32)[None])
    return o


def kernel(**inputs):
    import numpy as _np
    import concourse.bacc as _bacc
    from concourse import mybir as _mybir
    from concourse.bass_utils import run_bass_kernel_spmd as _run

    nc = _bacc.Bacc("TRN2", target_bir_lowering=False, num_devices=1)
    arrays = {"in_" + k: v for k, v in layout({k: _np.asarray(v) for k, v in inputs.items()}).items()}
    aps = {k[3:]: nc.dram_tensor(k, v.shape, _mybir.dt.from_np(v.dtype), kind="ExternalInput").ap()
           for k, v in arrays.items()}
    out = nc.dram_tensor("out", (B, N, D), F32, kind="ExternalOutput").ap()
    build(nc, aps, out)
    r = _run(nc, [arrays], core_ids=[0])
    return r.results[0]["out"]
```
